# Optimizing a Trainium2 kernel written in Bass

```python
import numpy as np
import jax
import jax.numpy as jnp

def _softmax(x, axis=-1):
    return jax.nn.softmax(x, axis=axis)

def _gelu(x):
    return jax.nn.gelu(x, approximate=True)

def _silu(x):
    return jax.nn.silu(x)

def _sigmoid(x):
    return jax.nn.sigmoid(x)

def _layernorm(x, axis=-1, eps=1e-05):
    m = jnp.mean(x, axis=axis, keepdims=True)
    v = jnp.var(x, axis=axis, keepdims=True)
    return (x - m) / jnp.sqrt(v + eps)

def _scatter_add(tgt, idx, src, axis=0):
    return tgt.at[idx].add(src)

def _segment_sum(src, seg, n):
    return jax.ops.segment_sum(src, seg, n)
kernel_name = 'mk_gnn_resnorm_d4_gnn_r8_882459'

def setup_inputs(seed: int=0):
    np.random.seed(seed)
    _w = jnp.asarray

    def _rec_inputs():
        import jax
        import jax.numpy as jnp
        _gk = jax.random.key(seed)
        x = -0.0005121 + 1.001 * jax.random.normal(jax.random.fold_in(_gk, 1), (12500, 64), jnp.float32)
        src = jax.random.randint(jax.random.fold_in(_gk, 2), (200000,), 0, 12500, jnp.int32)
        dst = jax.random.randint(jax.random.fold_in(_gk, 3), (200000,), 0, 12500, jnp.int32)
        _o = jnp.argsort(dst, stable=True)
        src = src[_o]
        dst = dst[_o]
        edge_attr_16 = 0.000254156 + 0.999948 * jax.random.normal(jax.random.fold_in(_gk, 13), (200000, 16), jnp.float32)
        edge_attr_64 = 0.000103221 + 1.00003 * jax.random.normal(jax.random.fold_in(_gk, 14), (200000, 64), jnp.float32)
        edge_weight1 = 0.00107675 + 0.999702 * jax.random.normal(jax.random.fold_in(_gk, 16), (200000, 1), jnp.float32)
        node_vec1 = jax.random.uniform(jax.random.fold_in(_gk, 17), (12500, 1), jnp.float32, 0.0, 1)
        return (x, src, dst, edge_attr_16, edge_attr_64, edge_weight1, node_vec1)
    x, src, dst, edge_attr_16, edge_attr_64, edge_weight1, node_vec1 = _rec_inputs()

    def _L0_gnn_setup():
        import jax, jax.numpy as jnp
        import numpy as np
        N_NODES = 6250
        N_EDGES = 100000
        C_IN = 64
        N_HEADS = 4
        HEAD_DIM = 16
        FC = 64
        key = jax.random.key(seed)
        ks = jax.random.split(key, 20)
        d = {}
        d['node_input'] = jax.random.normal(ks[0], (N_NODES, C_IN), jnp.float32)
        d['node_attr'] = jnp.ones((N_NODES, 1), jnp.float32)
        d['edge_src'] = jax.random.randint(ks[1], (N_EDGES,), 0, N_NODES)
        d['edge_dst'] = jax.random.randint(ks[2], (N_EDGES,), 0, N_NODES)
        d['edge_attr'] = jax.random.normal(ks[3], (N_EDGES, 1), jnp.float32)
        d['edge_scalars'] = jax.random.normal(ks[4], (N_EDGES, FC), jnp.float32)
        d['batch'] = jnp.zeros((N_NODES,), jnp.int32)
        s = 1.0 / np.sqrt(C_IN)
        AD = N_HEADS * HEAD_DIM
        d['Wq'] = jax.random.normal(ks[5], (C_IN, AD), jnp.float32) * s
        d['bq'] = jnp.zeros((AD,), jnp.float32)
        d['W_src'] = jax.random.normal(ks[6], (C_IN, C_IN), jnp.float32) * s
        d['b_src'] = jnp.zeros((C_IN,), jnp.float32)
        d['W_dst'] = jax.random.normal(ks[7], (C_IN, C_IN), jnp.float32) * s
        d['W_fc1'] = jax.random.normal(ks[8], (FC, FC), jnp.float32) * (1.0 / np.sqrt(FC))
        d['b_fc1'] = jnp.zeros((FC,), jnp.float32)
        d['W_fc2'] = jax.random.normal(ks[9], (FC, FC), jnp.float32) * (1.0 / np.sqrt(FC))
        d['b_fc2'] = jnp.zeros((FC,), jnp.float32)
        d['W_fc3'] = jax.random.normal(ks[10], (FC, C_IN), jnp.float32) * (1.0 / np.sqrt(FC))
        d['b_fc3'] = jnp.zeros((C_IN,), jnp.float32)
        d['W_kv'] = jax.random.normal(ks[11], (C_IN, 2 * AD), jnp.float32) * s
        d['b_kv'] = jnp.zeros((2 * AD,), jnp.float32)
        d['W_proj'] = jax.random.normal(ks[12], (AD, C_IN), jnp.float32) * (1.0 / np.sqrt(AD))
        d['b_proj'] = jnp.zeros((C_IN,), jnp.float32)
        return d
    _L0_gnn_all = _L0_gnn_setup()
    _L0_gnn_in = {k: v for k, v in _L0_gnn_all.items() if k in ('Wq', 'bq', 'W_src', 'b_src', 'W_dst', 'W_fc1', 'b_fc1', 'W_fc2', 'b_fc2', 'W_fc3', 'b_fc3', 'W_kv', 'b_kv', 'W_proj', 'b_proj')}
    del _L0_gnn_all

    def _L1_gnn_setup():
        import jax, jax.numpy as jnp
        import numpy as np
        N = 12500
        E = 150000
        D_IN = 64
        D_OUT = 64

        def _augment(edge_index, num_nodes):
            src, dst = (edge_index[0], edge_index[1])
            loops = jnp.arange(num_nodes, dtype=edge_index.dtype)
            src_a = jnp.concatenate([src, dst, loops])
            dst_a = jnp.concatenate([dst, src, loops])
            return (src_a, dst_a)
        key = jax.random.key(seed)
        k1, k2, k3, k4 = jax.random.split(key, 4)
        x = jax.random.normal(k1, (N, D_IN), dtype=jnp.float32)
        edge_index = jax.random.randint(k2, (2, E), 0, N, dtype=jnp.int64)
        bound = 1.0 / np.sqrt(D_IN)
        W = jax.random.uniform(k3, (D_OUT, D_IN), minval=-bound, maxval=bound, dtype=jnp.float32)
        b = jax.random.uniform(k4, (D_OUT,), minval=-bound, maxval=bound, dtype=jnp.float32)
        return {'x': x, 'edge_index': edge_index, 'W': W, 'b': b}
    _L1_gnn_all = _L1_gnn_setup()
    _L1_gnn_in = {k: v for k, v in _L1_gnn_all.items() if k in ('W', 'b')}
    del _L1_gnn_all

    def _L2_gnn_setup():
        import jax, jax.numpy as jnp
        import numpy as np
        N_NODES = 12500
        N_EDGES = 200000
        D_IN = 64
        D_OUT = 64
        key = jax.random.key(seed)
        k1, k2, k3, k4, k5 = jax.random.split(key, 5)
        feat = jax.random.normal(k1, (N_NODES, D_IN), dtype=jnp.float32)
        weight1 = jax.random.normal(k2, (D_IN, D_OUT), dtype=jnp.float32) * (1.0 / np.sqrt(D_IN))
        weight2 = jax.random.normal(k3, (D_IN, D_OUT), dtype=jnp.float32) * (1.0 / np.sqrt(D_IN))
        src = jax.random.randint(k4, (N_EDGES,), 0, N_NODES, dtype=jnp.int32)
        dst = jax.random.randint(k5, (N_EDGES,), 0, N_NODES, dtype=jnp.int32)
        return {'feat': feat, 'weight1': weight1, 'weight2': weight2, 'src': src, 'dst': dst}
    _L2_gnn_all = _L2_gnn_setup()
    _L2_gnn_in = {k: v for k, v in _L2_gnn_all.items() if k in ('weight1', 'weight2')}
    del _L2_gnn_all

    def _L3_gnn_setup():
        import jax, jax.numpy as jnp
        import numpy as np
        NUM_NODES = 6250
        NUM_EDGES = 100000
        IN_F = 64
        OUT_F = 64
        EDGE_DIM = 16
        NUM_GRAPHS = 64
        T = 1.0
        NEG_SLOPE = 0.2
        key = jax.random.key(seed)
        k = jax.random.split(key, 6)
        x = jax.random.normal(k[0], (NUM_NODES, IN_F), dtype=jnp.float32)
        edge_index = jax.random.randint(k[1], (2, NUM_EDGES), 0, NUM_NODES, dtype=jnp.int32)
        edge_attr = jax.random.normal(k[2], (NUM_EDGES, EDGE_DIM), dtype=jnp.float32)
        batch_id = jnp.sort(jax.random.randint(k[3], (NUM_NODES,), 0, NUM_GRAPHS, dtype=jnp.int32))
        W = jax.random.normal(k[4], (IN_F, OUT_F), dtype=jnp.float32) * (1.0 / np.sqrt(IN_F))
        a = jax.random.normal(k[5], (2 * OUT_F + EDGE_DIM, 1), dtype=jnp.float32) * 0.1
        return {'x': x, 'edge_index': edge_index, 'edge_attr': edge_attr, 'batch_id': batch_id, 'W': W, 'a': a}
    _L3_gnn_all = _L3_gnn_setup()
    _L3_gnn_in = {k: v for k, v in _L3_gnn_all.items() if k in ('W', 'a')}
    del _L3_gnn_all
    return {'x': x, 'src': src, 'dst': dst, 'edge_attr_16': edge_attr_16, 'edge_attr_64': edge_attr_64, 'edge_weight1': edge_weight1, 'node_vec1': node_vec1, 'L0_gnn_Wq': _L0_gnn_in['Wq'], 'L0_gnn_bq': _L0_gnn_in['bq'], 'L0_gnn_W_src': _L0_gnn_in['W_src'], 'L0_gnn_b_src': _L0_gnn_in['b_src'], 'L0_gnn_W_dst': _L0_gnn_in['W_dst'], 'L0_gnn_W_fc1': _L0_gnn_in['W_fc1'], 'L0_gnn_b_fc1': _L0_gnn_in['b_fc1'], 'L0_gnn_W_fc2': _L0_gnn_in['W_fc2'], 'L0_gnn_b_fc2': _L0_gnn_in['b_fc2'], 'L0_gnn_W_fc3': _L0_gnn_in['W_fc3'], 'L0_gnn_b_fc3': _L0_gnn_in['b_fc3'], 'L0_gnn_W_kv': _L0_gnn_in['W_kv'], 'L0_gnn_b_kv': _L0_gnn_in['b_kv'], 'L0_gnn_W_proj': _L0_gnn_in['W_proj'], 'L0_gnn_b_proj': _L0_gnn_in['b_proj'], 'L1_gnn_W': _L1_gnn_in['W'], 'L1_gnn_b': _L1_gnn_in['b'], 'L2_gnn_weight1': _L2_gnn_in['weight1'], 'L2_gnn_weight2': _L2_gnn_in['weight2'], 'L3_gnn_W': _L3_gnn_in['W'], 'L3_gnn_a': _L3_gnn_in['a']}

def reference(x, src, dst, edge_attr_16, edge_attr_64, edge_weight1, node_vec1, L0_gnn_Wq, L0_gnn_bq, L0_gnn_W_src, L0_gnn_b_src, L0_gnn_W_dst, L0_gnn_W_fc1, L0_gnn_b_fc1, L0_gnn_W_fc2, L0_gnn_b_fc2, L0_gnn_W_fc3, L0_gnn_b_fc3, L0_gnn_W_kv, L0_gnn_b_kv, L0_gnn_W_proj, L0_gnn_b_proj, L1_gnn_W, L1_gnn_b, L2_gnn_weight1, L2_gnn_weight2, L3_gnn_W, L3_gnn_a):
    import jax
    import jax.numpy as jnp

    def _L0_gnn_ref(node_input, node_attr, edge_src, edge_dst, edge_attr, edge_scalars, batch, Wq, bq, W_src, b_src, W_dst, W_fc1, b_fc1, W_fc2, b_fc2, W_fc3, b_fc3, W_kv, b_kv, W_proj, b_proj):
        import jax, jax.numpy as jnp
        import numpy as np
        N_NODES = 6250
        N_EDGES = 100000
        C_IN = 64
        N_HEADS = 4
        HEAD_DIM = 16
        FC = 64
        N = node_input.shape[0]
        q = (node_input @ Wq + bq).reshape(N, N_HEADS, HEAD_DIM)
        q = q * (1.0 / jnp.sqrt(jnp.float32(HEAD_DIM)))
        msg_src = node_input @ W_src + b_src
        msg_dst = node_input @ W_dst
        kv = msg_src[edge_src] + msg_dst[edge_dst]
        h = jax.nn.silu(edge_scalars @ W_fc1 + b_fc1)
        h = jax.nn.silu(h @ W_fc2 + b_fc2)
        w = h @ W_fc3 + b_fc3
        tp = kv * edge_attr * w
        kv2 = (tp @ W_kv + b_kv).reshape(-1, 2 * N_HEADS, HEAD_DIM)
        k = kv2[:, :N_HEADS]
        v = kv2[:, N_HEADS:]
        alpha = jnp.einsum('ehd,ehd->eh', q[edge_dst], k)
        seg_max = jax.ops.segment_max(alpha, edge_dst, num_segments=N)
        seg_max = jnp.where(jnp.isfinite(seg_max), seg_max, 0.0)
        ex = jnp.exp(alpha - seg_max[edge_dst])
        denom = jax.ops.segment_sum(ex, edge_dst, num_segments=N)
        alpha = ex / (denom[edge_dst] + 1e-16)
        attn = jax.ops.segment_sum(v * alpha[..., None], edge_dst, num_segments=N)
        attn = attn.reshape(N, N_HEADS * HEAD_DIM)
        return attn @ W_proj + b_proj

    def _L1_gnn_ref(x, edge_index, W, b):
        import jax, jax.numpy as jnp
        import numpy as np
        N = 12500
        E = 150000
        D_IN = 64
        D_OUT = 64

        def _augment(edge_index, num_nodes):
            src, dst = (edge_index[0], edge_index[1])
            loops = jnp.arange(num_nodes, dtype=edge_index.dtype)
            src_a = jnp.concatenate([src, dst, loops])
            dst_a = jnp.concatenate([dst, src, loops])
            return (src_a, dst_a)
        num_nodes = x.shape[0]
        src, dst = _augment(edge_index, num_nodes)
        ones = jnp.ones(src.shape[0], dtype=jnp.float32)
        deg = jnp.clip(jax.ops.segment_sum(ones, src, num_segments=num_nodes), 1.0)
        dinv = jax.lax.rsqrt(deg)
        norm = (dinv[src] * dinv[dst])[:, None]
        h = x @ W.T + b
        msg = h[src] * norm
        out = jax.ops.segment_sum(msg, dst, num_segments=num_nodes)
        return out

    def _L2_gnn_ref(feat, weight1, weight2, src, dst):
        import jax, jax.numpy as jnp
        import numpy as np
        N_NODES = 12500
        N_EDGES = 200000
        D_IN = 64
        D_OUT = 64
        N = feat.shape[0]
        ones_e = jnp.ones(src.shape[0], dtype=feat.dtype)
        out_deg = jnp.clip(jax.ops.segment_sum(ones_e, src, num_segments=N), 1.0)
        feat_n = feat * jax.lax.rsqrt(out_deg)[:, None]
        h_src = feat_n[src]
        copy_sum = jax.ops.segment_sum(h_src, dst, num_segments=N)
        inner_sum = jax.ops.segment_sum(h_src * feat_n[dst], dst, num_segments=N)
        rst = copy_sum @ weight1 + inner_sum @ weight2
        in_deg = jnp.clip(jax.ops.segment_sum(ones_e, dst, num_segments=N), 1.0)
        rst = rst * jax.lax.rsqrt(in_deg)[:, None]
        return rst

    def _L3_gnn_ref(x, edge_index, edge_attr, batch_id, W, a):
        import jax, jax.numpy as jnp
        import numpy as np
        NUM_NODES = 6250
        NUM_EDGES = 100000
        IN_F = 64
        OUT_F = 64
        EDGE_DIM = 16
        NUM_GRAPHS = 64
        T = 1.0
        NEG_SLOPE = 0.2
        num_nodes = x.shape[0]
        src0, dst0 = (edge_index[0], edge_index[1])
        loop = jnp.arange(num_nodes, dtype=src0.dtype)
        src = jnp.concatenate([src0, dst0, loop])
        dst = jnp.concatenate([dst0, src0, loop])
        xt = x @ W
        a_src = a[:OUT_F, 0]
        a_dst = a[OUT_F:2 * OUT_F, 0]
        a_edge = a[2 * OUT_F:, 0]
        s_node = xt @ a_src
        d_node = xt @ a_dst
        e_contrib = edge_attr @ a_edge
        e_all = jnp.concatenate([e_contrib, e_contrib, jnp.zeros((num_nodes,), xt.dtype)])
        logits = jax.nn.leaky_relu(s_node[src] + d_node[dst] + e_all, NEG_SLOPE) / T
        m = jax.ops.segment_max(logits, dst, num_segments=num_nodes)
        z = jnp.exp(logits - m[dst])
        denom = jax.ops.segment_sum(z, dst, num_segments=num_nodes)
        att = z / denom[dst]
        h_src = xt[src]
        out = jax.ops.segment_sum(att[:, None] * h_src, dst, num_segments=num_nodes)
        return out
    edge_index = jnp.stack([src, dst])
    batch0 = jnp.zeros((12500,), jnp.int32)
    x = _layernorm(x + _L0_gnn_ref(x, node_vec1, src, dst, edge_weight1, edge_attr_64, batch0, L0_gnn_Wq, L0_gnn_bq, L0_gnn_W_src, L0_gnn_b_src, L0_gnn_W_dst, L0_gnn_W_fc1, L0_gnn_b_fc1, L0_gnn_W_fc2, L0_gnn_b_fc2, L0_gnn_W_fc3, L0_gnn_b_fc3, L0_gnn_W_kv, L0_gnn_b_kv, L0_gnn_W_proj, L0_gnn_b_proj), axis=-1)
    x = _layernorm(x + _L1_gnn_ref(x, edge_index, L1_gnn_W, L1_gnn_b), axis=-1)
    x = _layernorm(x + _L2_gnn_ref(x, L2_gnn_weight1, L2_gnn_weight2, src, dst), axis=-1)
    x = _layernorm(x + _L3_gnn_ref(x, edge_index, edge_attr_16, batch0, L3_gnn_W, L3_gnn_a), axis=-1)
    return x

_drawn_inputs = setup_inputs


def setup_inputs(seed=0):
    import zlib

    import numpy as np

    out = dict(_drawn_inputs(seed))
    spreads = {'L0_gnn_bq': (0.0, 0.476),
     'L0_gnn_b_src': (0.0, 0.508),
     'L0_gnn_b_fc1': (0.0, 0.336),
     'L0_gnn_b_fc2': (0.0, 0.1),
     'L0_gnn_b_fc3': (0.0, 0.1),
     'L0_gnn_b_kv': (0.0, 0.1),
     'L0_gnn_b_proj': (0.0, 0.1)}
    factors = {}
    for name, (base, spread) in spreads.items():
        noise = np.random.default_rng([zlib.crc32(name.encode()), seed]).standard_normal(out[name].shape)
        drawn = base * np.exp(spread * noise) if base else spread * noise
        out[name] = jnp.asarray(drawn.astype(out[name].dtype))
    for name, factor in factors.items():
        out[name] = (out[name] * factor).astype(out[name].dtype)
    return out
```

```python
import concourse.bass as bass
from concourse import mybir
from contextlib import ExitStack

I32 = mybir.dt.int32
F32 = mybir.dt.float32
BF16 = mybir.dt.bfloat16
ALU = mybir.AluOpType
ACT = mybir.ActivationFunctionType
AX = mybir.AxisListType
DVE_ONLY = (mybir.EngineType.DVE,)
PE_ONLY = (mybir.EngineType.PE,)

P = 128
C = 64
HEADS = 4
REC = 68
SRC, DST, EC = 64, 65, 66
BIG = 1.0e30
LN_EPS = 1e-5
G = 4
RING = 4
BODY = G * RING
SG = 8


class Dims:
    def __init__(self, nodes, edges):
        self.N, self.E = nodes, edges
        self.NB = -(-nodes // (P * 8)) * 8
        assert nodes < self.NB * P <= P * P
        self.T1 = -(-edges // (P * 2 * SG)) * 2 * SG
        self.last_cols = edges - (P - 1) * self.T1
        assert self.last_cols > 0 and self.last_cols % (2 * SG) == 0
        self.NT = -(-((edges + self.NB * (P - 1)) // P) // BODY) * BODY
        self.NSLOT = self.NT * P
        self.PHANTOM = self.NB * P - 1

    def chunks(self):
        return [(c, min(P, self.NT - c)) for c in range(0, self.NT, P)]


def bcast(ap, axis, shape):
    return ap.unsqueeze(axis).to_broadcast(shape)


def constants(nc, sb, sem, K):
    K.ident = sb("ident", [P, P], F32)
    K.identb = sb("identb", [P, P], BF16)
    K.iota = sb("iota", [P, P], F32)
    K.iotab = sb("iotab", [P, P], BF16)
    K.ident128b = sb("ident128b", [P, P], BF16)
    K.ones = sb("ones", [P, P], F32)
    K.zero = sb("zero", [P, P], BF16)
    s_zero, s_made = sem("const_zeroed"), sem("const_made")
    with nc.Block() as block:
        @block.gpsimd
        def _(pool):
            nc.gpsimd.memset(K.ident[:, :], 0.0).then_inc(s_zero, 1)
            nc.gpsimd.memset(K.identb[:, :], 0.0).then_inc(s_zero, 1)
            nc.gpsimd.memset(K.ident128b[:, :], 0.0).then_inc(s_zero, 1)
            nc.gpsimd.memset(K.ones[:, :], 1.0).then_inc(s_made, 1)
            nc.gpsimd.memset(K.zero[:, :], 0.0).then_inc(s_made, 1)
            nc.gpsimd.iota(K.iota[:, :], pattern=[[1, P]], base=0, channel_multiplier=0,
                           allow_small_or_imprecise_dtypes=True).then_inc(s_made, 1)
            nc.gpsimd.iota(K.iotab[:, :], pattern=[[1, P]], base=0, channel_multiplier=0,
                           allow_small_or_imprecise_dtypes=True).then_inc(s_made, 1)
            pool.wait_ge(s_zero, 3)
            for m, v in ((K.ident, 1.0), (K.identb, 1.0), (K.ident128b, 128.0)):
                nc.gpsimd.affine_select(out=m[:, :], in_=m[:, :], compare_op=ALU.not_equal, fill=v, base=0,
                                        pattern=[[-1, P]], channel_multiplier=1).then_inc(s_made, 1)
            pool.wait_ge(s_made, 7)


def sort_edges(nc, sem, D, K, dram, A, Bl):
    T1, NB, NT, E = D.T1, D.NB, D.NT, D.E
    NG = T1 // SG
    with ExitStack() as ctx:
        def sb(n, s, d):
            return ctx.enter_context(nc.sbuf_tensor(n, s, d))

        def ps(n, s, d=F32):
            return ctx.enter_context(nc.psum_tensor(n, s, d))

        keyi = sb("keyi", [P, 2, T1], I32)
        parti = sb("parti", [P, T1], I32)
        keyf = sb("keyf", [P, 2, T1 + SG], F32)
        hilo = sb("hilo", [P, NG + 1, 2, 2, SG], BF16)
        w1 = sb("w1", [P, T1], F32)
        onehot = sb("onehot", [P, 2, 2, 2, SG, P], BF16)
        tri = sb("tri", [P, P], F32)
        triU = sb("triU", [P, P], F32)
        notph = sb("notph", [P, P], F32)
        tcol = sb("tcol", [P, NT], F32)
        ge = sb("ge", [P, NT], F32)
        hist = sb("hist", [P, 2, P], F32)
        base = sb("base", [P, 2, P], F32)
        tmp = sb("tmp_sort", [P, P], F32)
        rows = sb("rows", [P, 2], F32)
        rowi = sb("rowi", [P, 2], I32)
        ts = sb("ts", [P, 2], F32)
        patA = sb("patA", [P, 16, REC], F32)
        patB = sb("patB", [P, 16, 4], F32)
        keycol = sb("keycol", [P, 2, 2, SG], F32)
        hlcol = sb("hlcol", [P, 2, 2, 2, SG], BF16)
        ohT = sb("ohT", [P, 2, 2, SG, P], F32)
        Csb = sb("Csb", [P, 2, P], F32)
        junk = sb("junk", [P, 4, 2, 2, P], F32)
        cnt = sb("cnt", [P, 2, 2, SG], F32)
        sel = sb("sel", [P, 2, 2, SG], F32)
        pos = sb("pos", [P, 2, 2, SG], I32)
        rec = sb("rec", [P, 2, SG, REC], F32)
        ea = sb("ea", [P, 2, SG, C], F32)
        ea16 = sb("ea16", [P, 2, SG, 16], F32)
        prod16 = sb("prod16", [P, SG, 16], F32)
        a16 = sb("a16", [P, 16], F32)
        w1d = sb("w1d", [P, P], F32)
        w2d = sb("w2d", [P, P], F32)
        w3d = sb("w3d", [P, P], F32)
        bb = sb("bb", [P, 2], F32)
        b3 = sb("b3", [1, SG * C], F32)
        eaT = sb("eaT", [P, 4 * P], F32)
        h1 = sb("h1", [P, 4 * P], F32)
        h2 = sb("h2", [P, 4 * P], F32)

        s_key, s_par, s_wz = sem("keys_loaded"), sem("params_loaded"), sem("weights_zeroed")
        s_fill = sem("lists_prefilled")
        s_pat, s_tri0, s_tri = sem("patterns_made"), sem("tri_zeroed"), sem("tri_made")
        s_ph = sem("phantom_keys_set")
        s_chain = sem("keys_split_steps")

        with nc.Block() as block:
            @block.sync
            def _(sp):
                sp.wait_ge(s_ph, 1)
                for k, name in ((0, "dst"), (1, "src")):
                    n = (P - 1) * T1
                    sp.dma_start(keyi[0:P - 1, k, :], dram[name][0:n].rearrange("(p t) -> p t", t=T1)).then_inc(s_key, 16)
                    sp.dma_start(keyi[P - 1:P, k, 0:D.last_cols], dram[name][n:E].rearrange("(p t) -> p t", p=1)).then_inc(s_key, 16)
                n = (P - 1) * T1
                ew = dram["edge_weight1"].rearrange("e one -> (e one)")
                sp.dma_start(w1[0:P - 1, :], ew[0:n].rearrange("(p t) -> p t", t=T1)).then_inc(s_par, 16)
                sp.dma_start(w1[P - 1:P, 0:D.last_cols], ew[n:E].rearrange("(p t) -> p t", p=1)).then_inc(s_par, 16)
                sp.wait_ge(s_wz, 1)
                for w, name in ((w1d, "L0_gnn_W_fc1"), (w2d, "L0_gnn_W_fc2"), (w3d, "L0_gnn_W_fc3")):
                    for h in range(2):
                        sp.dma_start(w[h * C:(h + 1) * C, h * C:(h + 1) * C], dram[name]).then_inc(s_par, 16)
                for c, name in ((0, "L0_gnn_b_fc1"), (1, "L0_gnn_b_fc2")):
                    for h in range(2):
                        sp.dma_start(bb[h * C:(h + 1) * C, c:c + 1], dram[name].rearrange("(c o) -> c o", o=1)).then_inc(s_par, 16)
                for j in range(SG):
                    sp.dma_start(b3[0:1, j * C:(j + 1) * C], dram["L0_gnn_b_fc3"].rearrange("(o c) -> o c", o=1)).then_inc(s_par, 16)
                sp.dma_start(a16[:, :], dram["L3_gnn_a"][2 * C:2 * C + 16, :].rearrange("c o -> o c").to_broadcast([P, 16])).then_inc(s_par, 16)
                sp.wait_ge(s_pat, 4)
                sp.dma_start(A.rearrange("(p n t) c -> p n (t c)", p=P, t=16),
                             bcast(patA[:, :, :].rearrange("p t c -> p (t c)"), 1, [P, NT // 16, 16 * REC])).then_inc(s_fill, 16)
                sp.dma_start(Bl.rearrange("(p n t) c -> p n (t c)", p=P, t=16),
                             bcast(patB[:, :, :].rearrange("p t c -> p (t c)"), 1, [P, NT // 16, 64])).then_inc(s_fill, 16)
                sp.wait_ge(s_par, 16 * 21)
                sp.wait_ge(s_fill, 32)

            @block.gpsimd
            def _(pool):
                nc.gpsimd.memset(patA[:, :, :], 0.0).then_inc(s_pat, 1)
                nc.gpsimd.memset(patB[:, :, :], 0.0).then_inc(s_pat, 1)
                pool.wait_ge(s_pat, 2)
                nc.gpsimd.memset(patA[:, :, DST:DST + 1], -1.0).then_inc(s_pat, 1)
                nc.gpsimd.memset(patB[:, :, 0:1], -1.0).then_inc(s_pat, 1)
                nc.gpsimd.memset(rec[:, :, :, :], 0.0).then_inc(s_tri, 1)
                nc.gpsimd.iota(tcol[:, :], pattern=[[1, NT]], base=0, channel_multiplier=0,
                               allow_small_or_imprecise_dtypes=True).then_inc(s_tri, 1)
                nc.gpsimd.affine_select(out=tri[:, :], in_=K.ones[:, :], compare_op=ALU.is_gt, fill=0.0, base=0,
                                        pattern=[[-1, P]], channel_multiplier=1).then_inc(s_tri, 1)
                nc.gpsimd.affine_select(out=triU[:, :], in_=K.ones[:, :], compare_op=ALU.is_gt, fill=0.0, base=0,
                                        pattern=[[1, P]], channel_multiplier=-1).then_inc(s_tri, 1)
                nc.gpsimd.affine_select(out=notph[:, :], in_=K.ones[:, :], compare_op=ALU.not_equal, fill=0.0,
                                        base=-D.PHANTOM, pattern=[[1, P]], channel_multiplier=P).then_inc(s_tri, 1)
                pool.wait_ge(s_tri, 5)

            @block.vector
            def _(dve):
                n = [0]

                def step(ins):
                    n[0] += 1
                    ins.then_inc(s_chain, 1)
                    dve.wait_ge(s_chain, n[0])
                nc.vector.memset(w1[:, :], 0.0)
                nc.vector.memset(keyf[:, :, T1:T1 + SG], 0.0)
                nc.vector.memset(hilo[:, NG, :, :, :], 0.0)
                nc.vector.memset(keyi[:, :, :], D.PHANTOM).then_inc(s_ph, 1)
                nc.vector.memset(w1d[:, :], 0.0)
                nc.vector.memset(w2d[:, :], 0.0)
                nc.vector.memset(w3d[:, :], 0.0).then_inc(s_wz, 1)
                dve.wait_ge(s_key, 64)
                for k in range(2):
                    nc.vector.tensor_copy(keyf[:, k, 0:T1], keyi[:, k, :])
                    step(nc.vector.tensor_single_scalar(parti[:, :], keyi[:, k, :], 7, ALU.arith_shift_right))
                    step(nc.vector.tensor_copy(hilo[:, 0:NG, k, 0, :], parti[:, :].rearrange("p (g t) -> p g t", t=SG)))
                    step(nc.vector.tensor_single_scalar(parti[:, :], keyi[:, k, :], 127, ALU.bitwise_and))
                    step(nc.vector.tensor_copy(hilo[:, 0:NG, k, 1, :], parti[:, :].rearrange("p (g t) -> p g t", t=SG)))

        s_oh, s_h = sem("hist_onehot"), sem("hist_added")
        with ExitStack() as pctx:
            hps = [pctx.enter_context(nc.psum_tensor(f"hps{k}", [P, P], F32)) for k in range(2)]
            tps = pctx.enter_context(nc.psum_tensor("tps", [P, 2], F32))
            bps = pctx.enter_context(nc.psum_tensor("bps", [P, 512], F32))
            dps = pctx.enter_context(nc.psum_tensor("dps", [P, 2, P], F32))
            with nc.Block() as block:
                @block.vector
                def _(dve):
                    dve.sem_inc(s_h, 2)
                    with dve.Fori(0, NG // 2) as i:
                        for u in range(2):
                            g = i * 2 + u
                            dve.wait_ge(s_h, g + 1)
                            nc.vector.tensor_tensor(
                                onehot[:, u, :, :, :, :].rearrange("p k h t v -> p (k h t) v"),
                                bcast(K.iotab[:, :], 1, [P, 4 * SG, P]),
                                bcast(hilo[:, bass.ds(g, 1), :, :, :].rearrange("p o k h t -> p (o k h t)"), 2, [P, 4 * SG, P]),
                                ALU.is_equal).then_inc(s_oh, 1)

                @block.tensor
                def _(pe):
                    zero = K.zero
                    for k in range(2):
                        nc.tensor.matmul(hps[k][:, :], zero[:, :], zero[:, :], start=True, stop=False)
                    with pe.Fori(0, NG // 2) as i:
                        for u in range(2):
                            g = i * 2 + u
                            pe.wait_ge(s_oh, g + 1)
                            for j in range(SG):
                                for k in range(2):
                                    m = nc.tensor.matmul(hps[k][:, :], onehot[:, u, k, 0, j, :], onehot[:, u, k, 1, j, :],
                                                         start=False, stop=False)
                            m.then_inc(s_h, 1)
                    for k in range(2):
                        m = nc.tensor.matmul(hps[k][:, :], zero[:, :], zero[:, :], start=False, stop=True)
                    m.then_inc(s_h, 1)

            s_b, s_tp, s_bp, s_d, s_dp = (sem("base_steps"), sem("tile_starts_summed"), sem("tile_blocks_summed"),
                                          sem("hist_ready"), sem("degrees_turned"))
            s_ge, s_bc = sem("tile_compare"), sem("tile_blocks_copied")
            nchunk = -(-NT // 512)
            with nc.Block() as block:
                @block.vector
                def _(dve):
                    n = [0]

                    def step(ins):
                        n[0] += 1
                        ins.then_inc(s_b, 1)
                        dve.wait_ge(s_b, n[0])
                    for k in range(2):
                        step(nc.vector.tensor_tensor(hist[:, k, :], hps[k][:, :], notph[:, :], ALU.mult))
                    step(nc.vector.tensor_reduce(rows[:, :], hist[:, :, :], AX.X, ALU.add))
                    step(nc.vector.tensor_single_scalar(rowi[:, :], rows[:, :], float(P - 1), ALU.add))
                    step(nc.vector.tensor_single_scalar(rowi[:, :], rowi[:, :], 7, ALU.arith_shift_right))
                    nc.vector.tensor_copy(rows[:, :], rowi[:, :]).then_inc(s_d, 1)
                    dve.wait_ge(s_tp, 1)
                    step(nc.vector.tensor_copy(ts[:, :], tps[:, :]))
                    for k in range(2):
                        step(nc.vector.tensor_tensor_scan(base[:, k, :], K.ones[:, :], hist[:, k, :], 0.0, ALU.mult, ALU.add))
                        step(nc.vector.tensor_tensor(base[:, k, :], base[:, k, :], hist[:, k, :], ALU.subtract))
                        step(nc.vector.tensor_single_scalar(tmp[:, 0:1], ts[:, k:k + 1], float(P), ALU.mult))
                        step(nc.vector.tensor_scalar(base[:, k, :], base[:, k, :], tmp[:, 0:1], None, ALU.add))
                        step(nc.vector.tensor_scalar(tmp[:, :], notph[:, :], -1.0e6, 1.0e6, ALU.mult, ALU.add))
                        step(nc.vector.tensor_tensor(base[:, k, :], base[:, k, :], tmp[:, :], ALU.add))
                    for k in range(2):
                        if k:
                            dve.wait_ge(s_bp, nchunk)
                        nc.vector.tensor_scalar(ge[:, :], tcol[:, :], ts[:, k:k + 1], None, ALU.is_ge).then_inc(s_ge, 1)
                        for c in range(nchunk):
                            w = min(512, NT - c * 512)
                            dve.wait_ge(s_bp, k * nchunk + c + 1)
                            step(nc.vector.tensor_scalar(K.first[:, k, c * 512:c * 512 + w], bps[:, 0:w], -1.0, float(NB - 1), ALU.add, ALU.min))
                            nc.vector.tensor_copy(K.blk[0:1, k, c * 512:c * 512 + w], K.first[0:1, k, c * 512:c * 512 + w]).then_inc(s_bc, 1)
                        dve.wait_ge(s_bc, (k + 1) * nchunk)
                        step(nc.vector.tensor_single_scalar(K.first[:, k, :], K.first[:, k, :], float(P), ALU.mult))
                    dve.wait_ge(s_dp, 1)
                    step(nc.vector.tensor_copy(K.deg[:, :, :], dps[:, :, 0:NB]))

                @block.tensor
                def _(pe):
                    pe.wait_ge(s_d, 1)
                    nc.tensor.matmul(tps[:, :], triU[:, :], rows[:, :], start=True, stop=True).then_inc(s_tp, 1)
                    for k in range(2):
                        m = nc.tensor.transpose(dps[:, k, :], hist[:, k, :], K.ident[:, :])
                    m.then_inc(s_dp, 1)
                    for k in range(2):
                        pe.wait_ge(s_ge, k + 1)
                        for c in range(nchunk):
                            w = min(512, NT - c * 512)
                            if k or c:
                                pe.wait_ge(s_bc, k * nchunk + c)
                            nc.tensor.matmul(bps[:, 0:w], K.ones[:, :], ge[:, c * 512:c * 512 + w], start=True, stop=True).then_inc(s_bp, 1)

        look = [ps(f"look{i}", [P, 2, 2, P]) for i in range(4)]
        cps = [ps(f"cps{k}", [P, P]) for k in range(2)]
        otp = ps("otp", [P, SG, P], BF16)
        xps = ps("xps", [P, 512])

        s_ea = [sem(f"edge_attr_loaded{u}") for u in range(2)]
        s_one, s_kc = sem("sort_onehot"), sem("key_columns")
        s_ot, s_oc = sem("onehot_turned"), sem("onehot_copied")
        s_c0 = sem("counters_based")
        s_get, s_upd, s_cs = sem("counters_read"), [sem(f"counters_added{k}") for k in range(2)], [sem(f"counters_copied{k}") for k in range(2)]
        s_pick = sem("slots_picked")
        s_psum, s_pos = sem("slots_summed"), sem("slots_ready")
        s_xt, s_xc, s_m1, s_h1, s_m2, s_h2, s_m3 = (sem("attr_turned"), sem("attr_copied"), sem("fc1_done"), sem("silu1_done"),
                                                    sem("fc2_done"), sem("silu2_done"), sem("fc3_done"))
        s_free = sem("record_slots_free")
        s_p16, s_rec = sem("edge_term_products"), sem("records_ready")
        s_sc = [sem(f"scattered{u}") for u in range(2)]
        with nc.Block() as block:
            @block.sync
            def _(sp):
                def loads(i, rows_hi, after=None):
                    for u in range(2):
                        if after is not None:
                            sp.wait_ge(s_sc[u], (after + 1) * 2 * SG * 16)
                            sp.sem_inc(s_free, 1)
                        for lo, hi in ((0, 112), (112, rows_hi)):
                            for buf, view in ((ea, ea_v), (ea16, ea16_v)):
                                sp.dma_start(buf[lo:hi, u, :, :], view(lo, hi, i * 2 + u)).then_inc(s_ea[u], 16)

                def view_of(name, width):
                    full = dram[name][0:(P - 1) * T1, :].rearrange("(p t) c -> p t c", t=T1)
                    tail = dram[name][112 * T1:112 * T1 + (P - 113) * T1, :].rearrange("(p t) c -> p t c", t=T1)

                    def view(lo, hi, g):
                        if hi <= P - 1:
                            return full[lo:hi, bass.ds(g * SG, SG), :]
                        return bass.AP(tensor=tail.tensor, offset=tail.offset + g * (SG * width),
                                       ap=[[T1 * width, hi - lo], [width, SG], [1, width]])
                    return view
                ea_v, ea16_v = view_of("edge_attr_64", C), view_of("edge_attr_16", 16)
                full_bodies = D.last_cols // (2 * SG)
                loads(0, P)
                if full_bodies > 1:
                    with sp.Fori(0, full_bodies - 1) as i:
                        loads(i + 1, P, i)
                if full_bodies < NG // 2:
                    with sp.Fori(full_bodies - 1, NG // 2 - 1) as i:
                        loads(i + 1, P - 1, i)

            def onehots(g, u):
                nc.vector.tensor_tensor(
                    onehot[:, u, :, :, :, :].rearrange("p k h t v -> p (k h t) v"),
                    bcast(K.iotab[:, :], 1, [P, 4 * SG, P]),
                    bcast(hilo[:, bass.ds(g, 1), :, :, :].rearrange("p o k h t -> p (o k h t)"), 2, [P, 4 * SG, P]),
                    ALU.is_equal).then_inc(s_one, 1)

            @block.vector
            def _(dve):
                dve.sem_inc(s_rec, 2)
                dve.sem_inc(s_free, 2)
                onehots(0, 0)
                with dve.Fori(0, NG // 2) as i:
                    for u in range(2):
                        g = i * 2 + u
                        dve.wait_ge(s_upd[1], g * SG + 1)
                        onehots(g + 1, 1 - u)
                        dve.wait_ge(s_ea[u], (i + 1) * 64)
                        nc.vector.tensor_tensor(prod16[:, :, :], ea16[:, u, :, :], bcast(a16[:, :], 1, [P, SG, 16]), ALU.mult).then_inc(s_p16, 1)
                        dve.wait_ge(s_kc, g + 1)
                        dve.wait_ge(s_free, g + 1)
                        dve.wait_ge(s_p16, g + 1)
                        nc.vector.tensor_reduce(rec[:, u, :, EC], prod16[:, :, :], AX.X, ALU.add)
                        nc.vector.tensor_copy(rec[:, u, :, SRC], keycol[:, u, 1, :])
                        nc.vector.tensor_copy(rec[:, u, :, DST], keycol[:, u, 0, :])
                        for j in range(SG):
                            for k in range(2):
                                if k == 0:
                                    dve.wait_ge(s_get, g * SG + j + 1)
                                nc.vector.scalar_tensor_tensor(junk[:, j % 4, k, 0, :], look[j % 4][:, k, 0, :], keycol[:, u, k, j:j + 1],
                                                               tri[:, :], ALU.is_equal, ALU.mult, accum_out=cnt[:, u, k, j:j + 1])
                                m = nc.vector.scalar_tensor_tensor(junk[:, j % 4, k, 1, :], look[j % 4][:, k, 1, :], 1.0,
                                                                   onehot[:, u, k, 1, j, :], ALU.mult, ALU.mult,
                                                                   accum_out=sel[:, u, k, j:j + 1])
                            m.then_inc(s_pick, 1)
                        dve.wait_ge(s_pick, (g + 1) * SG + 4)
                        nc.vector.tensor_tensor(pos[:, u, :, :], cnt[:, u, :, :], sel[:, u, :, :], ALU.add).then_inc(s_pos, 1)
                        dve.wait_ge(s_m3, g + 1)
                        nc.vector.tensor_tensor(rec[:, u, :, 0:C], xps[:, :].rearrange("p (t c) -> p t c", c=C),
                                                bcast(w1[:, bass.ds(g * SG, SG)], 2, [P, SG, C]), ALU.mult).then_inc(s_rec, 1)

            @block.gpsimd
            def _(pool):
                with pool.Fori(0, NG // 2) as i:
                    for u in range(2):
                        g = i * 2 + u
                        pool.wait_ge(s_pos, g + 1)
                        pool.wait_ge(s_rec, g + 3)
                        pool.nop(nofuse=True)
                        for j in range(SG):
                            for k, out, row in ((0, A, rec[:, u, j, :]), (1, Bl, rec[:, u, j, SRC:SRC + 4])):
                                nc.gpsimd.indirect_dma_start(
                                    out=out, out_offset=bass.IndirectOffsetOnAxis(ap=pos[:, u, k, j:j + 1], axis=0),
                                    in_=row, in_offset=None, bounds_check=D.NSLOT - 1, oob_is_err=False).then_inc(s_sc[u], 16)
                for u in range(2):
                    pool.wait_ge(s_sc[u], NG // 2 * 2 * SG * 16)

            @block.scalar
            def _(act):
                act.wait_ge(s_c0, 1)
                for k in range(2):
                    nc.scalar.copy(Csb[:, k, :], cps[k][:, :]).then_inc(s_cs[k], 1)
                def keycols(g, u):
                    nc.scalar.copy(keycol[:, u, :, :], keyf[:, :, bass.ds(g * SG, SG)])
                    nc.scalar.copy(hlcol[:, u, :, :, :].rearrange("p k h t -> p (k h t)"),
                                   hilo[:, bass.ds(g, 1), :, :, :].rearrange("p o k h t -> p (o k h t)")).then_inc(s_kc, 1)

                def turn_copy(g, u, k):
                    act.wait_ge(s_ot, g * 2 + k + 1)
                    nc.scalar.copy(ohT[:, u, k, :, :], otp[:, :, :]).then_inc(s_oc, 1)
                for k in range(2):
                    turn_copy(0, 0, k)
                keycols(0, 0)
                with act.Fori(0, NG // 2) as i:
                    for u in range(2):
                        g = i * 2 + u
                        v = 1 - u
                        for j in range(SG):
                            for k in range(2):
                                act.wait_ge(s_upd[k], g * SG + j + 2)
                                nc.scalar.copy(Csb[:, k, :], cps[k][:, :]).then_inc(s_cs[k], 1)
                            if j == 1:
                                act.wait_ge(s_xt, g + 1)
                                nc.scalar.copy(eaT[:, :], xps[:, :]).then_inc(s_xc, 1)
                            if j == 1:
                                turn_copy(g + 1, v, 0)
                            if j == 3:
                                act.wait_ge(s_m1, g + 1)
                                nc.scalar.activation(h1[:, :], xps[:, :], ACT.Silu, bias=bb[:, 0:1]).then_inc(s_h1, 1)
                            if j == 5:
                                act.wait_ge(s_m2, g + 1)
                                nc.scalar.activation(h2[:, :], xps[:, :], ACT.Silu, bias=bb[:, 1:2]).then_inc(s_h2, 1)
                            if j == 5:
                                turn_copy(g + 1, v, 1)
                            if j == 3:
                                act.wait_ge(s_pick, g * SG + 4)
                                keycols(g + 1, v)

            @block.tensor
            def _(pe):
                def turn(g, u, k):
                    pe.wait_ge(s_oc, g * 2 + k + 1)
                    for j in range(SG):
                        m = nc.tensor.transpose(otp[:, j, :], onehot[:, u, k, 0, j, :], K.identb[:, :])
                    m.then_inc(s_ot, 1)
                pe.sem_inc(s_oc, 1)
                pe.sem_inc(s_pick, 4)
                pe.sem_inc(s_upd[0], 1)
                pe.sem_inc(s_upd[1], 1)
                for k in range(2):
                    m = nc.tensor.matmul(cps[k][:, :], K.ident[:, :], base[:, k, :], start=True, stop=True)
                m.then_inc(s_c0, 1)
                pe.wait_ge(s_one, 1)
                for k in range(2):
                    turn(0, 0, k)
                with pe.Fori(0, NG // 2) as i:
                    for u in range(2):
                        g = i * 2 + u
                        v = 1 - u
                        pe.wait_ge(s_kc, g + 1)
                        pe.wait_ge(s_oc, g * 2 + 3)
                        for j in range(SG):
                            pe.wait_ge(s_pick, g * SG + j + 1)
                            for k in range(2):
                                nc.tensor.matmul(look[j % 4][:, k, 0, :], hlcol[:, u, k, 0, j:j + 1].to_broadcast([P, P]),
                                                 K.ident128b[:, :], start=True, stop=False)
                                nc.tensor.matmul(look[j % 4][:, k, 0, :], hlcol[:, u, k, 1, j:j + 1].to_broadcast([P, P]),
                                                 K.identb[:, :], start=False, stop=True)
                            for k in range(2):
                                pe.wait_ge(s_cs[k], g * SG + j + 1)
                                m = nc.tensor.matmul(look[j % 4][:, k, 1, :], ohT[:, u, k, j, :], Csb[:, k, :], start=True, stop=True)
                                if k == 1:
                                    m.then_inc(s_get, 1)
                                nc.tensor.matmul(cps[k][:, :], K.ident[:, :], Csb[:, k, :], start=True, stop=False)
                                nc.tensor.matmul(cps[k][:, :], onehot[:, u, k, 0, j, :], onehot[:, u, k, 1, j, :],
                                                 start=False, stop=True).then_inc(s_upd[k], 1)
                            if j == 1:
                                pe.wait_ge(s_ea[u], (i + 1) * 64)
                                pe.wait_ge(s_rec, g + 2)
                                for q in range(SG // 2):
                                    m = nc.tensor.transpose(xps[:, q * P:(q + 1) * P],
                                                            ea[:, u, 2 * q:2 * q + 2, :].rearrange("p t c -> p (t c)"), K.ident[:, :])
                                m.then_inc(s_xt, 1)
                            if j == 0:
                                pe.wait_ge(s_one, g + 2)
                                turn(g + 1, v, 0)
                            if j == 3:
                                pe.wait_ge(s_xc, g + 1)
                                nc.tensor.matmul(xps[:, :], w1d[:, :], eaT[:, :], start=True, stop=True).then_inc(s_m1, 1)
                            if j == 4:
                                turn(g + 1, v, 1)
                            if j == 5:
                                pe.wait_ge(s_h1, g + 1)
                                nc.tensor.matmul(xps[:, :], w2d[:, :], h1[:, :], start=True, stop=True).then_inc(s_m2, 1)
                            if j == 7:
                                pe.wait_ge(s_h2, g + 1)
                                for q in range(SG // 2):
                                    nc.tensor.matmul(xps[:, q * P:(q + 1) * P], h2[:, q * P:(q + 1) * P], w3d[:, :], start=True, stop=False)
                                    m = nc.tensor.matmul(xps[:, q * P:(q + 1) * P], K.ones[0:1, :], b3[0:1, q * P:(q + 1) * P],
                                                         start=False, stop=True)
                                m.then_inc(s_m3, 1)


class Shared:
    pass


class Count:

    def __init__(self, s):
        self.sem = s
        self.base = 0


class Counts:

    def __init__(self, sem):
        self.make, self.known = sem, {}

    def get(self, name):
        if name not in self.known:
            self.known[name] = Count(self.make(name))
        return self.known[name]


def finished(*added):
    for s, n in added:
        s.base += n


def wait(eng, s, value):
    if isinstance(value, int) and value <= 0:
        return
    if isinstance(s, Count):
        eng.wait_ge(s.sem, value + s.base)
    else:
        eng.wait_ge(s, value)


def loop(eng, n, body):
    body(0, n == 1)
    if n > 2:
        with eng.Fori(1, n - 1) as i:
            body(i, False)
    if n > 1:
        body(n - 1, True)


def node_stage(nc, counts, D, K, name, kin, weights, widths, feed, evict, table=None, bias=True, feed_ops=1):
    n = D.NB // 8
    tw = table.shape[1] if table is not None else 4
    rows = kin + 1 if bias else kin
    with ExitStack() as ctx:
        fed = ctx.enter_context(nc.sbuf_tensor(f"{name}_fed", [P, 2, 4, kin], F32))
        fedT = ctx.enter_context(nc.sbuf_tensor(f"{name}_fedT", [P, 2, 4 * P], F32))
        stage = ctx.enter_context(nc.sbuf_tensor(f"{name}_stage", [P, 2, 4, tw], F32))
        turned = [ctx.enter_context(nc.psum_tensor(f"{name}_turned{u}", [P, 4 * P], F32)) for u in range(2)]
        prod = [[ctx.enter_context(nc.psum_tensor(f"{name}_prod{u}{c}", [P, 4, w], F32)) for c, w in enumerate(widths)]
                for u in range(2)]
        s_fed, s_turn, s_copy, s_mm, s_ev = (counts.get("node_fed"), counts.get("node_turned"), counts.get("node_copied"),
                                             counts.get("node_products"), counts.get("node_evicted"))
        s_one = counts.get("node_ones")
        s_tab = [counts.get(f"node_stored{u}") for u in range(2)]
        with nc.Block() as block:
            @block.gpsimd
            def _(pool):
                nc.gpsimd.memset(stage[:, :, :, :], 0.0).then_inc(s_one.sem, 1)

            @block.vector
            def _(dve):
                def fed_group(i, u):
                    g = i * 2 + u
                    wait(dve, s_turn, g - 1)
                    feed(dve, g, fed[:, u, :, :]).then_inc(s_fed.sem, 1)
                if bias:
                    nc.vector.memset(fedT[kin:kin + 1, :, :], 1.0).then_inc(s_one.sem, 1)
                wait(dve, s_one, 2 if bias else 1)
                for u in range(2):
                    fed_group(0, u)

                def body(i, last):
                    for u in range(2):
                        g = i * 2 + u
                        wait(dve, s_mm, g + 1)
                        if table is not None:
                            wait(dve, s_tab[u], i * 16)
                        evict(dve, g, [prod[u][c][:, :, :] for c in range(len(widths))], stage[:, u, :, :]).then_inc(s_ev.sem, 1)
                        if not last:
                            fed_group(i + 1, u)
                loop(dve, n, body)

            @block.scalar
            def _(act):
                wait(act, s_one, 2 if bias else 1)

                def body(i, last):
                    for u in range(2):
                        g = i * 2 + u
                        wait(act, s_turn, g + 1)
                        wait(act, s_mm, g - 1)
                        nc.scalar.copy(fedT[0:kin, u, :], turned[u][0:kin, :]).then_inc(s_copy.sem, 1)
                loop(act, n, body)

            @block.tensor
            def _(pe):
                def body(i, last):
                    for u in range(2):
                        g = i * 2 + u
                        wait(pe, s_fed, g + 1)
                        wait(pe, s_copy, g - 1)
                        pe.nop(nofuse=True)
                        for j in range(4):
                            m = nc.tensor.transpose(turned[u][0:kin, j * P:(j + 1) * P], fed[:, u, j, :], K.ident[:, :])
                        m.then_inc(s_turn.sem, 1)
                        wait(pe, s_copy, g + 1)
                        wait(pe, s_ev, g - 1)
                        for j in range(4):
                            c0 = 0
                            for c, w in enumerate(widths):
                                m = nc.tensor.matmul(prod[u][c][:, j, :], fedT[0:rows, u, j * P:(j + 1) * P],
                                                     weights[0:rows, c0:c0 + w], start=True, stop=True)
                                c0 += w
                        m.then_inc(s_mm.sem, 1)
                loop(pe, n, body)

            if table is not None:
                @block.sync
                def _(sp):
                    view = table.rearrange("(g j p) c -> p g j c", j=4, p=P)

                    def body(i, last):
                        for u in range(2):
                            g = i * 2 + u
                            wait(sp, s_ev, g + 1)
                            sp.dma_start(view[:, bass.ds(g, 1), :, :].rearrange("p o j c -> p (o j) c"), stage[:, u, :, :]).then_inc(s_tab[u].sem, 16)
                    loop(sp, n, body)
                    for u in range(2):
                        wait(sp, s_tab[u], n * 16)
        finished(*[(s, 2 * n) for s in (s_fed, s_turn, s_copy, s_mm, s_ev)], (s_one, 2 if bias else 1),
                 *[(s, 16 * n) for s in s_tab if table is not None])



def layer_norm(nc, counts, D, K, name, out=None):
    NB = D.NB
    with ExitStack() as ctx:
        sq = ctx.enter_context(nc.sbuf_tensor(f"{name}_sq", [P, NB, C], F32))
        m = ctx.enter_context(nc.sbuf_tensor(f"{name}_m", [P, NB], F32))
        v = ctx.enter_context(nc.sbuf_tensor(f"{name}_v", [P, NB], F32))
        s_step, s_c, s_sq, s_v, s_sd, s_out = (counts.get("norm_steps"), counts.get("norm_centred"), counts.get("norm_squared"),
                                               counts.get("norm_var"), counts.get("norm_sd"), counts.get("norm_stored"))
        s_x = counts.get("norm_normed")
        with nc.Block() as block:
            @block.vector
            def _(dve):
                step = stepper(dve, s_step)
                step(nc.vector.tensor_reduce(m[:, :], K.x[:, :, :], AX.X, ALU.add))
                step(nc.vector.tensor_single_scalar(m[:, :], m[:, :], 1.0 / C, ALU.mult))
                nc.vector.tensor_tensor(K.x[:, :, :], K.x[:, :, :], bcast(m[:, :], 2, [P, NB, C]), ALU.subtract).then_inc(s_c.sem, 1)
                wait(dve, s_sq, 1)
                step(nc.vector.tensor_reduce(v[:, :], sq[:, :, :], AX.X, ALU.add))
                nc.vector.tensor_scalar(v[:, :], v[:, :], 1.0 / C, LN_EPS, ALU.mult, ALU.add).then_inc(s_v.sem, 1)
                wait(dve, s_sd, 1)
                step(nc.vector.reciprocal(v[:, :], v[:, :]))
                nc.vector.tensor_tensor(K.x[:, :, :], K.x[:, :, :], bcast(v[:, :], 2, [P, NB, C]), ALU.mult).then_inc(s_x.sem, 1)

            @block.scalar
            def _(act):
                wait(act, s_c, 1)
                nc.scalar.activation(sq[:, :, :], K.x[:, :, :], ACT.Square).then_inc(s_sq.sem, 1)
                wait(act, s_v, 1)
                nc.scalar.activation(v[:, :], v[:, :], ACT.Sqrt).then_inc(s_sd.sem, 1)

            if out is not None:
                @block.sync
                def _(sp):
                    full = D.N // P
                    wait(sp, s_x, 1)
                    sp.dma_start(out[0:full * P, :].rearrange("(b p) c -> p b c", p=P), K.x[:, 0:full, :]).then_inc(s_out.sem, 16)
                    if D.N > full * P:
                        sp.dma_start(out[full * P:D.N, :], K.x[0:D.N - full * P, full, :]).then_inc(s_out.sem, 16)
                    wait(sp, s_out, 32 if D.N > full * P else 16)
        finished((s_step, 4), *[(s, 1) for s in (s_c, s_sq, s_v, s_sd, s_x)])



def stepper(eng, s):
    n = [0]

    def step(ins):
        n[0] += 1
        ins.then_inc(s.sem if isinstance(s, Count) else s, 1)
        wait(eng, s, n[0])
    return step


def load_nodes(nc, sem, D, K, dram):
    s_z, s_x = sem("nodes_zeroed"), sem("nodes_loaded")
    with nc.Block() as block:
        @block.gpsimd
        def _(pool):
            nc.gpsimd.memset(K.x[:, :, :], 0.0).then_inc(s_z, 1)

        @block.sync
        def _(sp):
            full = D.N // P
            sp.wait_ge(s_z, 1)
            sp.dma_start(K.x[:, 0:full, :], dram["x"][0:full * P, :].rearrange("(b p) c -> p b c", p=P)).then_inc(s_x, 16)
            if D.N > full * P:
                sp.dma_start(K.x[0:D.N - full * P, full, :], dram["x"][full * P:D.N, :]).then_inc(s_x, 16)
            sp.wait_ge(s_x, 32 if D.N > full * P else 16)


def score_edges(nc, sem, D, K, A, tabS, tabD, wkv, al, V):
    NT = D.NT
    n = NT // BODY
    with ExitStack() as ctx:
        def sb(nm, s, d=F32):
            return ctx.enter_context(nc.sbuf_tensor(nm, s, d))

        def ps(nm, s, d=F32):
            return ctx.enter_context(nc.psum_tensor(nm, s, d))
        rec = sb("sc_rec", [P, RING, G, REC])
        idx = sb("sc_idx", [P, RING, G], I32)
        rows = sb("sc_rows", [P, RING, G, C])
        oh = sb("sc_oh", [P, 2, G, P], BF16)
        ohT = sb("sc_ohT", [P, 2, G, P])
        tp = sb("sc_tp", [P, 2, G, C])
        tpT = sb("sc_tpT", [P, 2, G * P])
        kv = sb("sc_kv", [P, RING, G, P])
        qk = sb("sc_qk", [P, 2, G, C])
        ot = [ps(f"sc_ot{u}", [P, G, P], BF16) for u in range(2)]
        loc = [ps(f"sc_loc{u}", [P, G, P]) for u in range(2)]
        tt = ps("sc_tt", [P, G * P])
        kvp = [ps(f"sc_kvp{u}", [P, G, P]) for u in range(2)]
        s_ld = [sem(f"sc_loaded{u}") for u in range(RING)]
        s_ga = [sem(f"sc_gathered{u}") for u in range(RING)]
        s_vs = [sem(f"sc_stored{u}") for u in range(RING)]
        s_idx, s_kl, s_oh, s_ot, s_ohT, s_loc, s_sum, s_tp, s_tt, s_tpT, s_kvp, s_kv, s_qk, s_al, s_one, s_keep = (
            sem("sc_" + x) for x in ("indices", "keys", "onehots", "turned", "turned_copied", "dst_rows", "sums", "messages",
                                     "msg_turned", "msg_copied", "kv_products", "kv_copied", "qk_products", "scores", "ones", "kept"))
        recv = A.rearrange("(g j p) c -> p g j c", j=G, p=P)
        vv = V.rearrange("(g p j) c -> p g j c", j=G, p=P)
        with nc.Block() as block:
            @block.sync
            def _(sp):
                def load(g, u):
                    sp.dma_start(rec[:, u, :, :], recv[:, bass.ds(g, 1), :, :].rearrange("p o j c -> p (o j) c")).then_inc(s_ld[u], 16)
                for u in range(RING):
                    load(u, u)

                def body(i, last):
                    for u in range(RING):
                        g = i * RING + u
                        sp.wait_ge(s_kv, g + 1)
                        sp.dma_start(vv[:, bass.ds(g, 1), :, :].rearrange("p o j c -> p (o j) c"), kv[:, u, :, C:2 * C]).then_inc(s_vs[u], 16)
                        if not last:
                            sp.wait_ge(s_tp, g + 1)
                            sp.wait_ge(s_keep, g + 1)
                            load(g + RING, u)
                loop(sp, n, body)
                for u in range(RING):
                    sp.wait_ge(s_vs[u], n * 16)

            @block.gpsimd
            def _(pool):
                def body(i, last):
                    for u in range(RING):
                        g = i * RING + u
                        pool.wait_ge(s_idx, g + 1)
                        pool.nop(nofuse=True)
                        for j in range(G):
                            nc.gpsimd.indirect_dma_start(out=rows[:, u, j, :], out_offset=None, in_=tabS,
                                                         in_offset=bass.IndirectOffsetOnAxis(ap=idx[:, u, j:j + 1], axis=0)).then_inc(s_ga[u], 16)
                loop(pool, n, body)

            @block.scalar
            def _(act):
                def prep(i, u):
                    g = i * RING + u
                    act.wait_ge(s_ld[u], (i + 1) * 16)
                    nc.scalar.copy(idx[:, u, :], rec[:, u, :, SRC]).then_inc(s_idx, 1)
                    nc.scalar.copy(K.idx[0][:, bass.ds(g * G, G)], rec[:, u, :, SRC])
                    nc.scalar.copy(K.ec[0][:, bass.ds(g * G, G)], rec[:, u, :, EC]).then_inc(s_keep, 1)

                def body(i, last):
                    for u in range(RING):
                        g = i * RING + u
                        w = u % 2
                        if u < 2:
                            prep(i, u + 2)
                        elif not last:
                            prep(i + 1, u - 2)
                        act.wait_ge(s_ot, g + 1)
                        wait(act, s_loc, g - 1)
                        nc.scalar.copy(ohT[:, w, :, :], ot[w][:, :, :]).then_inc(s_ohT, 1)
                        act.wait_ge(s_tt, g + 1)
                        wait(act, s_kvp, g - 1)
                        nc.scalar.copy(tpT[0:C, w, :], tt[0:C, :]).then_inc(s_tpT, 1)
                        act.wait_ge(s_kvp, g + 1)
                        wait(act, s_qk, g - RING + 1)
                        wait(act, s_vs[u], i * 16)
                        nc.scalar.copy(kv[:, u, :, :], kvp[w][:, :, :]).then_inc(s_kv, 1)
                prep(0, 0)
                prep(0, 1)
                loop(act, n, body)

            @block.tensor
            def _(pe):
                pe.wait_ge(s_one, 1)

                def body(i, last):
                    bs = nc.values_load_multi_w_load_instructions(K.blk[0:1, 0, bass.ds(i * BODY, BODY)], engines=PE_ONLY,
                                                                  min_val=0, max_val=D.NB - 1)[1]
                    for u in range(RING):
                        g = i * RING + u
                        w = u % 2
                        pe.wait_ge(s_oh, g + 1)
                        wait(pe, s_ohT, g - 1)
                        for j in range(G):
                            m = nc.tensor.transpose(ot[w][:, j, :], oh[:, w, j, :], K.identb[:, :])
                        m.then_inc(s_ot, 1)
                        pe.wait_ge(s_ohT, g + 1)
                        wait(pe, s_qk, g - 1)
                        for j in range(G):
                            m = nc.tensor.matmul(loc[w][:, j, :], ohT[:, w, j, :], tabD[:, bass.ds(bs[u * G + j], 1), :].rearrange("p o c -> p (o c)"),
                                                 start=True, stop=True)
                        m.then_inc(s_loc, 1)
                        pe.wait_ge(s_tp, g + 1)
                        wait(pe, s_tpT, g)
                        pe.nop(nofuse=True)
                        for j in range(G):
                            m = nc.tensor.transpose(tt[0:C, j * P:(j + 1) * P], tp[:, w, j, :], K.ident[:, :])
                        m.then_inc(s_tt, 1)
                        pe.wait_ge(s_tpT, g + 1)
                        wait(pe, s_kv, g - 1)
                        for j in range(G):
                            m = nc.tensor.matmul(kvp[w][:, j, :], tpT[0:C + 1, w, j * P:(j + 1) * P], wkv[0:C + 1, :], start=True, stop=True)
                        m.then_inc(s_kvp, 1)
                loop(pe, n, body)

            @block.vector
            def _(dve):
                def prep(i, u):
                    g = i * RING + u
                    w = u % 2
                    dve.wait_ge(s_ld[u], (i + 1) * 16)
                    nc.vector.tensor_tensor(K.kl[0][:, bass.ds(g * G, G)], rec[:, u, :, DST], K.first[:, 0, bass.ds(g * G, G)],
                                            ALU.subtract).then_inc(s_kl, 1)
                    dve.wait_ge(s_kl, g + 1)
                    wait(dve, s_ot, g - 1)
                    nc.vector.tensor_tensor(oh[:, w, :, :], bcast(K.iota[:, :], 1, [P, G, P]),
                                            bcast(K.kl[0][:, bass.ds(g * G, G)], 2, [P, G, P]), ALU.is_equal).then_inc(s_oh, 1)

                def scores(i, u):
                    g = i * RING + u
                    w = u % 2
                    dve.wait_ge(s_kv, g + 1)
                    nc.vector.tensor_tensor(qk[:, w, :, :], loc[w][:, :, C:2 * C], kv[:, u, :, 0:C], ALU.mult).then_inc(s_qk, 1)
                    dve.wait_ge(s_qk, g + 1)
                    nc.vector.tensor_reduce(al[:, bass.ds(g * G, G), :], qk[:, w, :, :].rearrange("p j (h d) -> p j h d", h=HEADS),
                                            AX.X, ALU.add).then_inc(s_al, 1)

                def body(i, last):
                    for u in range(RING):
                        g = i * RING + u
                        w = u % 2
                        if u < 3:
                            prep(i, u + 1)
                        elif not last:
                            prep(i + 1, 0)
                        dve.wait_ge(s_loc, g + 1)
                        dve.wait_ge(s_ga[u], (i + 1) * 16 * G)
                        wait(dve, s_tt, g - 1)
                        nc.vector.tensor_tensor(tp[:, w, :, :], rows[:, u, :, :], loc[w][:, :, 0:C], ALU.add).then_inc(s_sum, 1)
                        dve.wait_ge(s_sum, g + 1)
                        nc.vector.tensor_tensor(tp[:, w, :, :], tp[:, w, :, :], rec[:, u, :, 0:C], ALU.mult).then_inc(s_tp, 1)
                        wait(dve, s_al, g - 2)
                        if u > 0:
                            scores(i, u - 1)
                        elif not (isinstance(i, int) and i == 0):
                            scores(i - 1, RING - 1)
                nc.vector.memset(tpT[C:C + 1, :, :], 1.0).then_inc(s_one, 1)
                prep(0, 0)
                loop(dve, n, body)
                scores(n - 1, RING - 1)


def segment_softmax(nc, counts, D, K, name, X, heads, k, slope=None, last=None):
    NT, NSLOT = D.NT, D.NSLOT
    chunks = D.chunks()
    with ExitStack() as ctx:
        def sb(nm, s, d=F32):
            return ctx.enter_context(nc.sbuf_tensor(f"{name}_{nm}", s, d))
        keyT = sb("key", [P, NT])
        keys = sb("keys", [P, 3, NT])
        pen = sb("pen", [P, 2, NT])
        val = sb("val", [P, NT])
        run = sb("run", [P, 2, NT])
        edge = sb("edge", [P, 2, 2])
        rowv = sb("row", [1, 2, 2, P])
        crow = sb("crow", [1, 2, P + 2])
        carry = sb("carry", [P, 2])
        turn = sb("turn", [P, 2, P])
        turnd = sb("turnd", [P, 2, P])
        sent = sb("sent", [1, 1])
        kd = nc.dram_tensor(f"{name}_keys_dram", (NSLOT + 2,), F32).ap()
        sd = nc.dram_tensor(f"{name}_scores_dram", (NSLOT,), F32).ap()
        md = nc.dram_tensor(f"{name}_maxima_dram", (NSLOT,), F32).ap()
        tps = [ctx.enter_context(nc.psum_tensor(f"{name}_t{u}", [P, P], F32)) for u in range(2)]
        rps = ctx.enter_context(nc.psum_tensor(f"{name}_r", [1, 2, 2, P], F32))
        cps = ctx.enter_context(nc.psum_tensor(f"{name}_c", [P, 2], F32))

        outward = [(keyT[:, :], kd[1:NSLOT + 1])]
        s_a = [counts.get(f"soft_out{u}") for u in range(2)]
        s_b = [counts.get(f"soft_in{u}") for u in range(2)]
        s_t, s_c = counts.get("soft_turned"), counts.get("soft_turn_copied")
        s_st, s_e, s_r, s_cr, s_cp, s_ld, s_v, s_x, s_w = (counts.get(f"soft_{x}") for x in (
            "steps", "ends", "rows", "carry_row", "carry_col", "loaded", "scanned", "exped", "written"))
        s_i = counts.get("soft_init")
        count = [0]
        outs = [0]
        ins_ = [0]

        def send(src_of, dst, n0, n_out):
            with nc.Block() as block:
                @block.tensor
                def _(pe):
                    for q, (c, w) in enumerate(chunks):
                        wait(pe, s_c, n0 + q - 1)
                        nc.tensor.transpose(tps[(n0 + q) % 2][0:w, :], src_of(c, w), K.ident[:, :]).then_inc(s_t.sem, 1)

                @block.vector
                def _(dve):
                    for q, (c, w) in enumerate(chunks):
                        wait(dve, s_t, n0 + q + 1)
                        u = (n_out + q) % 2
                        wait(dve, s_a[u], (n_out + q) // 2 * 16)
                        nc.vector.tensor_copy(turn[0:w, u, :], tps[(n0 + q) % 2][0:w, :]).then_inc(s_c.sem, 1)

                @block.sync
                def _(sp):
                    for q, (c, w) in enumerate(chunks):
                        wait(sp, s_c, n0 + q + 1)
                        u = (n_out + q) % 2
                        sp.dma_start(dst[c * P:(c + w) * P].rearrange("(t p) -> t p", p=P), turn[0:w, u, :]).then_inc(s_a[u].sem, 16)
                    for u in range(2):
                        wait(sp, s_a[u], (n_out + len(chunks) + 1 - u) // 2 * 16)

        def receive(src, dst_of, n0, n_in):
            with nc.Block() as block:
                @block.sync
                def _(sp):
                    for q, (c, w) in enumerate(chunks):
                        u = (n_in + q) % 2
                        wait(sp, s_t, n0 + q - 1)
                        sp.dma_start(turnd[0:w, u, :], src[c * P:(c + w) * P].rearrange("(t p) -> t p", p=P)).then_inc(s_b[u].sem, 16)

                @block.tensor
                def _(pe):
                    for q, (c, w) in enumerate(chunks):
                        u = (n_in + q) % 2
                        wait(pe, s_b[u], ((n_in + q) // 2 + 1) * 16)
                        wait(pe, s_c, n0 + q - 1)
                        nc.tensor.transpose(tps[(n0 + q) % 2][:, 0:w], turnd[0:w, u, :], K.ident[0:w, 0:w]).then_inc(s_t.sem, 1)

                @block.vector
                def _(dve):
                    for q, (c, w) in enumerate(chunks):
                        wait(dve, s_t, n0 + q + 1)
                        nc.vector.tensor_copy(dst_of(c, w), tps[(n0 + q) % 2][:, 0:w]).then_inc(s_c.sem, 1)

        with nc.Block() as block:
            @block.vector
            def _(dve):
                nc.vector.tensor_tensor(keyT[:, :], K.kl[k][:, 0:NT], K.first[:, k, :], ALU.add)
                nc.vector.memset(sent[:, :], -5.0).then_inc(s_i.sem, 1)
                nc.vector.memset(crow[:, :, :], -BIG)

            @block.sync
            def _(sp):
                wait(sp, s_i, 1)
                sp.dma_start(kd[0:1].rearrange("(o c) -> o c", o=1), sent[:, :]).then_inc(s_w.sem, 16)
                sp.dma_start(kd[NSLOT + 1:NSLOT + 2].rearrange("(o c) -> o c", o=1), sent[:, :]).then_inc(s_w.sem, 16)
                wait(sp, s_w, 32)
        nch = len(chunks)
        turns = stores = loads = 0
        send(lambda c, w: keyT[:, c:c + w], kd[1:NSLOT + 1], turns, stores)
        turns += nch
        stores += nch
        steps = [0]

        def stepv(dve, ins):
            steps[0] += 1
            ins.then_inc(s_st.sem, 1)
            wait(dve, s_st, steps[0])
        with nc.Block() as block:
            @block.sync
            def _(sp):
                for d in range(3):
                    sp.dma_start(keys[:, d, :], kd[d:d + NSLOT].rearrange("(p t) -> p t", p=P)).then_inc(s_ld.sem, 16)

            @block.vector
            def _(dve):
                wait(dve, s_ld, 48)
                for side, d in ((0, 0), (1, 2)):
                    stepv(dve, nc.vector.tensor_tensor(pen[:, side, :], keys[:, d, :], keys[:, 1, :], ALU.is_equal))
                if last is not None:
                    stepv(dve, nc.vector.tensor_scalar(keys[:, 0, :], pen[:, 1, :], -1.0, 1.0, ALU.mult, ALU.add))
                stepv(dve, nc.vector.tensor_scalar(pen[:, :, :], pen[:, :, :], BIG, -BIG, ALU.mult, ALU.add))
                for side in range(2):
                    stepv(dve, nc.vector.tensor_reduce(edge[:, side, 0:1], pen[:, side, :], AX.X, ALU.min))
        loaded = 3
        for h in range(heads):
            send(lambda c, w: X[:, c:c + w, h], sd, turns, stores)
            turns += nch
            stores += nch
            with nc.Block() as block:
                @block.sync
                def _(sp):
                    sp.dma_start(val[:, :], sd.rearrange("(p t) -> p t", p=P)).then_inc(s_ld.sem, 16)
                    wait(sp, s_x, h + 1)
                    sp.dma_start(sd.rearrange("(p t) -> p t", p=P), val[:, :]).then_inc(s_w.sem, 16)
                    if last is not None:
                        wait(sp, s_v, h + 1)
                        sp.dma_start(md.rearrange("(p t) -> p t", p=P), run[:, 1, :]).then_inc(s_w.sem, 16)
                    wait(sp, s_w, 32 + 16 * (h + 1) * (2 if last is not None else 1))

                @block.vector
                def _(dve):
                    wait(dve, s_ld, 16 * (4 + h))
                    if slope is not None:
                        stepv(dve, nc.vector.scalar_tensor_tensor(val[:, :], val[:, :], slope, val[:, :], ALU.mult, ALU.max))

                    def scans(initial):
                        f0, f1, fo = pen[:, 0, :], val[:, :], run[:, 0, :]
                        stepv(dve, nc.vector.tensor_tensor_scan(fo, f0, f1, initial(0), ALU.add, ALU.max))
                        b0, b1, bo = pen[:, 1, ::-1], val[:, ::-1], run[:, 1, ::-1]
                        stepv(dve, nc.vector.tensor_tensor_scan(bo, b0, b1, initial(1), ALU.add, ALU.max))
                    scans(lambda side: -BIG)
                    stepv(dve, nc.vector.tensor_copy(edge[:, 0, 1:2], run[:, 0, NT - 1:NT]))
                    nc.vector.tensor_copy(edge[:, 1, 1:2], run[:, 1, 0:1]).then_inc(s_e.sem, 1)
                    wait(dve, s_r, h + 1)
                    stepv(dve, nc.vector.tensor_copy(rowv[:, :, :, :], rps[:, :, :, :]))
                    stepv(dve, nc.vector.tensor_tensor_scan(crow[:, 0, 1:P + 1], rowv[:, 0, 0, :], rowv[:, 0, 1, :], -BIG, ALU.add, ALU.max))
                    stepv(dve, nc.vector.tensor_tensor_scan(crow[:, 1, P:0:-1], rowv[:, 1, 0, ::-1], rowv[:, 1, 1, ::-1], -BIG, ALU.add, ALU.max))
                    nc.vector.tensor_copy(rowv[:, 0, 0, 0:1], rowv[:, 0, 0, 0:1]).then_inc(s_cr.sem, 1)
                    wait(dve, s_cp, h + 1)
                    stepv(dve, nc.vector.tensor_copy(carry[:, :], cps[:, :]))
                    scans(lambda side: carry[:, side:side + 1])
                    stepv(dve, nc.vector.tensor_tensor(run[:, 0, :], run[:, 0, :], run[:, 1, :], ALU.max))
                    nc.vector.tensor_tensor(val[:, :], val[:, :], run[:, 0, :], ALU.subtract).then_inc(s_i.sem, 1)
                    if last is not None:
                        nc.vector.tensor_tensor(run[:, 1, :], run[:, 0, :], keys[:, 0, :], ALU.mult).then_inc(s_v.sem, 1)

                @block.scalar
                def _(act):
                    wait(act, s_i, 2 + h)
                    nc.scalar.activation(val[:, :], val[:, :], ACT.Exp).then_inc(s_x.sem, 1)

                @block.tensor
                def _(pe):
                    wait(pe, s_e, h + 1)
                    for side in range(2):
                        for q in range(2):
                            m = nc.tensor.transpose(rps[0:1, side, q, :], edge[:, side, q:q + 1], K.ident[:, :])
                    m.then_inc(s_r.sem, 1)
                    wait(pe, s_cr, h + 1)
                    for side, o in ((0, 0), (1, 2)):
                        m = nc.tensor.transpose(cps[:, side:side + 1], crow[0:1, side, o:o + P], K.ident[0:1, 0:1])
                    m.then_inc(s_cp.sem, 1)
            receive(sd, lambda c, w: X[:, c:c + w, h], turns, loads)
            turns += nch
            loads += nch
            if last is not None:
                receive(md, lambda c, w: last[:, c:c + w], turns, loads)
                turns += nch
                loads += nch
        finished(*[(s, (stores + 1 - u) // 2 * 16) for u, s in enumerate(s_a)],
                 *[(s, (loads + 1 - u) // 2 * 16) for u, s in enumerate(s_b)],
                 (s_t, turns), (s_c, turns), (s_st, steps[0]), *[(s, heads) for s in (s_e, s_r, s_cr, s_cp, s_x)],
                 (s_v, heads if last is not None else 0), (s_ld, 16 * (3 + heads)),
                 (s_w, 32 + 16 * heads * (2 if last is not None else 1)), (s_i, 1 + heads))



def gather_sum(nc, counts, D, K, name, k, table, acc):
    n = D.NT // BODY
    with ExitStack() as ctx:
        idx = ctx.enter_context(nc.sbuf_tensor(f"{name}_idx", [P, RING, G], I32))
        rows = ctx.enter_context(nc.sbuf_tensor(f"{name}_rows", [P, RING, G, C], F32))
        oh = ctx.enter_context(nc.sbuf_tensor(f"{name}_oh", [P, 2, G, P], F32))
        part = [ctx.enter_context(nc.psum_tensor(f"{name}_part{u}", [P, G, C], F32)) for u in range(2)]
        s_idx, s_oh, s_mm, s_acc = (counts.get(f"gather_{x}") for x in ("indices", "onehots", "products", "added"))
        s_ga = [counts.get(f"gather_gathered{u}") for u in range(RING)]
        with nc.Block() as block:
            @block.scalar
            def _(act):
                def body(i, last):
                    for u in range(RING):
                        g = i * RING + u
                        wait(act, s_mm, g - RING + 1)
                        nc.scalar.copy(idx[:, u, :], K.idx[k][:, bass.ds(g * G, G)]).then_inc(s_idx.sem, 1)
                loop(act, n, body)

            @block.gpsimd
            def _(pool):
                def body(i, last):
                    for u in range(RING):
                        g = i * RING + u
                        wait(pool, s_idx, g + 1)
                        pool.nop(nofuse=True)
                        for j in range(G):
                            nc.gpsimd.indirect_dma_start(out=rows[:, u, j, :], out_offset=None, in_=table,
                                                         in_offset=bass.IndirectOffsetOnAxis(ap=idx[:, u, j:j + 1], axis=0)).then_inc(s_ga[u].sem, 16)
                loop(pool, n, body)

            @block.tensor
            def _(pe):
                def body(i, last):
                    for u in range(RING):
                        g = i * RING + u
                        w = u % 2
                        wait(pe, s_ga[u], (i + 1) * 16 * G)
                        wait(pe, s_oh, g + 1)
                        wait(pe, s_acc, (g - 1) * G)
                        for j in range(G):
                            m = nc.tensor.matmul(part[w][:, j, :], oh[:, w, j, :], rows[:, u, j, :], start=True, stop=True)
                        m.then_inc(s_mm.sem, 1)
                loop(pe, n, body)
            add_parts(nc, D, K, block, k, n, oh, part, acc, C, s_oh, s_mm, s_acc)
        finished(*[(s, RING * n) for s in (s_idx, s_oh, s_mm)], (s_acc, D.NT), *[(s, 16 * G * n) for s in s_ga])



def add_parts(nc, D, K, block, k, n, oh, part, acc, width, s_oh, s_mm, s_acc, message=None):
    @block.vector
    def _(dve):
        def prep(i, u):
            g = i * RING + u
            w = u % 2
            wait(dve, s_mm, g - 1)
            if message is not None:
                message(dve, i, u)
            nc.vector.tensor_tensor(oh[:, w, :, :], bcast(K.iota[:, :], 1, [P, G, P]),
                                    bcast(K.kl[k][:, bass.ds(g * G, G)], 2, [P, G, P]), ALU.is_equal).then_inc(s_oh.sem, 1)
        prep(0, 0)

        def body(i, last):
            bs = nc.values_load_multi_w_load_instructions(K.blk[0:1, k, bass.ds(i * BODY, BODY)], engines=DVE_ONLY,
                                                          min_val=0, max_val=D.NB - 1)[1]
            for u in range(RING):
                g = i * RING + u
                w = u % 2
                if u < RING - 1:
                    prep(i, u + 1)
                elif not last:
                    prep(i + 1, 0)
                wait(dve, s_mm, g + 1)
                for j in range(G):
                    b = bs[u * G + j]
                    wait(dve, s_acc, g * G + j)
                    nc.vector.tensor_tensor(acc[:, bass.ds(b, 1), 0:width], acc[:, bass.ds(b, 1), 0:width],
                                            part[w][:, j:j + 1, 0:width], ALU.add).then_inc(s_acc.sem, 1)
        loop(dve, n, body)


def weighted_sum(nc, counts, D, K, name, k, V, X, heads, acc, last=None):
    n = D.NT // BODY
    width = C + heads + (1 if last is not None else 0)
    with ExitStack() as ctx:
        rows = ctx.enter_context(nc.sbuf_tensor(f"{name}_rows", [P, RING, G, C], F32))
        msg = ctx.enter_context(nc.sbuf_tensor(f"{name}_msg", [P, 2, G, REC], F32))
        oh = ctx.enter_context(nc.sbuf_tensor(f"{name}_oh", [P, 2, G, P], F32))
        part = [ctx.enter_context(nc.psum_tensor(f"{name}_part{u}", [P, G, P], F32)) for u in range(2)]
        s_oh, s_mm, s_acc, s_z = (counts.get(f"weigh_{x}") for x in ("messages", "products", "added", "zeroed"))
        s_ld = [counts.get(f"weigh_loaded{u}") for u in range(RING)]
        vv = V.rearrange("(g p j) c -> p g j c", j=G, p=P)
        with nc.Block() as block:
            @block.gpsimd
            def _(pool):
                nc.gpsimd.memset(acc[:, :, :], 0.0).then_inc(s_z.sem, 1)

            @block.sync
            def _(sp):
                def body(i, last_):
                    for u in range(RING):
                        g = i * RING + u
                        wait(sp, s_oh, g - RING + 1)
                        sp.dma_start(rows[:, u, :, :], vv[:, bass.ds(g, 1), :, :].rearrange("p o j c -> p (o j) c")).then_inc(s_ld[u].sem, 16)
                loop(sp, n, body)

            @block.tensor
            def _(pe):
                def body(i, last_):
                    for u in range(RING):
                        g = i * RING + u
                        w = u % 2
                        wait(pe, s_oh, g + 1)
                        wait(pe, s_acc, (g - 1) * G)
                        for j in range(G):
                            m = nc.tensor.matmul(part[w][:, j, 0:width], oh[:, w, j, :], msg[:, w, j, 0:width], start=True, stop=True)
                        m.then_inc(s_mm.sem, 1)
                loop(pe, n, body)

            def message(dve, i, u):
                g = i * RING + u
                w = u % 2
                if isinstance(i, int) and i == 0 and u == 0:
                    wait(dve, s_z, 1)
                wait(dve, s_ld[u], (i + 1) * 16)
                xs = X[:, bass.ds(g * G, G), :]
                nc.vector.tensor_tensor(msg[:, w, :, 0:C].rearrange("p j (h d) -> p j h d", h=heads),
                                        rows[:, u, :, :].rearrange("p j (h d) -> p j h d", h=heads),
                                        xs.unsqueeze(3).to_broadcast([P, G, heads, C // heads]), ALU.mult)
                nc.vector.tensor_copy(msg[:, w, :, C:C + heads], xs)
                if last is not None:
                    nc.vector.tensor_copy(msg[:, w, :, C + heads], last[:, bass.ds(g * G, G)])
            add_parts(nc, D, K, block, k, n, oh, part, acc, width, s_oh, s_mm, s_acc, message)
        finished(*[(s, RING * n) for s in (s_oh, s_mm)], (s_acc, D.NT), (s_z, 1), *[(s, 16 * n) for s in s_ld])


def read_list(nc, sem, D, K, Bl):
    chunks = D.chunks()
    with ExitStack() as ctx:
        raw = ctx.enter_context(nc.sbuf_tensor("rl_raw", [P, 2, P, 4], F32))
        tps = [ctx.enter_context(nc.psum_tensor(f"rl_t{u}", [P, 3, P], F32)) for u in range(2)]
        s_ld = [sem(f"rl_loaded{u}") for u in range(2)]
        s_t, s_c = sem("rl_turned"), sem("rl_copied")
        with nc.Block() as block:
            @block.sync
            def _(sp):
                for q, (c, w) in enumerate(chunks):
                    wait(sp, s_t, q - 1)
                    sp.dma_start(raw[0:w, q % 2, :, :].rearrange("t p c -> t (p c)"),
                                 Bl[c * P:(c + w) * P, :].rearrange("(t p) c -> t (p c)", p=P)).then_inc(s_ld[q % 2], 16)

            @block.tensor
            def _(pe):
                for q, (c, w) in enumerate(chunks):
                    pe.wait_ge(s_ld[q % 2], (q // 2 + 1) * 16)
                    wait(pe, s_c, q - 1)
                    for f in range(3):
                        m = nc.tensor.transpose(tps[q % 2][:, f, 0:w], raw[0:w, q % 2, :, f], K.ident[0:w, 0:w])
                    m.then_inc(s_t, 1)

            @block.vector
            def _(dve):
                for q, (c, w) in enumerate(chunks):
                    dve.wait_ge(s_t, q + 1)
                    nc.vector.tensor_tensor(K.kl[1][:, c:c + w], tps[q % 2][:, 0, 0:w], K.first[:, 1, c:c + w], ALU.subtract)
                    nc.vector.tensor_copy(K.idx[1][:, c:c + w], tps[q % 2][:, 1, 0:w])
                    nc.vector.tensor_copy(K.ec[1][:, c:c + w], tps[q % 2][:, 2, 0:w]).then_inc(s_c, 1)


def attention_logits(nc, counts, D, K, name, k, table, dnode, logit, V):
    n = D.NT // BODY
    with ExitStack() as ctx:
        def sb(nm, s, d=F32):
            return ctx.enter_context(nc.sbuf_tensor(f"{name}_{nm}", s, d))
        idx = sb("idx", [P, RING, G], I32)
        rows = sb("rows", [P, RING, G, REC])
        oh = sb("oh", [P, 2, G, P], BF16)
        ohT = sb("ohT", [P, 2, G, P])
        part = sb("sum", [P, 2, G])
        ot = [ctx.enter_context(nc.psum_tensor(f"{name}_ot{u}", [P, G, P], BF16)) for u in range(2)]
        loc = [ctx.enter_context(nc.psum_tensor(f"{name}_loc{u}", [P, G], F32)) for u in range(2)]
        s_idx, s_oh, s_ot, s_ohT, s_loc, s_sum, s_log = (counts.get(f"att_{x}") for x in (
            "indices", "onehots", "turned", "turned_copied", "node_terms", "sums", "logits"))
        s_ga = [counts.get(f"att_gathered{u}") for u in range(RING)]
        s_vs = [counts.get(f"att_stored{u}") for u in range(RING)]
        vv = V.rearrange("(g p j) c -> p g j c", j=G, p=P)
        with nc.Block() as block:
            @block.sync
            def _(sp):
                def body(i, last):
                    for u in range(RING):
                        g = i * RING + u
                        wait(sp, s_ga[u], (i + 1) * 16 * G)
                        sp.dma_start(vv[:, bass.ds(g, 1), :, :].rearrange("p o j c -> p (o j) c"), rows[:, u, :, 0:C]).then_inc(s_vs[u].sem, 16)
                loop(sp, n, body)
                for u in range(RING):
                    wait(sp, s_vs[u], n * 16)

            @block.gpsimd
            def _(pool):
                def body(i, last):
                    for u in range(RING):
                        g = i * RING + u
                        wait(pool, s_idx, g + 1)
                        pool.nop(nofuse=True)
                        for j in range(G):
                            nc.gpsimd.indirect_dma_start(out=rows[:, u, j, :], out_offset=None, in_=table,
                                                         in_offset=bass.IndirectOffsetOnAxis(ap=idx[:, u, j:j + 1], axis=0)).then_inc(s_ga[u].sem, 16)
                loop(pool, n, body)

            @block.scalar
            def _(act):
                def index(i, u):
                    g = i * RING + u
                    wait(act, s_log, g - RING + 1)
                    wait(act, s_vs[u], i * 16)
                    nc.scalar.copy(idx[:, u, :], K.idx[k][:, bass.ds(g * G, G)]).then_inc(s_idx.sem, 1)
                for u in range(RING - 1):
                    index(0, u)

                def body(i, last):
                    for u in range(RING):
                        g = i * RING + u
                        w = u % 2
                        wait(act, s_ot, g + 1)
                        wait(act, s_loc, g - 1)
                        nc.scalar.copy(ohT[:, w, :, :], ot[w][:, :, :]).then_inc(s_ohT.sem, 1)
                        if u == 0:
                            index(i, RING - 1)
                        elif not last:
                            index(i + 1, u - 1)
                loop(act, n, body)

            @block.tensor
            def _(pe):
                def body(i, last):
                    bs = nc.values_load_multi_w_load_instructions(K.blk[0:1, k, bass.ds(i * BODY, BODY)], engines=PE_ONLY,
                                                                  min_val=0, max_val=D.NB - 1)[1]
                    for u in range(RING):
                        g = i * RING + u
                        w = u % 2
                        wait(pe, s_oh, g + 1)
                        wait(pe, s_ohT, g - 1)
                        for j in range(G):
                            m = nc.tensor.transpose(ot[w][:, j, :], oh[:, w, j, :], K.identb[:, :])
                        m.then_inc(s_ot.sem, 1)
                        wait(pe, s_ohT, g + 1)
                        wait(pe, s_sum, g - 1)
                        for j in range(G):
                            m = nc.tensor.matmul(loc[w][:, j:j + 1], ohT[:, w, j, :], dnode[:, bass.ds(bs[u * G + j], 1)], start=True, stop=True)
                        m.then_inc(s_loc.sem, 1)
                loop(pe, n, body)

            @block.vector
            def _(dve):
                def prep(i, u):
                    g = i * RING + u
                    w = u % 2
                    wait(dve, s_ot, g - 1)
                    nc.vector.tensor_tensor(oh[:, w, :, :], bcast(K.iota[:, :], 1, [P, G, P]),
                                            bcast(K.kl[k][:, bass.ds(g * G, G)], 2, [P, G, P]), ALU.is_equal).then_inc(s_oh.sem, 1)
                prep(0, 0)

                def body(i, last):
                    for u in range(RING):
                        g = i * RING + u
                        w = u % 2
                        if u < RING - 1:
                            prep(i, u + 1)
                        elif not last:
                            prep(i + 1, 0)
                        wait(dve, s_loc, g + 1)
                        wait(dve, s_log, g - 1)
                        nc.vector.tensor_tensor(part[:, w, :], loc[w][:, :], K.ec[k][:, bass.ds(g * G, G)], ALU.add).then_inc(s_sum.sem, 1)
                        wait(dve, s_sum, g + 1)
                        wait(dve, s_ga[u], (i + 1) * 16 * G)
                        nc.vector.tensor_tensor(logit[:, bass.ds(g * G, G), :].rearrange("p j o -> p (j o)"), part[:, w, :],
                                                rows[:, u, :, C], ALU.add).then_inc(s_log.sem, 1)
                loop(dve, n, body)
        finished(*[(s, RING * n) for s in (s_idx, s_oh, s_ot, s_ohT, s_loc, s_sum, s_log)],
                 *[(s, 16 * G * n) for s in s_ga], *[(s, 16 * n) for s in s_vs])



def load_params(nc, sem, K, dram, sb):
    K.w_tab = sb("w_tab", [C + 1, 3 * C], F32)
    K.w_kv = sb("w_kv", [C + 1, 2 * C], F32)
    K.w_proj = sb("w_proj", [C + 1, C], F32)
    K.w_l1 = sb("w_l1", [C + 1, C], F32)
    K.w_l2 = sb("w_l2", [P, C], F32)
    K.w_l3 = sb("w_l3", [C, C + 2], F32)
    s_p, s_z, s_t, s_d = sem("node_params"), sem("node_params_zeroed"), sem("node_params_turned"), sem("node_params_steps")
    with ExitStack() as ctx:
        raw = ctx.enter_context(nc.sbuf_tensor("w_l1_raw", [C, C], F32))
        arow = ctx.enter_context(nc.sbuf_tensor("a_rows", [C, 2, C], F32))
        pr = ctx.enter_context(nc.sbuf_tensor("a_prod", [C, 2, C], F32))
        tps = ctx.enter_context(nc.psum_tensor("w_l1_t", [C, C], F32))
        with nc.Block() as block:
            @block.sync
            def _(sp):
                n = [0]

                def load(out, in_):
                    n[0] += 16
                    sp.dma_start(out, in_).then_inc(s_p, 16)
                sp.wait_ge(s_z, 1)
                for c, nm in ((0, "L0_gnn_W_src"), (1, "L0_gnn_W_dst"), (2, "L0_gnn_Wq")):
                    load(K.w_tab[0:C, c * C:(c + 1) * C], dram[nm])
                load(K.w_tab[C:C + 1, 0:C], dram["L0_gnn_b_src"].rearrange("(o c) -> o c", o=1))
                load(K.w_tab[C:C + 1, 2 * C:3 * C], dram["L0_gnn_bq"].rearrange("(o c) -> o c", o=1))
                load(K.w_kv[0:C, :], dram["L0_gnn_W_kv"])
                load(K.w_kv[C:C + 1, :], dram["L0_gnn_b_kv"].rearrange("(o c) -> o c", o=1))
                load(K.w_proj[0:C, :], dram["L0_gnn_W_proj"])
                load(K.w_proj[C:C + 1, :], dram["L0_gnn_b_proj"].rearrange("(o c) -> o c", o=1))
                load(raw[:, :], dram["L1_gnn_W"])
                load(K.w_l1[C:C + 1, :], dram["L1_gnn_b"].rearrange("(o c) -> o c", o=1))
                load(K.w_l2[0:C, :], dram["L2_gnn_weight1"])
                load(K.w_l2[C:2 * C, :], dram["L2_gnn_weight2"])
                load(K.w_l3[:, 0:C], dram["L3_gnn_W"])
                for s in range(2):
                    load(arow[:, s, :], dram["L3_gnn_a"][s * C:(s + 1) * C, :].rearrange("c o -> o c").to_broadcast([C, C]))
                assert n[0] == 16 * 16

            @block.tensor
            def _(pe):
                pe.wait_ge(s_p, 256)
                nc.tensor.transpose(tps[:, :], raw[:, :], K.ident[0:C, 0:C]).then_inc(s_t, 1)

            @block.vector
            def _(dve):
                step = stepper(dve, s_d)
                nc.vector.memset(K.w_tab[:, :], 0.0).then_inc(s_z, 1)
                dve.wait_ge(s_t, 1)
                step(nc.vector.tensor_copy(K.w_l1[0:C, :], tps[:, :]))
                step(nc.vector.tensor_single_scalar(K.w_tab[:, 2 * C:3 * C], K.w_tab[:, 2 * C:3 * C], 0.25, ALU.mult))
                for s in range(2):
                    step(nc.vector.tensor_tensor(pr[:, s, :], K.w_l3[:, 0:C], arow[:, s, :], ALU.mult))
                step(nc.vector.tensor_reduce(K.w_l3[:, C:C + 2], pr[:, :, :], AX.X, ALU.add))


def vector_block(nc, sem, name, ops):
    s = sem(name)
    with nc.Block() as block:
        @block.vector
        def _(dve):
            for n, (who, make) in enumerate(ops):
                if who == "v":
                    make(nc.vector).then_inc(s, 1)
                dve.wait_ge(s, n + 1)

        @block.scalar
        def _(act):
            for n, (who, make) in enumerate(ops):
                if who == "a":
                    wait(act, s, n)
                    make(nc.scalar).then_inc(s, 1)


def build(nc, dram, out, stop=None):
    D = Dims(dram["x"].shape[0], dram["src"].shape[0])
    K = Shared()
    NB, NT, NSLOT = D.NB, D.NT, D.NSLOT
    with ExitStack() as ctx:
        def sb(n, s, d):
            return ctx.enter_context(nc.sbuf_tensor(n, s, d))

        def sem(n):
            return ctx.enter_context(nc.semaphore(n))

        def node_dram(name, width):
            return nc.dram_tensor(name, (NB * P, width), F32).ap()
        counts = Counts(sem)
        K.first = sb("first_node", [P, 2, NT], F32)
        K.blk = sb("tile_block", [1, 2, NT], I32)
        K.deg = sb("degrees", [P, 2, NB], F32)
        constants(nc, sb, sem, K)
        A = nc.dram_tensor("edges_by_dst", (NSLOT, REC), F32).ap()
        Bl = nc.dram_tensor("edges_by_src", (NSLOT, 4), F32).ap()
        sort_edges(nc, sem, D, K, dram, A, Bl)

        K.x = sb("x_nodes", [P, NB, C], F32)
        K.kl = [sb(f"key_in_block{k}", [P, NT], F32) for k in range(2)]
        K.idx = [sb(f"other_end{k}", [P, NT], I32) for k in range(2)]
        K.ec = [sb(f"edge_term{k}", [P, NT], F32) for k in range(2)]
        load_params(nc, sem, K, dram, sb)
        load_nodes(nc, sem, D, K, dram)
        rows_dram = [nc.dram_tensor(f"rows_in_order{k}", (NSLOT, C), F32).ap() for k in range(2)]

        with ExitStack() as l1:
            al = l1.enter_context(nc.sbuf_tensor("scores", [P, NT, HEADS], F32))
            with ExitStack() as t:
                tabD = t.enter_context(nc.sbuf_tensor("dst_table", [P, NB, 2 * C], F32))
                tabS = node_dram("src_table", C)

                def feed(dve, g, o):
                    return nc.vector.tensor_copy(o, K.x[:, bass.ds(g * 4, 4), :])

                def evict(dve, g, prods, stage):
                    nc.vector.tensor_copy(tabD[:, bass.ds(g * 4, 4), :], prods[1])
                    return nc.vector.tensor_copy(stage, prods[0])
                node_stage(nc, counts, D, K, "tables", C, K.w_tab, (C, 2 * C), feed, evict, tabS)
                score_edges(nc, sem, D, K, A, tabS, tabD, K.w_kv, al, rows_dram[0])
            segment_softmax(nc, counts, D, K, "sm0", al, HEADS, 0)
            acc = l1.enter_context(nc.sbuf_tensor("acc0", [P, NB, REC], F32))
            weighted_sum(nc, counts, D, K, "ws0", 0, rows_dram[0], al, HEADS, acc)
            den = l1.enter_context(nc.sbuf_tensor("den0", [P, NB, HEADS], F32))
            vector_block(nc, sem, "den_steps", [
                ("v", lambda e: e.tensor_single_scalar(den[:, :, :], acc[:, :, C:C + HEADS], 1e-16, ALU.add)),
                ("v", lambda e: e.reciprocal(den[:, :, :], den[:, :, :]))])

            def feed(dve, g, o):
                return nc.vector.tensor_tensor(o.rearrange("p j (h d) -> p j h d", h=HEADS),
                                               acc[:, bass.ds(g * 4, 4), 0:C].rearrange("p j (h d) -> p j h d", h=HEADS),
                                               den[:, bass.ds(g * 4, 4), :].unsqueeze(3).to_broadcast([P, 4, HEADS, C // HEADS]), ALU.mult)

            def evict(dve, g, prods, stage):
                xs = K.x[:, bass.ds(g * 4, 4), :]
                return nc.vector.tensor_tensor(xs, xs, prods[0], ALU.add)
            node_stage(nc, counts, D, K, "proj", C, K.w_proj, (C,), feed, evict)
        layer_norm(nc, counts, D, K, "ln0", out if stop == "l0" else None)
        if stop == "l0":
            return

        read_list(nc, sem, D, K, Bl)
        scale = sb("node_scale", [P, 3, NB], F32)
        vector_block(nc, sem, "scale_steps", [
            ("v", lambda e: e.tensor_tensor(scale[:, 0, :], K.deg[:, 0, :], K.deg[:, 1, :], ALU.add)),
            ("v", lambda e: e.tensor_single_scalar(scale[:, 0, :], scale[:, 0, :], 1.0, ALU.add)),
            ("v", lambda e: e.tensor_single_scalar(scale[:, 1, :], K.deg[:, 1, :], 1.0, ALU.max)),
            ("v", lambda e: e.tensor_single_scalar(scale[:, 2, :], K.deg[:, 0, :], 1.0, ALU.max)),
            ("a", lambda e: e.activation(scale[:, :, :], scale[:, :, :], ACT.Sqrt)),
            ("v", lambda e: e.reciprocal(scale[:, :, :], scale[:, :, :]))])
        with ExitStack() as l2:
            acc = l2.enter_context(nc.sbuf_tensor("acc1", [P, NB, C], F32))
            tab = node_dram("layer2_table", C)

            def feed(dve, g, o):
                return nc.vector.tensor_copy(o, K.x[:, bass.ds(g * 4, 4), :])

            def evict(dve, g, prods, stage):
                ds = bass.ds(g * 4, 4)
                nc.vector.tensor_tensor(acc[:, ds, :], prods[0], scale[:, 0, ds].unsqueeze(2).to_broadcast([P, 4, C]), ALU.mult)
                return nc.vector.tensor_tensor(stage, prods[0], scale[:, 0, ds].unsqueeze(2).to_broadcast([P, 4, C]), ALU.mult)
            node_stage(nc, counts, D, K, "lin1", C, K.w_l1, (C,), feed, evict, tab)
            gather_sum(nc, counts, D, K, "gs1f", 0, tab, acc)
            gather_sum(nc, counts, D, K, "gs1b", 1, tab, acc)
            vector_block(nc, sem, "layer2_steps", [
                ("v", lambda e: e.tensor_tensor(acc[:, :, :], acc[:, :, :], bcast(scale[:, 0, :], 2, [P, NB, C]), ALU.mult)),
                ("v", lambda e: e.tensor_tensor(K.x[:, :, :], K.x[:, :, :], acc[:, :, :], ALU.add))])
        layer_norm(nc, counts, D, K, "ln1", out if stop == "l1" else None)
        if stop == "l1":
            return

        with ExitStack() as l3:
            acc = l3.enter_context(nc.sbuf_tensor("acc2", [P, NB, C], F32))
            fn = l3.enter_context(nc.sbuf_tensor("scaled_x", [P, NB, C], F32))
            tmp = l3.enter_context(nc.sbuf_tensor("layer3_tmp", [P, 2, 4, C], F32))
            tab = node_dram("layer3_table", C)
            s_f, s_t = sem("layer3_scaled"), sem("layer3_table_stored")
            with nc.Block() as block:
                @block.vector
                def _(dve):
                    nc.vector.tensor_tensor(fn[:, :, :], K.x[:, :, :], bcast(scale[:, 1, :], 2, [P, NB, C]), ALU.mult).then_inc(s_f, 1)

                @block.gpsimd
                def _(pool):
                    nc.gpsimd.memset(acc[:, :, :], 0.0)

                @block.sync
                def _(sp):
                    sp.wait_ge(s_f, 1)
                    sp.dma_start(tab.rearrange("(b p) c -> p b c", p=P), fn[:, :, :]).then_inc(s_t, 16)
                    sp.wait_ge(s_t, 16)
            gather_sum(nc, counts, D, K, "gs2", 0, tab, acc)

            def feed(dve, g, o):
                ds = bass.ds(g * 4, 4)
                nc.vector.tensor_copy(o[:, :, 0:C], acc[:, ds, :])
                return nc.vector.tensor_tensor(o[:, :, C:2 * C], acc[:, ds, :], fn[:, ds, :], ALU.mult)
            turn = [0]
            s_step = sem("layer3_scaled_sums")

            def evict(dve, g, prods, stage):
                ds = bass.ds(g * 4, 4)
                u = turn[0] % 2
                turn[0] += 1
                t = tmp[:, u, :, :]
                nc.vector.tensor_tensor(t, prods[0], scale[:, 2, ds].unsqueeze(2).to_broadcast([P, 4, C]), ALU.mult).then_inc(s_step, 1)
                dve.wait_ge(s_step, g + 1)
                return nc.vector.tensor_tensor(K.x[:, ds, :], K.x[:, ds, :], t, ALU.add)
            node_stage(nc, counts, D, K, "lin2", 2 * C, K.w_l2, (C,), feed, evict, bias=False)
        layer_norm(nc, counts, D, K, "ln2", out if stop == "l2" else None)
        if stop == "l2":
            return

        tab = node_dram("layer4_table", REC)
        sd = sb("s_and_d", [P, 2, NB], F32)

        def feed(dve, g, o):
            return nc.vector.tensor_copy(o, K.x[:, bass.ds(g * 4, 4), :])

        def evict(dve, g, prods, stage):
            ds = bass.ds(g * 4, 4)
            nc.vector.tensor_copy(sd[:, :, ds].rearrange("p s b -> p b s"), prods[0][:, :, C:C + 2])
            return nc.vector.tensor_copy(stage[:, :, 0:C + 2], prods[0])
        node_stage(nc, counts, D, K, "lin3", C, K.w_l3, (C + 2,), feed, evict, tab, bias=False)
        z = [sb(f"logits{k}", [P, NT, 1], F32) for k in range(2)]
        for k in range(2):
            attention_logits(nc, counts, D, K, f"al{k}", k, tab, sd[:, 1, :], z[k], rows_dram[k])
        for k in range(2):
            segment_softmax(nc, counts, D, K, f"sm3{k}", z[k], 1, k, slope=0.2, last=K.ec[k])
        acc = [sb(f"acc3{k}", [P, NB, C + 2], F32) for k in range(2)]
        for k in range(2):
            weighted_sum(nc, counts, D, K, f"ws3{k}", k, rows_dram[k], z[k], 1, acc[k], last=K.ec[k])
        merge_attention(nc, sem, D, K, tab, sd, acc)
        layer_norm(nc, counts, D, K, "ln3", out)


def merge_attention(nc, sem, D, K, tab, sd, acc):
    NB = D.NB
    with ExitStack() as ctx:
        xt = ctx.enter_context(nc.sbuf_tensor("mg_xt", [P, NB, C], F32))
        m = ctx.enter_context(nc.sbuf_tensor("mg_m", [P, 4, NB], F32))
        has = ctx.enter_context(nc.sbuf_tensor("mg_has", [P, 2, NB], F32))
        w = ctx.enter_context(nc.sbuf_tensor("mg_w", [P, 3, NB], F32))
        den = ctx.enter_context(nc.sbuf_tensor("mg_den", [P, 3, NB], F32))
        s_ld = sem("mg_loaded")
        with nc.Block() as block:
            @block.sync
            def _(sp):
                sp.dma_start(xt[:, :, :], tab.rearrange("(b p) c -> p b c", p=P)[:, :, 0:C]).then_inc(s_ld, 16)
                sp.wait_ge(s_ld, 16)
        ops = []

        def v(f):
            ops.append(("v", f))
        v(lambda e: e.tensor_single_scalar(has[:, :, :], K.deg[:, :, :], 1.0, ALU.min))
        v(lambda e: e.tensor_scalar(has[:, :, :], has[:, :, :], BIG, -BIG, ALU.mult, ALU.add))
        for k in range(2):
            v(lambda e, k=k: e.tensor_tensor(m[:, k, :], acc[k][:, :, C + 1], has[:, k, :], ALU.add))
        v(lambda e: e.tensor_tensor(m[:, 3, :], sd[:, 0, :], sd[:, 1, :], ALU.add))
        v(lambda e: e.scalar_tensor_tensor(m[:, 2, :], m[:, 3, :], 0.2, m[:, 3, :], ALU.mult, ALU.max))
        v(lambda e: e.tensor_tensor(m[:, 3, :], m[:, 0, :], m[:, 1, :], ALU.max))
        v(lambda e: e.tensor_tensor(m[:, 3, :], m[:, 3, :], m[:, 2, :], ALU.max))
        for k in range(3):
            v(lambda e, k=k: e.tensor_tensor(w[:, k, :], m[:, k, :], m[:, 3, :], ALU.subtract))
        ops.append(("a", lambda e: e.activation(w[:, :, :], w[:, :, :], ACT.Exp)))
        for k in range(2):
            v(lambda e, k=k: e.tensor_tensor(den[:, k, :], acc[k][:, :, C], w[:, k, :], ALU.mult))
        v(lambda e: e.tensor_tensor(den[:, 0, :], den[:, 0, :], den[:, 1, :], ALU.add))
        v(lambda e: e.tensor_tensor(den[:, 0, :], den[:, 0, :], w[:, 2, :], ALU.add))
        v(lambda e: e.reciprocal(den[:, 2, :], den[:, 0, :]))
        for k in range(3):
            v(lambda e, k=k: e.tensor_tensor(w[:, k, :], w[:, k, :], den[:, 2, :], ALU.mult))
        for k in range(2):
            v(lambda e, k=k: e.tensor_tensor(acc[k][:, :, 0:C], acc[k][:, :, 0:C], bcast(w[:, k, :], 2, [P, NB, C]), ALU.mult))
        v(lambda e: e.tensor_tensor(xt[:, :, :], xt[:, :, :], bcast(w[:, 2, :], 2, [P, NB, C]), ALU.mult))
        for k in range(2):
            v(lambda e, k=k: e.tensor_tensor(K.x[:, :, :], K.x[:, :, :], acc[k][:, :, 0:C], ALU.add))
        v(lambda e: e.tensor_tensor(K.x[:, :, :], K.x[:, :, :], xt[:, :, :], ALU.add))
        vector_block(nc, sem, "mg_steps", ops)


def kernel(**inputs):
    import numpy as _np
    import concourse.bacc as _bacc
    from concourse import mybir as _mybir
    from concourse.bass_utils import run_bass_kernel_spmd as _run
    nc = _bacc.Bacc("TRN2", target_bir_lowering=False, num_devices=1)
    arrays, dram = {}, {}
    for name, value in inputs.items():
        a = _np.ascontiguousarray(value)
        arrays[f"in_{name}_dram"] = a
        dram[name] = nc.dram_tensor(f"in_{name}_dram", a.shape, _mybir.dt.from_np(a.dtype), kind="ExternalInput").ap()
    out = nc.dram_tensor("out_x", inputs["x"].shape, F32, kind="ExternalOutput").ap()
    build(nc, dram, out)
    r = _run(nc, [arrays], core_ids=[0])
    return r.results[0]["out_x"]
```

```python
import concourse.bass as bass
from concourse import mybir
from contextlib import ExitStack

I32 = mybir.dt.int32
F32 = mybir.dt.float32
BF16 = mybir.dt.bfloat16
ALU = mybir.AluOpType
ACT = mybir.ActivationFunctionType
AX = mybir.AxisListType
DVE_ONLY = (mybir.EngineType.DVE,)
POOL_ONLY = (mybir.EngineType.Pool,)
PE_ONLY = (mybir.EngineType.PE,)

P = 128
C = 64
HEADS = 4
REC = 68
SRC, DST, EC = 64, 65, 66
BIG = 1.0e30
LN_EPS = 1e-5
G = 4
RING = 4
BODY = G * RING
SG = 8


class Dims:
    def __init__(self, nodes, edges):
        self.N, self.E = nodes, edges
        self.NB = -(-nodes // (P * 8)) * 8
        assert nodes < self.NB * P <= P * P
        self.T1 = -(-edges // (P * 2 * SG)) * 2 * SG
        self.last_cols = edges - (P - 1) * self.T1
        assert self.last_cols > 0 and self.last_cols % (2 * SG) == 0
        self.NT = -(-((edges + -(-nodes // P) * (P - 1)) // P) // BODY) * BODY
        self.NSLOT = self.NT * P
        self.PHANTOM = self.NB * P - 1

    def chunks(self):
        return [(c, min(P, self.NT - c)) for c in range(0, self.NT, P)]


def bcast(ap, axis, shape):
    return ap.unsqueeze(axis).to_broadcast(shape)


def constants(nc, sb, sem, K):
    K.ident = sb("ident", [P, P], F32)
    K.identb = sb("identb", [P, P], BF16)
    K.iota = sb("iota", [P, P], F32)
    K.iotab = sb("iotab", [P, P], BF16)
    K.ident128b = sb("ident128b", [P, P], BF16)
    K.ones = sb("ones", [P, P], F32)
    K.zero = sb("zero", [P, P], BF16)
    s_zero, s_made = sem("const_zeroed"), sem("const_made")
    with nc.Block() as block:
        @block.gpsimd
        def _(pool):
            nc.gpsimd.memset(K.ident[:, :], 0.0).then_inc(s_zero, 1)
            nc.gpsimd.memset(K.identb[:, :], 0.0).then_inc(s_zero, 1)
            nc.gpsimd.memset(K.ident128b[:, :], 0.0).then_inc(s_zero, 1)
            nc.gpsimd.memset(K.ones[:, :], 1.0).then_inc(s_made, 1)
            nc.gpsimd.memset(K.zero[:, :], 0.0).then_inc(s_made, 1)
            nc.gpsimd.iota(K.iota[:, :], pattern=[[1, P]], base=0, channel_multiplier=0,
                           allow_small_or_imprecise_dtypes=True).then_inc(s_made, 1)
            nc.gpsimd.iota(K.iotab[:, :], pattern=[[1, P]], base=0, channel_multiplier=0,
                           allow_small_or_imprecise_dtypes=True).then_inc(s_made, 1)
            pool.wait_ge(s_zero, 3)
            for m, v in ((K.ident, 1.0), (K.identb, 1.0), (K.ident128b, 128.0)):
                nc.gpsimd.affine_select(out=m[:, :], in_=m[:, :], compare_op=ALU.not_equal, fill=v, base=0,
                                        pattern=[[-1, P]], channel_multiplier=1).then_inc(s_made, 1)
            pool.wait_ge(s_made, 7)


def sort_edges(nc, sem, D, K, dram, A, Bl):
    T1, NB, NT, E = D.T1, D.NB, D.NT, D.E
    NG = T1 // SG
    with ExitStack() as ctx:
        def sb(n, s, d):
            return ctx.enter_context(nc.sbuf_tensor(n, s, d))

        def ps(n, s, d=F32):
            return ctx.enter_context(nc.psum_tensor(n, s, d))

        keyi = sb("keyi", [P, 2, T1], I32)
        parti = sb("parti", [P, T1], I32)
        keyf = sb("keyf", [P, 2, T1 + SG], F32)
        hilo = sb("hilo", [P, NG + 1, 2, 2, SG], BF16)
        w1 = sb("w1", [P, T1], F32)
        onehot = sb("onehot", [P, 2, 2, 2, SG, P], BF16)
        tri = sb("tri", [P, P], F32)
        triU = sb("triU", [P, P], F32)
        notph = sb("notph", [P, P], F32)
        tcol = sb("tcol", [P, NT], F32)
        ge = sb("ge", [P, NT], F32)
        hist = sb("hist", [P, 2, P], F32)
        base = sb("base", [P, 2, P], F32)
        tmp = sb("tmp_sort", [P, P], F32)
        rows = sb("rows", [P, 2], F32)
        rowi = sb("rowi", [P, 2], I32)
        ts = sb("ts", [P, 2], F32)
        patA = sb("patA", [P, 16, REC], F32)
        patB = sb("patB", [P, 16, 4], F32)
        keycol = sb("keycol", [P, 2, 2, SG], F32)
        hlcol = sb("hlcol", [P, 2, 2, 2, SG], BF16)
        ohT = sb("ohT", [P, 2, 2, SG, P], F32)
        Csb = sb("Csb", [P, 2, P], F32)
        junk = sb("junk", [P, 4, 2, 2, P], F32)
        cnt = sb("cnt", [P, 2, 2, SG], F32)
        sel = sb("sel", [P, 2, 2, SG], F32)
        pos = sb("pos", [P, 2, 2, SG], I32)
        rec = sb("rec", [P, 2, SG, REC], F32)
        ea = sb("ea", [P, 2, SG, C], F32)
        ea16 = sb("ea16", [P, 2, SG, 16], F32)
        prod16 = sb("prod16", [P, SG, 16], F32)
        a16 = sb("a16", [P, 16], F32)
        w1d = sb("w1d", [P, P], F32)
        w2d = sb("w2d", [P, P], F32)
        w3d = sb("w3d", [P, P], F32)
        bb = sb("bb", [P, 2], F32)
        warm = sb("warm", [P, 1], F32)
        b3 = sb("b3", [1, SG * C], F32)
        eaT = sb("eaT", [P, 4 * P], F32)
        h1 = sb("h1", [P, 4 * P], F32)
        h2 = sb("h2", [P, 4 * P], F32)

        s_key, s_par, s_wz = sem("keys_loaded"), sem("params_loaded"), sem("weights_zeroed")
        s_fill = sem("lists_prefilled")
        s_pat, s_tri = sem("patterns_made"), sem("tri_made")
        s_ph = sem("phantom_keys_set")
        s_chain = sem("key_and_base_steps")

        with nc.Block() as block:
            @block.sync
            def _(sp):
                sp.wait_ge(s_ph, 1)
                for k, name in ((0, "dst"), (1, "src")):
                    n = (P - 1) * T1
                    sp.dma_start(keyi[0:P - 1, k, :], dram[name][0:n].rearrange("(p t) -> p t", t=T1)).then_inc(s_key, 16)
                    sp.dma_start(keyi[P - 1:P, k, 0:D.last_cols], dram[name][n:E].rearrange("(p t) -> p t", p=1)).then_inc(s_key, 16)
                n = (P - 1) * T1
                ew = dram["edge_weight1"].rearrange("e one -> (e one)")
                sp.dma_start(w1[0:P - 1, :], ew[0:n].rearrange("(p t) -> p t", t=T1)).then_inc(s_par, 16)
                sp.dma_start(w1[P - 1:P, 0:D.last_cols], ew[n:E].rearrange("(p t) -> p t", p=1)).then_inc(s_par, 16)
                sp.wait_ge(s_wz, 1)
                for w, name in ((w1d, "L0_gnn_W_fc1"), (w2d, "L0_gnn_W_fc2"), (w3d, "L0_gnn_W_fc3")):
                    for h in range(2):
                        sp.dma_start(w[h * C:(h + 1) * C, h * C:(h + 1) * C], dram[name]).then_inc(s_par, 16)
                for c, name in ((0, "L0_gnn_b_fc1"), (1, "L0_gnn_b_fc2")):
                    for h in range(2):
                        sp.dma_start(bb[h * C:(h + 1) * C, c:c + 1], dram[name].rearrange("(c o) -> c o", o=1)).then_inc(s_par, 16)
                for j in range(SG):
                    sp.dma_start(b3[0:1, j * C:(j + 1) * C], dram["L0_gnn_b_fc3"].rearrange("(o c) -> o c", o=1)).then_inc(s_par, 16)
                sp.dma_start(a16[:, :], dram["L3_gnn_a"][2 * C:2 * C + 16, :].rearrange("c o -> o c").to_broadcast([P, 16])).then_inc(s_par, 16)
                sp.wait_ge(s_pat, 4)
                sp.dma_start(A.rearrange("(p n t) c -> p n (t c)", p=P, t=16),
                             bcast(patA[:, :, :].rearrange("p t c -> p (t c)"), 1, [P, NT // 16, 16 * REC])).then_inc(s_fill, 16)
                sp.dma_start(Bl.rearrange("(p n t) c -> p n (t c)", p=P, t=16),
                             bcast(patB[:, :, :].rearrange("p t c -> p (t c)"), 1, [P, NT // 16, 64])).then_inc(s_fill, 16)
                sp.wait_ge(s_par, 16 * 21)
                sp.wait_ge(s_fill, 32)

            @block.gpsimd
            def _(pool):
                nc.gpsimd.memset(patA[:, :, :], 0.0).then_inc(s_pat, 1)
                nc.gpsimd.memset(patB[:, :, :], 0.0).then_inc(s_pat, 1)
                pool.wait_ge(s_pat, 2)
                nc.gpsimd.memset(patA[:, :, DST:DST + 1], -1.0).then_inc(s_pat, 1)
                nc.gpsimd.memset(patB[:, :, 0:1], -1.0).then_inc(s_pat, 1)
                nc.gpsimd.memset(rec[:, :, :, :], 0.0).then_inc(s_tri, 1)
                nc.gpsimd.iota(tcol[:, :], pattern=[[1, NT]], base=0, channel_multiplier=0,
                               allow_small_or_imprecise_dtypes=True).then_inc(s_tri, 1)
                nc.gpsimd.affine_select(out=tri[:, :], in_=K.ones[:, :], compare_op=ALU.is_gt, fill=0.0, base=0,
                                        pattern=[[-1, P]], channel_multiplier=1).then_inc(s_tri, 1)
                nc.gpsimd.affine_select(out=triU[:, :], in_=K.ones[:, :], compare_op=ALU.is_gt, fill=0.0, base=0,
                                        pattern=[[1, P]], channel_multiplier=-1).then_inc(s_tri, 1)
                nc.gpsimd.affine_select(out=notph[:, :], in_=K.ones[:, :], compare_op=ALU.not_equal, fill=0.0,
                                        base=-D.PHANTOM, pattern=[[1, P]], channel_multiplier=P).then_inc(s_tri, 1)
                pool.wait_ge(s_tri, 5)

            @block.vector
            def _(dve):
                n = [0]

                def step(ins):
                    n[0] += 1
                    ins.then_inc(s_chain, 1)
                    dve.wait_ge(s_chain, n[0])
                nc.vector.memset(K.blk[:, :, :], 0)
                nc.vector.memset(w1[:, :], 0.0)
                nc.vector.memset(keyf[:, :, T1:T1 + SG], 0.0)
                nc.vector.memset(hilo[:, NG, :, :, :], 0.0)
                nc.vector.memset(keyi[:, :, :], D.PHANTOM).then_inc(s_ph, 1)
                nc.vector.memset(w1d[:, :], 0.0)
                nc.vector.memset(w2d[:, :], 0.0)
                nc.vector.memset(w3d[:, :], 0.0).then_inc(s_wz, 1)
                dve.wait_ge(s_key, 64)
                for k in range(2):
                    nc.vector.tensor_copy(keyf[:, k, 0:T1], keyi[:, k, :])
                    step(nc.vector.tensor_single_scalar(parti[:, :], keyi[:, k, :], 7, ALU.arith_shift_right))
                    step(nc.vector.tensor_copy(hilo[:, 0:NG, k, 0, :], parti[:, :].rearrange("p (g t) -> p g t", t=SG)))
                    step(nc.vector.tensor_single_scalar(parti[:, :], keyi[:, k, :], 127, ALU.bitwise_and))
                    step(nc.vector.tensor_copy(hilo[:, 0:NG, k, 1, :], parti[:, :].rearrange("p (g t) -> p g t", t=SG)))

        s_oh, s_h = sem("hist_onehot"), sem("hist_added")
        with ExitStack() as pctx:
            hps = [pctx.enter_context(nc.psum_tensor(f"hps{k}", [P, P], F32)) for k in range(2)]
            tps = pctx.enter_context(nc.psum_tensor("tps", [P, 2], F32))
            bps = pctx.enter_context(nc.psum_tensor("bps", [P, 512], F32))
            dps = pctx.enter_context(nc.psum_tensor("dps", [P, 2, P], F32))
            with nc.Block() as block:
                @block.vector
                def _(dve):
                    dve.sem_inc(s_h, 2)
                    with dve.Fori(0, NG // 2) as i:
                        for u in range(2):
                            g = i * 2 + u
                            dve.wait_ge(s_h, g + 1)
                            nc.vector.tensor_tensor(
                                onehot[:, u, :, 0, :, 0:NB], bcast(bcast(K.iotab[:, 0:NB], 1, [P, SG, NB]), 1, [P, 2, SG, NB]),
                                bcast(hilo[:, bass.ds(g, 1), :, 0, :].rearrange("p o k t -> p (o k) t"), 3, [P, 2, SG, NB]), ALU.is_equal)
                            nc.vector.tensor_tensor(
                                onehot[:, u, :, 1, :, :], bcast(bcast(K.iotab[:, :], 1, [P, SG, P]), 1, [P, 2, SG, P]),
                                bcast(hilo[:, bass.ds(g, 1), :, 1, :].rearrange("p o k t -> p (o k) t"), 3, [P, 2, SG, P]), ALU.is_equal).then_inc(s_oh, 1)

                @block.tensor
                def _(pe):
                    zero = K.zero
                    for k in range(2):
                        nc.tensor.matmul(hps[k][:, :], zero[:, :], zero[:, :], start=True, stop=False)
                    with pe.Fori(0, NG // 2) as i:
                        for u in range(2):
                            g = i * 2 + u
                            pe.wait_ge(s_oh, g + 1)
                            for j in range(SG):
                                for k in range(2):
                                    m = nc.tensor.matmul(hps[k][0:NB, :], onehot[:, u, k, 0, j, 0:NB], onehot[:, u, k, 1, j, :],
                                                         start=False, stop=False)
                            m.then_inc(s_h, 1)
                    for k in range(2):
                        m = nc.tensor.matmul(hps[k][:, :], zero[:, :], zero[:, :], start=False, stop=True)
                    m.then_inc(s_h, 1)

            s_tp, s_bp, s_d, s_dp = (sem("tile_starts_summed"), sem("tile_blocks_summed"),
                                          sem("hist_ready"), sem("degrees_turned"))
            s_ge, s_bc = sem("tile_compare"), sem("tile_blocks_copied")
            nchunk = -(-NT // 512)
            with nc.Block() as block:
                @block.vector
                def _(dve):
                    n = [8]

                    def step(ins):
                        n[0] += 1
                        ins.then_inc(s_chain, 1)
                        dve.wait_ge(s_chain, n[0])
                    for k in range(2):
                        step(nc.vector.tensor_tensor(hist[:, k, :], hps[k][:, :], notph[:, :], ALU.mult))
                    step(nc.vector.tensor_reduce(rows[:, :], hist[:, :, :], AX.X, ALU.add))
                    step(nc.vector.tensor_single_scalar(rowi[:, :], rows[:, :], float(P - 1), ALU.add))
                    step(nc.vector.tensor_single_scalar(rowi[:, :], rowi[:, :], 7, ALU.arith_shift_right))
                    nc.vector.tensor_copy(rows[:, :], rowi[:, :]).then_inc(s_d, 1)
                    dve.wait_ge(s_tp, 1)
                    step(nc.vector.tensor_copy(ts[:, :], tps[:, :]))
                    for k in range(2):
                        step(nc.vector.tensor_tensor_scan(base[:, k, :], K.ones[:, :], hist[:, k, :], 0.0, ALU.mult, ALU.add))
                        step(nc.vector.tensor_tensor(base[:, k, :], base[:, k, :], hist[:, k, :], ALU.subtract))
                        step(nc.vector.tensor_single_scalar(tmp[:, 0:1], ts[:, k:k + 1], float(P), ALU.mult))
                        step(nc.vector.tensor_scalar(base[:, k, :], base[:, k, :], tmp[:, 0:1], None, ALU.add))
                        step(nc.vector.tensor_scalar(tmp[:, :], notph[:, :], -1.0e6, 1.0e6, ALU.mult, ALU.add))
                        step(nc.vector.tensor_tensor(base[:, k, :], base[:, k, :], tmp[:, :], ALU.add))
                    for k in range(2):
                        if k:
                            dve.wait_ge(s_bp, nchunk)
                        nc.vector.tensor_scalar(ge[:, :], tcol[:, :], ts[:, k:k + 1], None, ALU.is_ge).then_inc(s_ge, 1)
                        for c in range(nchunk):
                            w = min(512, NT - c * 512)
                            dve.wait_ge(s_bp, k * nchunk + c + 1)
                            step(nc.vector.tensor_scalar(K.first[:, k, c * 512:c * 512 + w], bps[:, 0:w], -1.0, float(NB - 1), ALU.add, ALU.min))
                            nc.vector.tensor_copy(K.blk[0:1, k, c * 512:c * 512 + w], K.first[0:1, k, c * 512:c * 512 + w]).then_inc(s_bc, 1)
                        dve.wait_ge(s_bc, (k + 1) * nchunk)
                        step(nc.vector.tensor_single_scalar(K.first[:, k, :], K.first[:, k, :], float(P), ALU.mult))
                    dve.wait_ge(s_dp, 1)
                    step(nc.vector.tensor_copy(K.deg[:, :, :], dps[:, :, 0:NB]))

                @block.tensor
                def _(pe):
                    pe.wait_ge(s_d, 1)
                    nc.tensor.matmul(tps[:, :], triU[:, :], rows[:, :], start=True, stop=True).then_inc(s_tp, 1)
                    for k in range(2):
                        m = nc.tensor.transpose(dps[:, k, :], hist[:, k, :], K.ident[:, :])
                    m.then_inc(s_dp, 1)
                    for k in range(2):
                        pe.wait_ge(s_ge, k + 1)
                        for c in range(nchunk):
                            w = min(512, NT - c * 512)
                            if k or c:
                                pe.wait_ge(s_bc, k * nchunk + c)
                            nc.tensor.matmul(bps[:, 0:w], K.ones[:, :], ge[:, c * 512:c * 512 + w], start=True, stop=True).then_inc(s_bp, 1)

        look = [ps(f"look{i}", [P, 2, 2, P]) for i in range(4)]
        cps = [ps(f"cps{k}", [P, P]) for k in range(2)]
        otp = ps("otp", [P, SG, P], BF16)
        xps = ps("xps", [P, 512])

        s_ea = [sem(f"edge_attr_loaded{u}") for u in range(2)]
        s_one, s_kc = sem("sort_onehot"), sem("key_columns")
        s_ot, s_oc = sem("onehot_turned"), sem("onehot_copied")
        s_c0 = sem("counters_based")
        s_get, s_upd, s_cs = sem("counters_read"), [sem(f"counters_added{k}") for k in range(2)], [sem(f"counters_copied{k}") for k in range(2)]
        s_pick = sem("slots_picked")
        s_pos = sem("slots_ready")
        s_free = sem("record_slots_free")
        s_xt, s_xc, s_m1, s_h1, s_m2, s_h2, s_m3 = (sem("attr_turned"), sem("attr_copied"), sem("fc1_done"), sem("silu1_done"),
                                                    sem("fc2_done"), sem("silu2_done"), sem("fc3_done"))
        s_p16, s_rec = sem("edge_term_products"), sem("records_ready")
        s_sc = [sem(f"scattered{u}") for u in range(2)]
        with nc.Block() as block:
            @block.sync
            def _(sp):
                def loads(i, rows_hi, after=None):
                    for u in range(2):
                        if after is not None:
                            sp.wait_ge(s_xt, after * 2 + u + 1)
                            sp.wait_ge(s_p16, after * 2 + u + 1)
                        for lo, hi in ((0, 112), (112, rows_hi)):
                            for buf, view in ((ea, ea_v), (ea16, ea16_v)):
                                sp.dma_start(buf[lo:hi, u, :, :], view(lo, hi, i * 2 + u)).then_inc(s_ea[u], 16)
                        if after is not None:
                            sp.wait_ge(s_sc[u], (after + 1) * 2 * SG * 16)
                            sp.sem_inc(s_free, 1)

                def view_of(name, width):
                    full = dram[name][0:(P - 1) * T1, :].rearrange("(p t) c -> p t c", t=T1)
                    tail = dram[name][112 * T1:112 * T1 + (P - 113) * T1, :].rearrange("(p t) c -> p t c", t=T1)

                    def view(lo, hi, g):
                        if hi <= P - 1:
                            return full[lo:hi, bass.ds(g * SG, SG), :]
                        return bass.AP(tensor=tail.tensor, offset=tail.offset + g * (SG * width),
                                       ap=[[T1 * width, hi - lo], [width, SG], [1, width]])
                    return view
                ea_v, ea16_v = view_of("edge_attr_64", C), view_of("edge_attr_16", 16)
                full_bodies = D.last_cols // (2 * SG)
                loads(0, P)
                if full_bodies > 1:
                    with sp.Fori(0, full_bodies - 1) as i:
                        loads(i + 1, P, i)
                if full_bodies < NG // 2:
                    with sp.Fori(full_bodies - 1, NG // 2 - 1) as i:
                        loads(i + 1, P - 1, i)

            def onehots(g, u, part):
                h, k, half = part // 4, part // 2 % 2, part % 2 * (SG // 2)
                nc.vector.tensor_tensor(
                    onehot[:, u, k, h, half:half + SG // 2, :], bcast(K.iotab[:, :], 1, [P, SG // 2, P]),
                    bcast(hilo[:, bass.ds(g, 1), k, h, half:half + SG // 2].rearrange("p o t -> p (o t)"), 2, [P, SG // 2, P]),
                    ALU.is_equal).then_inc(s_one, 1)

            @block.vector
            def _(dve):
                dve.sem_inc(s_rec, 2)
                dve.sem_inc(s_free, 2)
                for part in range(SG):
                    onehots(0, 0, part)
                with dve.Fori(0, NG // 2) as i:
                    for u in range(2):
                        g = i * 2 + u
                        dve.wait_ge(s_ea[u], (i + 1) * 64)
                        nc.vector.tensor_tensor(prod16[:, :, :], ea16[:, u, :, :], bcast(a16[:, :], 1, [P, SG, 16]), ALU.mult).then_inc(s_p16, 1)
                        dve.wait_ge(s_kc, g + 1)
                        dve.wait_ge(s_upd[1], g * SG + 1)
                        for j in range(SG):
                            for k in range(2):
                                if k == 0:
                                    dve.wait_ge(s_get, g * SG + j + 1)
                                nc.vector.scalar_tensor_tensor(junk[:, j % 4, k, 0, :], look[j % 4][:, k, 0, :], keycol[:, u, k, j:j + 1],
                                                               tri[:, :], ALU.is_equal, ALU.mult, accum_out=cnt[:, u, k, j:j + 1])
                                m = nc.vector.scalar_tensor_tensor(junk[:, j % 4, k, 1, :], look[j % 4][:, k, 1, :], 1.0,
                                                                   onehot[:, u, k, 1, j, :], ALU.mult, ALU.mult,
                                                                   accum_out=sel[:, u, k, j:j + 1])
                            m.then_inc(s_pick, 1)
                            onehots(g + 1, 1 - u, j)
                            if j == 5:
                                dve.wait_ge(s_free, g + 1)
                                dve.wait_ge(s_p16, g + 1)
                                nc.vector.tensor_reduce(rec[:, u, :, EC], prod16[:, :, :], AX.X, ALU.add)
                                nc.vector.tensor_copy(rec[:, u, :, SRC], keycol[:, u, 1, :])
                                nc.vector.tensor_copy(rec[:, u, :, DST], keycol[:, u, 0, :])
                        dve.wait_ge(s_pick, (g + 1) * SG + 4)
                        nc.vector.tensor_tensor(pos[:, u, :, :], cnt[:, u, :, :], sel[:, u, :, :], ALU.add).then_inc(s_pos, 1)
                        dve.wait_ge(s_m3, g + 1)
                        nc.vector.tensor_tensor(rec[:, u, :, 0:C], xps[:, :].rearrange("p (t c) -> p t c", c=C),
                                                bcast(w1[:, bass.ds(g * SG, SG)], 2, [P, SG, C]), ALU.mult).then_inc(s_rec, 1)

            @block.gpsimd
            def _(pool):
                with pool.Fori(0, NG // 2) as i:
                    for u in range(2):
                        g = i * 2 + u
                        pool.wait_ge(s_pos, g + 1)
                        pool.wait_ge(s_rec, g + 3)
                        pool.nop(nofuse=True)
                        for j in range(SG):
                            for k, out, row in ((0, A, rec[:, u, j, :]), (1, Bl, rec[:, u, j, SRC:SRC + 4])):
                                nc.gpsimd.indirect_dma_start(
                                    out=out, out_offset=bass.IndirectOffsetOnAxis(ap=pos[:, u, k, j:j + 1], axis=0),
                                    in_=row, in_offset=None, bounds_check=D.NSLOT - 1, oob_is_err=False).then_inc(s_sc[u], 16)
                for u in range(2):
                    pool.wait_ge(s_sc[u], NG // 2 * 2 * SG * 16)

            @block.scalar
            def _(act):
                act.wait_ge(s_c0, 1)
                for k in range(2):
                    nc.scalar.copy(Csb[:, k, :], cps[k][:, :]).then_inc(s_cs[k], 1)
                def keycols(g, u):
                    nc.scalar.copy(keycol[:, u, :, :], keyf[:, :, bass.ds(g * SG, SG)])
                    nc.scalar.copy(hlcol[:, u, :, :, :].rearrange("p k h t -> p (k h t)"),
                                   hilo[:, bass.ds(g, 1), :, :, :].rearrange("p o k h t -> p (o k h t)")).then_inc(s_kc, 1)

                def turn_copy(g, u, k):
                    act.wait_ge(s_ot, g * 2 + k + 1)
                    nc.scalar.copy(ohT[:, u, k, :, :], otp[:, :, :]).then_inc(s_oc, 1)
                for k in range(2):
                    turn_copy(0, 0, k)
                keycols(0, 0)
                act.wait_ge(s_kc, 1)
                nc.scalar.activation(warm[:, :], keycol[:, 0, 0, 0:1], ACT.Silu)
                with act.Fori(0, NG // 2) as i:
                    for u in range(2):
                        g = i * 2 + u
                        v = 1 - u
                        for j in range(SG):
                            for k in range(2):
                                act.wait_ge(s_upd[k], g * SG + j + 2)
                                nc.scalar.copy(Csb[:, k, :], cps[k][:, :]).then_inc(s_cs[k], 1)
                            if j == 1:
                                act.wait_ge(s_xt, g + 1)
                                nc.scalar.copy(eaT[:, :], xps[:, :]).then_inc(s_xc, 1)
                            if j == 4:
                                turn_copy(g + 1, v, 0)
                            if j == 3:
                                act.wait_ge(s_m1, g + 1)
                                nc.scalar.activation(h1[:, :], xps[:, :], ACT.Silu, bias=bb[:, 0:1]).then_inc(s_h1, 1)
                            if j == 5:
                                act.wait_ge(s_m2, g + 1)
                                nc.scalar.activation(h2[:, :], xps[:, :], ACT.Silu, bias=bb[:, 1:2]).then_inc(s_h2, 1)
                            if j == 6:
                                turn_copy(g + 1, v, 1)
                            if j == 3:
                                act.wait_ge(s_pick, g * SG + 4)
                                keycols(g + 1, v)

            @block.tensor
            def _(pe):
                def turn(g, u, k):
                    pe.wait_ge(s_oc, g * 2 + k + 1)
                    for j in range(SG):
                        m = nc.tensor.transpose(otp[:, j, :], onehot[:, u, k, 0, j, :], K.identb[:, :])
                    m.then_inc(s_ot, 1)
                pe.sem_inc(s_oc, 1)
                pe.sem_inc(s_pick, 4)
                pe.sem_inc(s_upd[0], 1)
                pe.sem_inc(s_upd[1], 1)
                for k in range(2):
                    m = nc.tensor.matmul(cps[k][:, :], K.ident[:, :], base[:, k, :], start=True, stop=True)
                m.then_inc(s_c0, 1)
                for k in range(2):
                    pe.wait_ge(s_one, 2 * k + 2)
                    turn(0, 0, k)
                with pe.Fori(0, NG // 2) as i:
                    for u in range(2):
                        g = i * 2 + u
                        v = 1 - u
                        pe.wait_ge(s_kc, g + 1)
                        pe.wait_ge(s_oc, g * 2 + 3)
                        pe.wait_ge(s_one, (g + 1) * SG)
                        for j in range(SG):
                            pe.wait_ge(s_pick, g * SG + j + 1)
                            for k in range(2):
                                nc.tensor.matmul(look[j % 4][:, k, 0, :], hlcol[:, u, k, 0, j:j + 1].to_broadcast([P, P]),
                                                 K.ident128b[:, :], start=True, stop=False)
                                nc.tensor.matmul(look[j % 4][:, k, 0, :], hlcol[:, u, k, 1, j:j + 1].to_broadcast([P, P]),
                                                 K.identb[:, :], start=False, stop=True)
                            for k in range(2):
                                pe.wait_ge(s_cs[k], g * SG + j + 1)
                                m = nc.tensor.matmul(look[j % 4][:, k, 1, :], ohT[:, u, k, j, :], Csb[:, k, :], start=True, stop=True)
                                if k == 1:
                                    m.then_inc(s_get, 1)
                                nc.tensor.matmul(cps[k][:, :], K.ident[:, :], Csb[:, k, :], start=True, stop=False)
                                nc.tensor.matmul(cps[k][:, :], onehot[:, u, k, 0, j, :], onehot[:, u, k, 1, j, :],
                                                 start=False, stop=True).then_inc(s_upd[k], 1)
                            if j == 1:
                                pe.wait_ge(s_ea[u], (i + 1) * 64)
                                pe.wait_ge(s_rec, g + 2)
                                for q in range(SG // 2):
                                    m = nc.tensor.transpose(xps[:, q * P:(q + 1) * P],
                                                            ea[:, u, 2 * q:2 * q + 2, :].rearrange("p t c -> p (t c)"), K.ident[:, :])
                                m.then_inc(s_xt, 1)
                            if j == 3:
                                pe.wait_ge(s_one, (g + 1) * SG + 2)
                                turn(g + 1, v, 0)
                            if j == 3:
                                pe.wait_ge(s_xc, g + 1)
                                nc.tensor.matmul(xps[:, :], w1d[:, :], eaT[:, :], start=True, stop=True).then_inc(s_m1, 1)
                            if j == 5:
                                pe.wait_ge(s_one, (g + 1) * SG + 4)
                                turn(g + 1, v, 1)
                            if j == 5:
                                pe.wait_ge(s_h1, g + 1)
                                nc.tensor.matmul(xps[:, :], w2d[:, :], h1[:, :], start=True, stop=True).then_inc(s_m2, 1)
                            if j == 7:
                                pe.wait_ge(s_h2, g + 1)
                                for q in range(SG // 2):
                                    nc.tensor.matmul(xps[:, q * P:(q + 1) * P], h2[:, q * P:(q + 1) * P], w3d[:, :], start=True, stop=False)
                                    m = nc.tensor.matmul(xps[:, q * P:(q + 1) * P], K.ones[0:1, :], b3[0:1, q * P:(q + 1) * P],
                                                         start=False, stop=True)
                                m.then_inc(s_m3, 1)


class Shared:
    pass


def skewed(eng, n, stages, enter=None):
    first = max(a for a, _ in stages)
    lastly = -min(min(a for a, _ in stages), 0)

    def step(i, u, low, high):
        for ahead, run in stages:
            q = u + ahead
            if low is not None and q < low or high is not None and q >= high:
                continue
            run(i + q // RING, q % RING)
    for s in range(-first, 0):
        step(0, s, 0, n * RING)

    def body(i, last):
        if enter is not None:
            enter(i)
        for u in range(RING):
            step(i, u, 0 if isinstance(i, int) and i == 0 else None, RING if last else None)
    loop(eng, n, body)
    for s in range(RING, RING + lastly):
        step(n - 1, s, None, RING)


class Count:

    def __init__(self, s):
        self.sem = s
        self.base = 0


class Counts:

    def __init__(self, sem):
        self.make, self.known = sem, {}

    def get(self, name):
        if name not in self.known:
            self.known[name] = Count(self.make(name))
        return self.known[name]


def finished(*added):
    for s, n in added:
        s.base += n


def wait(eng, s, value):
    if isinstance(value, int) and value <= 0:
        return
    if isinstance(s, Count):
        eng.wait_ge(s.sem, value + s.base)
    else:
        eng.wait_ge(s, value)


def loop(eng, n, body):
    body(0, n == 1)
    if n > 2:
        with eng.Fori(1, n - 1) as i:
            body(i, False)
    if n > 1:
        body(n - 1, True)


def node_stage(nc, counts, D, K, name, kin, weights, widths, feed, evict, table=None, bias=True):
    n = D.NB // 8
    tw = table.shape[1] if table is not None else 4
    rows = kin + 1 if bias else kin
    with ExitStack() as ctx:
        fed = ctx.enter_context(nc.sbuf_tensor(f"{name}_fed", [P, 2, 4, kin], F32))
        fedT = ctx.enter_context(nc.sbuf_tensor(f"{name}_fedT", [P, 2, 4 * P], F32))
        stage = ctx.enter_context(nc.sbuf_tensor(f"{name}_stage", [P, 2, 4, tw], F32))
        turned = [ctx.enter_context(nc.psum_tensor(f"{name}_turned{u}", [P, 4 * P], F32)) for u in range(2)]
        prod = [[ctx.enter_context(nc.psum_tensor(f"{name}_prod{u}{c}", [P, 4, w], F32)) for c, w in enumerate(widths)]
                for u in range(2)]
        s_fed, s_turn, s_copy, s_mm, s_ev = (counts.get("node_fed"), counts.get("node_turned"), counts.get("node_copied"),
                                             counts.get("node_products"), counts.get("node_evicted"))
        s_one = counts.get("node_ones")
        s_tab = [counts.get(f"node_stored{u}") for u in range(2)]
        with nc.Block() as block:
            @block.gpsimd
            def _(pool):
                nc.gpsimd.memset(stage[:, :, :, :], 0.0).then_inc(s_one.sem, 1)

            @block.vector
            def _(dve):
                def fed_group(i, u):
                    g = i * 2 + u
                    wait(dve, s_turn, g - 1)
                    feed(dve, g, fed[:, u, :, :]).then_inc(s_fed.sem, 1)
                if bias:
                    nc.vector.memset(fedT[kin:kin + 1, :, :], 1.0).then_inc(s_one.sem, 1)
                wait(dve, s_one, 2 if bias else 1)
                for u in range(2):
                    fed_group(0, u)

                def body(i, last):
                    for u in range(2):
                        g = i * 2 + u
                        wait(dve, s_mm, g + 1)
                        if table is not None:
                            wait(dve, s_tab[u], i * 16)
                        evict(dve, g, [prod[u][c][:, :, :] for c in range(len(widths))], stage[:, u, :, :]).then_inc(s_ev.sem, 1)
                        if not last:
                            fed_group(i + 1, u)
                loop(dve, n, body)

            @block.scalar
            def _(act):
                wait(act, s_one, 2 if bias else 1)

                def body(i, last):
                    for u in range(2):
                        g = i * 2 + u
                        wait(act, s_turn, g + 1)
                        wait(act, s_mm, g - 1)
                        nc.scalar.copy(fedT[0:kin, u, :], turned[u][0:kin, :]).then_inc(s_copy.sem, 1)
                loop(act, n, body)

            @block.tensor
            def _(pe):
                def body(i, last):
                    for u in range(2):
                        g = i * 2 + u
                        wait(pe, s_fed, g + 1)
                        wait(pe, s_copy, g - 1)
                        pe.nop(nofuse=True)
                        for j in range(4):
                            m = nc.tensor.transpose(turned[u][0:kin, j * P:(j + 1) * P], fed[:, u, j, :], K.ident[:, :])
                        m.then_inc(s_turn.sem, 1)
                        wait(pe, s_copy, g + 1)
                        wait(pe, s_ev, g - 1)
                        for j in range(4):
                            c0 = 0
                            for c, w in enumerate(widths):
                                m = nc.tensor.matmul(prod[u][c][:, j, :], fedT[0:rows, u, j * P:(j + 1) * P],
                                                     weights[0:rows, c0:c0 + w], start=True, stop=True)
                                c0 += w
                        m.then_inc(s_mm.sem, 1)
                loop(pe, n, body)

            if table is not None:
                @block.sync
                def _(sp):
                    view = table.rearrange("(g j p) c -> p g j c", j=4, p=P)

                    def body(i, last):
                        for u in range(2):
                            g = i * 2 + u
                            wait(sp, s_ev, g + 1)
                            sp.dma_start(view[:, bass.ds(g, 1), :, :].rearrange("p o j c -> p (o j) c"), stage[:, u, :, :]).then_inc(s_tab[u].sem, 16)
                    loop(sp, n, body)
                    for u in range(2):
                        wait(sp, s_tab[u], n * 16)
        finished(*[(s, 2 * n) for s in (s_fed, s_turn, s_copy, s_mm, s_ev)], (s_one, 2 if bias else 1),
                 *[(s, 16 * n) for s in s_tab if table is not None])



def layer_norm(nc, counts, D, K, name, out=None):
    NB = D.NB
    with ExitStack() as ctx:
        sq = ctx.enter_context(nc.sbuf_tensor(f"{name}_sq", [P, NB, C], F32))
        m = ctx.enter_context(nc.sbuf_tensor(f"{name}_m", [P, NB], F32))
        v = ctx.enter_context(nc.sbuf_tensor(f"{name}_v", [P, NB], F32))
        s_step, s_c, s_sq, s_v, s_sd, s_out = (counts.get("norm_steps"), counts.get("norm_centred"), counts.get("norm_squared"),
                                               counts.get("norm_var"), counts.get("norm_sd"), counts.get("norm_stored"))
        s_x = counts.get("norm_normed")
        with nc.Block() as block:
            @block.vector
            def _(dve):
                step = stepper(dve, s_step)
                step(nc.vector.tensor_reduce(m[:, :], K.x[:, :, :], AX.X, ALU.add))
                step(nc.vector.tensor_single_scalar(m[:, :], m[:, :], 1.0 / C, ALU.mult))
                nc.vector.tensor_tensor(K.x[:, :, :], K.x[:, :, :], bcast(m[:, :], 2, [P, NB, C]), ALU.subtract).then_inc(s_c.sem, 1)
                wait(dve, s_sq, 1)
                step(nc.vector.tensor_reduce(v[:, :], sq[:, :, :], AX.X, ALU.add))
                nc.vector.tensor_scalar(v[:, :], v[:, :], 1.0 / C, LN_EPS, ALU.mult, ALU.add).then_inc(s_v.sem, 1)
                wait(dve, s_sd, 1)
                step(nc.vector.reciprocal(v[:, :], v[:, :]))
                nc.vector.tensor_tensor(K.x[:, :, :], K.x[:, :, :], bcast(v[:, :], 2, [P, NB, C]), ALU.mult).then_inc(s_x.sem, 1)

            @block.scalar
            def _(act):
                wait(act, s_c, 1)
                nc.scalar.activation(sq[:, :, :], K.x[:, :, :], ACT.Square).then_inc(s_sq.sem, 1)
                wait(act, s_v, 1)
                nc.scalar.activation(v[:, :], v[:, :], ACT.Sqrt).then_inc(s_sd.sem, 1)

            if out is not None:
                @block.sync
                def _(sp):
                    full = D.N // P
                    wait(sp, s_x, 1)
                    sp.dma_start(out[0:full * P, :].rearrange("(b p) c -> p b c", p=P), K.x[:, 0:full, :]).then_inc(s_out.sem, 16)
                    if D.N > full * P:
                        sp.dma_start(out[full * P:D.N, :], K.x[0:D.N - full * P, full, :]).then_inc(s_out.sem, 16)
                    wait(sp, s_out, 32 if D.N > full * P else 16)
        finished((s_step, 4), *[(s, 1) for s in (s_c, s_sq, s_v, s_sd, s_x)])



def stepper(eng, s):
    n = [0]

    def step(ins):
        n[0] += 1
        ins.then_inc(s.sem if isinstance(s, Count) else s, 1)
        wait(eng, s, n[0])
    return step


def load_nodes(nc, sem, D, K, dram):
    s_z, s_x = sem("nodes_zeroed"), sem("nodes_loaded")
    with nc.Block() as block:
        @block.gpsimd
        def _(pool):
            nc.gpsimd.memset(K.x[:, :, :], 0.0).then_inc(s_z, 1)

        @block.sync
        def _(sp):
            full = D.N // P
            sp.wait_ge(s_z, 1)
            sp.dma_start(K.x[:, 0:full, :], dram["x"][0:full * P, :].rearrange("(b p) c -> p b c", p=P)).then_inc(s_x, 16)
            if D.N > full * P:
                sp.dma_start(K.x[0:D.N - full * P, full, :], dram["x"][full * P:D.N, :]).then_inc(s_x, 16)
            sp.wait_ge(s_x, 32 if D.N > full * P else 16)


def score_edges(nc, sem, D, K, A, tabS, tabD, wkv, al, V):
    NT = D.NT
    n = NT // BODY
    with ExitStack() as ctx:
        def sb(nm, s, d=F32):
            return ctx.enter_context(nc.sbuf_tensor(nm, s, d))

        def ps(nm, s, d=F32):
            return ctx.enter_context(nc.psum_tensor(nm, s, d))
        rec = sb("sc_rec", [P, RING, G, REC])
        idx = sb("sc_idx", [P, RING, G], I32)
        rows = sb("sc_rows", [P, RING, G, C])
        oh = sb("sc_oh", [P, 2, G, P], BF16)
        ohT = sb("sc_ohT", [P, 2, G, P])
        tp = sb("sc_tp", [P, 2, G, C])
        tpT = sb("sc_tpT", [P, 2, G * P])
        kv = sb("sc_kv", [P, RING, G, P])
        qk = sb("sc_qk", [P, 2, G, C])
        ot = ps("sc_ot", [P, G, P], BF16)
        loc = [ps(f"sc_loc{u}", [P, G, P]) for u in range(RING)]
        tt = ps("sc_tt", [P, G * P])
        kvp = [ps(f"sc_kvp{u}", [P, G, P]) for u in range(2)]
        s_ld = [sem(f"sc_loaded{u}") for u in range(RING)]
        s_ga = [sem(f"sc_gathered{u}") for u in range(RING)]
        s_vs = [sem(f"sc_stored{u}") for u in range(RING)]
        s_idx, s_kl, s_oh, s_ot, s_ohT, s_loc, s_sum, s_tp, s_tt, s_tpT, s_kvp, s_kv, s_qk, s_al, s_one, s_keep = (
            sem("sc_" + x) for x in ("indices", "keys", "onehots", "turned", "turned_copied", "dst_rows", "sums", "messages",
                                     "msg_turned", "msg_copied", "kv_products", "kv_copied", "qk_products", "scores", "ones", "kept"))
        recv = A.rearrange("(g j p) c -> p g j c", j=G, p=P)
        vv = V.rearrange("(g p j) c -> p g j c", j=G, p=P)
        with nc.Block() as block:
            @block.sync
            def _(sp):
                def load(i, u):
                    g = i * RING + u
                    wait(sp, s_tp, g - RING + 1)
                    wait(sp, s_keep, g - RING + 1)
                    wait(sp, s_kl, g - RING + 1)
                    sp.dma_start(rec[:, u, :, :], recv[:, bass.ds(g, 1), :, :].rearrange("p o j c -> p (o j) c")).then_inc(s_ld[u], 16)

                def store(i, u):
                    g = i * RING + u
                    sp.wait_ge(s_kv, g + 1)
                    sp.dma_start(vv[:, bass.ds(g, 1), :, :].rearrange("p o j c -> p (o j) c"), kv[:, u, :, C:2 * C]).then_inc(s_vs[u], 16)
                skewed(sp, n, [(3, load), (-2, store)])
                for u in range(RING):
                    sp.wait_ge(s_vs[u], n * 16)

            @block.gpsimd
            def _(pool):
                def gather(i, u):
                    g = i * RING + u
                    pool.wait_ge(s_idx, g + 1)
                    wait(pool, s_sum, g - RING + 1)
                    pool.nop(nofuse=True)
                    for j in range(G):
                        nc.gpsimd.indirect_dma_start(out=rows[:, u, j, :], out_offset=None, in_=tabS,
                                                     in_offset=bass.IndirectOffsetOnAxis(ap=idx[:, u, j:j + 1], axis=0)).then_inc(s_ga[u], 16)
                skewed(pool, n, [(0, gather)])

            @block.scalar
            def _(act):
                def ids(i, u):
                    g = i * RING + u
                    act.wait_ge(s_ld[u], (i + 1) * 16)
                    wait(act, s_ga[u], i * 16 * G)
                    nc.scalar.copy(idx[:, u, :], rec[:, u, :, SRC]).then_inc(s_idx, 1)
                    nc.scalar.copy(K.idx[0][:, bass.ds(g * G, G)], rec[:, u, :, SRC])
                    nc.scalar.copy(K.ec[0][:, bass.ds(g * G, G)], rec[:, u, :, EC]).then_inc(s_keep, 1)

                def copy_onehot(i, u):
                    g = i * RING + u
                    act.wait_ge(s_ot, g + 1)
                    wait(act, s_loc, g - 1)
                    nc.scalar.copy(ohT[:, u % 2, :, :], ot[:, :, :]).then_inc(s_ohT, 1)

                def copy_messages(i, u):
                    g = i * RING + u
                    act.wait_ge(s_tt, g + 1)
                    wait(act, s_kvp, g - 1)
                    nc.scalar.copy(tpT[0:C, u % 2, :], tt[0:C, :]).then_inc(s_tpT, 1)

                def copy_kv(i, u):
                    g = i * RING + u
                    act.wait_ge(s_kvp, g + 1)
                    wait(act, s_qk, g - RING + 1)
                    wait(act, s_vs[u], i * 16)
                    nc.scalar.copy(kv[:, u, :, :], kvp[u % 2][:, :, :]).then_inc(s_kv, 1)
                skewed(act, n, [(-1, copy_kv), (2, copy_onehot), (0, copy_messages), (3, ids)])

            @block.tensor
            def _(pe):
                pe.wait_ge(s_one, 1)
                held = {}

                def turn_onehot(i, u):
                    g = i * RING + u
                    pe.wait_ge(s_oh, g + 1)
                    wait(pe, s_ohT, g)
                    for j in range(G):
                        m = nc.tensor.transpose(ot[:, j, :], oh[:, u % 2, j, :], K.identb[:, :])
                    m.then_inc(s_ot, 1)

                def dst_rows(i, u):
                    g = i * RING + u
                    pe.wait_ge(s_ohT, g + 1)
                    wait(pe, s_qk, g - RING + 1)
                    for j in range(G):
                        m = nc.tensor.matmul(loc[u][:, j, :], ohT[:, u % 2, j, :],
                                             tabD[:, bass.ds(held["b"][(u - 1) % RING * G + j], 1), :].rearrange("p o c -> p (o c)"),
                                             start=True, stop=True)
                    m.then_inc(s_loc, 1)

                def turn_messages(i, u):
                    g = i * RING + u
                    pe.wait_ge(s_tp, g + 1)
                    wait(pe, s_tpT, g)
                    pe.nop(nofuse=True)
                    for j in range(G):
                        m = nc.tensor.transpose(tt[0:C, j * P:(j + 1) * P], tp[:, u % 2, j, :], K.ident[:, :])
                    m.then_inc(s_tt, 1)

                def kv_products(i, u):
                    g = i * RING + u
                    pe.wait_ge(s_tpT, g + 1)
                    wait(pe, s_kv, g - 1)
                    for j in range(G):
                        m = nc.tensor.matmul(kvp[u % 2][:, j, :], tpT[0:C + 1, u % 2, j * P:(j + 1) * P], wkv[0:C + 1, :], start=True, stop=True)
                    m.then_inc(s_kvp, 1)

                def blocks(i):
                    held["b"] = nc.values_load_multi_w_load_instructions(
                        K.blk[0:1, 0, bass.ds(i * BODY + G, BODY)], engines=PE_ONLY, min_val=0, max_val=D.NB - 1)[1]
                held["b"] = [0] * (3 * G) + list(nc.values_load_multi_w_load_instructions(
                    K.blk[0:1, 0, 0:G], engines=PE_ONLY, min_val=0, max_val=D.NB - 1)[1])
                skewed(pe, n, [(1, dst_rows), (-1, kv_products), (2, turn_onehot), (0, turn_messages)], blocks)

            @block.vector
            def _(dve):
                def prep(i, u):
                    g = i * RING + u
                    dve.wait_ge(s_ld[u], (i + 1) * 16)
                    nc.vector.tensor_tensor(K.kl[0][:, bass.ds(g * G, G)], rec[:, u, :, DST], K.first[:, 0, bass.ds(g * G, G)],
                                            ALU.subtract).then_inc(s_kl, 1)
                    dve.wait_ge(s_kl, g + 1)
                    wait(dve, s_ot, g - 1)
                    nc.vector.tensor_tensor(oh[:, u % 2, :, :], bcast(K.iota[:, :], 1, [P, G, P]),
                                            bcast(K.kl[0][:, bass.ds(g * G, G)], 2, [P, G, P]), ALU.is_equal).then_inc(s_oh, 1)

                def add_rows(i, u):
                    g = i * RING + u
                    dve.wait_ge(s_loc, g + 1)
                    dve.wait_ge(s_ga[u], (i + 1) * 16 * G)
                    wait(dve, s_tt, g - 1)
                    nc.vector.tensor_tensor(tp[:, u % 2, :, :], rows[:, u, :, :], loc[u][:, :, 0:C], ALU.add).then_inc(s_sum, 1)

                def weigh(i, u):
                    g = i * RING + u
                    dve.wait_ge(s_sum, g + 1)
                    nc.vector.tensor_tensor(tp[:, u % 2, :, :], tp[:, u % 2, :, :], rec[:, u, :, 0:C], ALU.mult).then_inc(s_tp, 1)

                def multiply(i, u):
                    g = i * RING + u
                    dve.wait_ge(s_kv, g + 1)
                    wait(dve, s_al, g - 1)
                    nc.vector.tensor_tensor(qk[:, u % 2, :, :], loc[u][:, :, C:2 * C], kv[:, u, :, 0:C], ALU.mult).then_inc(s_qk, 1)

                def reduce(i, u):
                    g = i * RING + u
                    dve.wait_ge(s_qk, g + 1)
                    nc.vector.tensor_reduce(al[:, bass.ds(g * G, G), :], qk[:, u % 2, :, :].rearrange("p j (h d) -> p j h d", h=HEADS),
                                            AX.X, ALU.add).then_inc(s_al, 1)
                nc.vector.memset(tpT[C:C + 1, :, :], 1.0).then_inc(s_one, 1)
                skewed(dve, n, [(2, prep), (-2, multiply), (0, add_rows), (-2, reduce), (0, weigh)])


def segment_softmax(nc, counts, D, K, name, X, heads, k, slope=None, last=None):
    NT, NSLOT = D.NT, D.NSLOT
    chunks = D.chunks()
    with ExitStack() as ctx:
        def sb(nm, s, d=F32):
            return ctx.enter_context(nc.sbuf_tensor(f"{name}_{nm}", s, d))
        keyT = sb("key", [P, NT])
        keys = sb("keys", [P, 3, NT])
        pen = sb("pen", [P, 2, NT])
        val = sb("val", [P, NT])
        run = sb("run", [P, 2, NT])
        edge = sb("edge", [P, 2, 2])
        rowv = sb("row", [1, 2, 2, P])
        crow = sb("crow", [1, 2, P + 2])
        carry = sb("carry", [P, 2])
        turn = sb("turn", [P, 2, P])
        turnd = sb("turnd", [P, 2, P])
        sent = sb("sent", [1, 1])
        kd = nc.dram_tensor(f"{name}_keys_dram", (NSLOT + 2,), F32).ap()
        sd = nc.dram_tensor(f"{name}_scores_dram", (NSLOT,), F32).ap()
        md = nc.dram_tensor(f"{name}_maxima_dram", (NSLOT,), F32).ap()
        tps = [ctx.enter_context(nc.psum_tensor(f"{name}_t{u}", [P, P], F32)) for u in range(2)]
        rps = ctx.enter_context(nc.psum_tensor(f"{name}_r", [1, 2, 2, P], F32))
        cps = ctx.enter_context(nc.psum_tensor(f"{name}_c", [P, 2], F32))

        s_a = [counts.get(f"soft_out{u}") for u in range(2)]
        s_b = [counts.get(f"soft_in{u}") for u in range(2)]
        s_t, s_c = counts.get("soft_turned"), counts.get("soft_turn_copied")
        s_st, s_e, s_r, s_cr, s_cp, s_ld, s_v, s_x, s_w = (counts.get(f"soft_{x}") for x in (
            "steps", "ends", "rows", "carry_row", "carry_col", "loaded", "scanned", "exped", "written"))
        s_i = counts.get("soft_init")

        def send(src_of, dst, n0, n_out):
            with nc.Block() as block:
                @block.tensor
                def _(pe):
                    for q, (c, w) in enumerate(chunks):
                        wait(pe, s_c, n0 + q - 1)
                        nc.tensor.transpose(tps[(n0 + q) % 2][0:w, :], src_of(c, w), K.ident[:, :]).then_inc(s_t.sem, 1)

                @block.vector
                def _(dve):
                    for q, (c, w) in enumerate(chunks):
                        wait(dve, s_t, n0 + q + 1)
                        u = (n_out + q) % 2
                        wait(dve, s_a[u], (n_out + q) // 2 * 16)
                        nc.vector.tensor_copy(turn[0:w, u, :], tps[(n0 + q) % 2][0:w, :]).then_inc(s_c.sem, 1)

                @block.sync
                def _(sp):
                    for q, (c, w) in enumerate(chunks):
                        wait(sp, s_c, n0 + q + 1)
                        u = (n_out + q) % 2
                        sp.dma_start(dst[c * P:(c + w) * P].rearrange("(t p) -> t p", p=P), turn[0:w, u, :]).then_inc(s_a[u].sem, 16)
                    for u in range(2):
                        wait(sp, s_a[u], (n_out + len(chunks) + 1 - u) // 2 * 16)

        def receive(src, dst_of, n0, n_in):
            with nc.Block() as block:
                @block.sync
                def _(sp):
                    for q, (c, w) in enumerate(chunks):
                        u = (n_in + q) % 2
                        wait(sp, s_t, n0 + q - 1)
                        sp.dma_start(turnd[0:w, u, :], src[c * P:(c + w) * P].rearrange("(t p) -> t p", p=P)).then_inc(s_b[u].sem, 16)

                @block.tensor
                def _(pe):
                    for q, (c, w) in enumerate(chunks):
                        u = (n_in + q) % 2
                        wait(pe, s_b[u], ((n_in + q) // 2 + 1) * 16)
                        wait(pe, s_c, n0 + q - 1)
                        nc.tensor.transpose(tps[(n0 + q) % 2][:, 0:w], turnd[0:w, u, :], K.ident[0:w, 0:w]).then_inc(s_t.sem, 1)

                @block.vector
                def _(dve):
                    for q, (c, w) in enumerate(chunks):
                        wait(dve, s_t, n0 + q + 1)
                        nc.vector.tensor_copy(dst_of(c, w), tps[(n0 + q) % 2][:, 0:w]).then_inc(s_c.sem, 1)

        with nc.Block() as block:
            @block.vector
            def _(dve):
                nc.vector.tensor_tensor(keyT[:, :], K.kl[k][:, 0:NT], K.first[:, k, :], ALU.add)
                nc.vector.memset(sent[:, :], -5.0).then_inc(s_i.sem, 1)
                nc.vector.memset(crow[:, :, :], -BIG)

            @block.sync
            def _(sp):
                wait(sp, s_i, 1)
                sp.dma_start(kd[0:1].rearrange("(o c) -> o c", o=1), sent[:, :]).then_inc(s_w.sem, 16)
                sp.dma_start(kd[NSLOT + 1:NSLOT + 2].rearrange("(o c) -> o c", o=1), sent[:, :]).then_inc(s_w.sem, 16)
                wait(sp, s_w, 32)
        nch = len(chunks)
        turns = stores = loads = 0
        send(lambda c, w: keyT[:, c:c + w], kd[1:NSLOT + 1], turns, stores)
        turns += nch
        stores += nch
        steps = [0]

        def stepv(dve, ins):
            steps[0] += 1
            ins.then_inc(s_st.sem, 1)
            wait(dve, s_st, steps[0])
        with nc.Block() as block:
            @block.sync
            def _(sp):
                for d in range(3):
                    sp.dma_start(keys[:, d, :], kd[d:d + NSLOT].rearrange("(p t) -> p t", p=P)).then_inc(s_ld.sem, 16)

            @block.vector
            def _(dve):
                wait(dve, s_ld, 48)
                for side, d in ((0, 0), (1, 2)):
                    stepv(dve, nc.vector.tensor_tensor(pen[:, side, :], keys[:, d, :], keys[:, 1, :], ALU.is_equal))
                if last is not None:
                    stepv(dve, nc.vector.tensor_scalar(keys[:, 0, :], pen[:, 1, :], -1.0, 1.0, ALU.mult, ALU.add))
                stepv(dve, nc.vector.tensor_scalar(pen[:, :, :], pen[:, :, :], BIG, -BIG, ALU.mult, ALU.add))
                for side in range(2):
                    stepv(dve, nc.vector.tensor_reduce(edge[:, side, 0:1], pen[:, side, :], AX.X, ALU.min))
        loaded = 3
        for h in range(heads):
            send(lambda c, w: X[:, c:c + w, h], sd, turns, stores)
            turns += nch
            stores += nch
            with nc.Block() as block:
                @block.sync
                def _(sp):
                    sp.dma_start(val[:, :], sd.rearrange("(p t) -> p t", p=P)).then_inc(s_ld.sem, 16)
                    wait(sp, s_x, h + 1)
                    sp.dma_start(sd.rearrange("(p t) -> p t", p=P), val[:, :]).then_inc(s_w.sem, 16)
                    if last is not None:
                        wait(sp, s_v, h + 1)
                        sp.dma_start(md.rearrange("(p t) -> p t", p=P), run[:, 1, :]).then_inc(s_w.sem, 16)
                    wait(sp, s_w, 32 + 16 * (h + 1) * (2 if last is not None else 1))

                @block.vector
                def _(dve):
                    wait(dve, s_ld, 16 * (4 + h))
                    if slope is not None:
                        stepv(dve, nc.vector.scalar_tensor_tensor(val[:, :], val[:, :], slope, val[:, :], ALU.mult, ALU.max))

                    def scans(initial):
                        f0, f1, fo = pen[:, 0, :], val[:, :], run[:, 0, :]
                        stepv(dve, nc.vector.tensor_tensor_scan(fo, f0, f1, initial(0), ALU.add, ALU.max))
                        b0, b1, bo = pen[:, 1, ::-1], val[:, ::-1], run[:, 1, ::-1]
                        stepv(dve, nc.vector.tensor_tensor_scan(bo, b0, b1, initial(1), ALU.add, ALU.max))
                    scans(lambda side: -BIG)
                    stepv(dve, nc.vector.tensor_copy(edge[:, 0, 1:2], run[:, 0, NT - 1:NT]))
                    nc.vector.tensor_copy(edge[:, 1, 1:2], run[:, 1, 0:1]).then_inc(s_e.sem, 1)
                    wait(dve, s_r, h + 1)
                    stepv(dve, nc.vector.tensor_copy(rowv[:, :, :, :], rps[:, :, :, :]))
                    stepv(dve, nc.vector.tensor_tensor_scan(crow[:, 0, 1:P + 1], rowv[:, 0, 0, :], rowv[:, 0, 1, :], -BIG, ALU.add, ALU.max))
                    stepv(dve, nc.vector.tensor_tensor_scan(crow[:, 1, P:0:-1], rowv[:, 1, 0, ::-1], rowv[:, 1, 1, ::-1], -BIG, ALU.add, ALU.max))
                    nc.vector.tensor_copy(rowv[:, 0, 0, 0:1], rowv[:, 0, 0, 0:1]).then_inc(s_cr.sem, 1)
                    wait(dve, s_cp, h + 1)
                    stepv(dve, nc.vector.tensor_copy(carry[:, :], cps[:, :]))
                    scans(lambda side: carry[:, side:side + 1])
                    stepv(dve, nc.vector.tensor_tensor(run[:, 0, :], run[:, 0, :], run[:, 1, :], ALU.max))
                    nc.vector.tensor_tensor(val[:, :], val[:, :], run[:, 0, :], ALU.subtract).then_inc(s_i.sem, 1)
                    if last is not None:
                        nc.vector.tensor_tensor(run[:, 1, :], run[:, 0, :], keys[:, 0, :], ALU.mult).then_inc(s_v.sem, 1)

                @block.scalar
                def _(act):
                    wait(act, s_i, 2 + h)
                    nc.scalar.activation(val[:, :], val[:, :], ACT.Exp).then_inc(s_x.sem, 1)

                @block.tensor
                def _(pe):
                    wait(pe, s_e, h + 1)
                    for side in range(2):
                        for q in range(2):
                            m = nc.tensor.transpose(rps[0:1, side, q, :], edge[:, side, q:q + 1], K.ident[:, :])
                    m.then_inc(s_r.sem, 1)
                    wait(pe, s_cr, h + 1)
                    for side, o in ((0, 0), (1, 2)):
                        m = nc.tensor.transpose(cps[:, side:side + 1], crow[0:1, side, o:o + P], K.ident[0:1, 0:1])
                    m.then_inc(s_cp.sem, 1)
            receive(sd, lambda c, w: X[:, c:c + w, h], turns, loads)
            turns += nch
            loads += nch
            if last is not None:
                receive(md, lambda c, w: last[:, c:c + w], turns, loads)
                turns += nch
                loads += nch
        finished(*[(s, (stores + 1 - u) // 2 * 16) for u, s in enumerate(s_a)],
                 *[(s, (loads + 1 - u) // 2 * 16) for u, s in enumerate(s_b)],
                 (s_t, turns), (s_c, turns), (s_st, steps[0]), *[(s, heads) for s in (s_e, s_r, s_cr, s_cp, s_x)],
                 (s_v, heads if last is not None else 0), (s_ld, 16 * (3 + heads)),
                 (s_w, 32 + 16 * heads * (2 if last is not None else 1)), (s_i, 1 + heads))



def gather_sum(nc, counts, D, K, name, k, table, acc):
    n = D.NT // BODY
    with ExitStack() as ctx:
        idx = ctx.enter_context(nc.sbuf_tensor(f"{name}_idx", [P, RING, G], I32))
        rows = ctx.enter_context(nc.sbuf_tensor(f"{name}_rows", [P, RING, G, C], F32))
        oh = ctx.enter_context(nc.sbuf_tensor(f"{name}_oh", [P, 2, G, P], F32))
        part = [ctx.enter_context(nc.psum_tensor(f"{name}_part{u}", [P, G, C], F32)) for u in range(2)]
        s_idx, s_oh, s_mm, s_acc = (counts.get(f"gather_{x}") for x in ("indices", "onehots", "products", "added"))
        s_ga = [counts.get(f"gather_gathered{u}") for u in range(RING)]
        with nc.Block() as block:
            @block.scalar
            def _(act):
                def body(i, last):
                    for u in range(RING):
                        g = i * RING + u
                        wait(act, s_mm, g - RING + 1)
                        nc.scalar.copy(idx[:, u, :], K.idx[k][:, bass.ds(g * G, G)]).then_inc(s_idx.sem, 1)
                loop(act, n, body)

            @block.gpsimd
            def _(pool):
                def body(i, last):
                    for u in range(RING):
                        g = i * RING + u
                        wait(pool, s_idx, g + 1)
                        pool.nop(nofuse=True)
                        for j in range(G):
                            nc.gpsimd.indirect_dma_start(out=rows[:, u, j, :], out_offset=None, in_=table,
                                                         in_offset=bass.IndirectOffsetOnAxis(ap=idx[:, u, j:j + 1], axis=0)).then_inc(s_ga[u].sem, 16)
                loop(pool, n, body)

            @block.tensor
            def _(pe):
                def body(i, last):
                    for u in range(RING):
                        g = i * RING + u
                        w = u % 2
                        wait(pe, s_ga[u], (i + 1) * 16 * G)
                        wait(pe, s_oh, g + 1)
                        wait(pe, s_acc, (g - 1) * G)
                        for j in range(G):
                            m = nc.tensor.matmul(part[w][:, j, :], oh[:, w, j, :], rows[:, u, j, :], start=True, stop=True)
                        m.then_inc(s_mm.sem, 1)
                loop(pe, n, body)
            add_parts(nc, D, K, block, k, n, oh, part, acc, C, s_oh, s_mm, s_acc)
        finished(*[(s, RING * n) for s in (s_idx, s_oh, s_mm)], (s_acc, D.NT), *[(s, 16 * G * n) for s in s_ga])



def add_parts(nc, D, K, block, k, n, oh, part, acc, width, s_oh, s_mm, s_acc, message=None):
    @block.vector
    def _(dve):
        def prep(i, u):
            g = i * RING + u
            w = u % 2
            wait(dve, s_mm, g - 1)
            if message is not None:
                message(dve, i, u)
            nc.vector.tensor_tensor(oh[:, w, :, :], bcast(K.iota[:, :], 1, [P, G, P]),
                                    bcast(K.kl[k][:, bass.ds(g * G, G)], 2, [P, G, P]), ALU.is_equal).then_inc(s_oh.sem, 1)
        prep(0, 0)

        def body(i, last):
            bs = nc.values_load_multi_w_load_instructions(K.blk[0:1, k, bass.ds(i * BODY, BODY)], engines=DVE_ONLY,
                                                          min_val=0, max_val=D.NB - 1)[1]
            for u in range(RING):
                g = i * RING + u
                w = u % 2
                if u < RING - 1:
                    prep(i, u + 1)
                elif not last:
                    prep(i + 1, 0)
                wait(dve, s_mm, g + 1)
                for j in range(G):
                    b = bs[u * G + j]
                    wait(dve, s_acc, g * G + j)
                    nc.vector.tensor_tensor(acc[:, bass.ds(b, 1), 0:width], acc[:, bass.ds(b, 1), 0:width],
                                            part[w][:, j:j + 1, 0:width], ALU.add).then_inc(s_acc.sem, 1)
        loop(dve, n, body)


def weighted_sum(nc, counts, D, K, name, k, V, X, heads, acc, last=None, spare=None):
    n = D.NT // BODY
    width = C + heads + (1 if last is not None else 0)
    half = RING // 2
    with ExitStack() as ctx:
        rows = ctx.enter_context(nc.sbuf_tensor(f"{name}_rows", [P, RING, G, C], F32))
        msg = ctx.enter_context(nc.sbuf_tensor(f"{name}_msg", [P, RING, G, REC], F32))
        if spare is None or spare.shape[1] < RING * G * P:
            oh = ctx.enter_context(nc.sbuf_tensor(f"{name}_oh", [P, RING, G, P], F32))
        else:
            oh = spare[:, 0:RING * G * P].rearrange("p (u j v) -> p u j v", u=RING, j=G)
        other = ctx.enter_context(nc.sbuf_tensor(f"{name}_other", [P, D.NB, width], F32))
        sums = ctx.enter_context(nc.sbuf_tensor(f"{name}_sums", [P, half, G, width], F32))
        part = [ctx.enter_context(nc.psum_tensor(f"{name}_part{u}", [P, G, P], F32)) for u in range(RING)]
        s_sum = counts.get("weigh_sums_copied")
        s_oh, s_mm, s_z, s_ex, s_one = (counts.get(f"weigh_{x}") for x in ("messages", "products", "zeroed", "extras", "onehots"))
        s_acc = [counts.get("weigh_added"), counts.get("weigh_other_added")]
        s_ld = [counts.get(f"weigh_loaded{u}") for u in range(RING)]
        vv = V.rearrange("(g p j) c -> p g j c", j=G, p=P)

        def add(on, eng, y, i, u, blocks):
            if u // half != y:
                return
            for j in range(G):
                done = (i * half + u - y * half) * G + j
                if j == 0 and y == 0:
                    wait(eng, s_mm, i * RING + u + 1)
                elif j == 0:
                    wait(eng, s_sum, i * half + u - half + 1)
                wait(eng, s_acc[y], done)
                b = blocks[(u - y * half) * G + j]
                to = (acc, other)[y]
                new = part[u][:, j:j + 1, 0:width] if y == 0 else sums[:, u - half, j:j + 1, :]
                on.tensor_tensor(to[:, bass.ds(b, 1), 0:width], to[:, bass.ds(b, 1), 0:width], new, ALU.add).then_inc(s_acc[y].sem, 1)

        def blocks_of(i, y, engines):
            return nc.values_load_multi_w_load_instructions(
                K.blk[0:1, k, bass.ds(i * BODY + y * (BODY // 2), BODY // 2)], engines=engines, min_val=0, max_val=D.NB - 1)[1]
        with nc.Block() as block:
            @block.gpsimd
            def _(pool):
                held = {}
                nc.gpsimd.memset(acc[:, :, :], 0.0).then_inc(s_z.sem, 1)
                nc.gpsimd.memset(other[:, :, :], 0.0).then_inc(s_z.sem, 1)
                wait(pool, s_z, 2)

                def message(i, u):
                    g = i * RING + u
                    wait(pool, s_mm, g - RING + 1)
                    wait(pool, s_ld[u], (i + 1) * 16)
                    xs = X[:, bass.ds(g * G, G), :]
                    nc.gpsimd.tensor_tensor(msg[:, u, :, 0:C].rearrange("p j (h d) -> p j h d", h=heads),
                                            rows[:, u, :, :].rearrange("p j (h d) -> p j h d", h=heads),
                                            xs.unsqueeze(3).to_broadcast([P, G, heads, C // heads]), ALU.mult).then_inc(s_oh.sem, 1)

                def blocks(i):
                    held["b"] = blocks_of(i, 1, POOL_ONLY)
                adding = (0, lambda i, u: add(nc.gpsimd, pool, 1, i, u, held["b"]))
                skewed(pool, n, [adding] if heads == 1 else [(2, message), adding], blocks)

            @block.sync
            def _(sp):
                def body(i, last_):
                    for u in range(RING):
                        g = i * RING + u
                        wait(sp, s_oh, g - RING + 1)
                        sp.dma_start(rows[:, u, :, :], vv[:, bass.ds(g, 1), :, :].rearrange("p o j c -> p (o j) c")).then_inc(s_ld[u].sem, 16)
                loop(sp, n, body)

            @block.tensor
            def _(pe):
                def body(i, last_):
                    for u in range(RING):
                        g = i * RING + u
                        wait(pe, s_oh, g + 1)
                        wait(pe, s_ex, g + 1)
                        wait(pe, s_one, g + 1)
                        if u < half:
                            wait(pe, s_acc[0], ((i - 1) * half + u + 1) * G)
                        else:
                            wait(pe, s_sum, (i - 1) * half + u - half + 1)
                        for j in range(G):
                            m = nc.tensor.matmul(part[u][:, j, 0:width], oh[:, u, j, :], msg[:, u, j, 0:width], start=True, stop=True)
                        m.then_inc(s_mm.sem, 1)
                loop(pe, n, body)

            @block.vector
            def _(dve):
                held = {}
                wait(dve, s_z, 2)

                def onehots(i, u):
                    g = i * RING + u
                    wait(dve, s_mm, g - RING + 1)
                    nc.vector.tensor_tensor(oh[:, u, :, :], bcast(K.iota[:, :], 1, [P, G, P]),
                                            bcast(K.kl[k][:, bass.ds(g * G, G)], 2, [P, G, P]), ALU.is_equal).then_inc(s_one.sem, 1)

                def blocks(i):
                    held["b"] = blocks_of(i, 0, DVE_ONLY)
                skewed(dve, n, [(2, onehots), (0, lambda i, u: add(nc.vector, dve, 0, i, u, held["b"]))], blocks)
                for y in range(2):
                    wait(dve, s_acc[y], D.NT // 2)
                nc.vector.tensor_tensor(acc[:, :, 0:width], acc[:, :, 0:width], other[:, :, :], ALU.add)

            @block.scalar
            def _(act):
                def extras(i, u):
                    g = i * RING + u
                    wait(act, s_mm, g - RING + 1)
                    m = nc.scalar.copy(msg[:, u, :, C:C + heads], X[:, bass.ds(g * G, G), :])
                    if last is not None:
                        m = nc.scalar.copy(msg[:, u, :, C + heads], last[:, bass.ds(g * G, G)])
                    m.then_inc(s_ex.sem, 1)

                def copy_sums(i, u):
                    if u >= half:
                        wait(act, s_mm, i * RING + u + 1)
                        wait(act, s_acc[1], ((i - 1) * half + u - half + 1) * G)
                        nc.scalar.copy(sums[:, u - half, :, :], part[u][:, :, 0:width]).then_inc(s_sum.sem, 1)

                def message(i, u):
                    g = i * RING + u
                    wait(act, s_ex, g + 1)
                    wait(act, s_ld[u], (i + 1) * 16)
                    for j in range(G):
                        m = nc.scalar.activation(msg[:, u, j, 0:C], rows[:, u, j, :], ACT.Copy, scale=msg[:, u, j, C:C + 1])
                    m.then_inc(s_oh.sem, 1)
                skewed(act, n, [(3, extras), (2, message), (0, copy_sums)] if heads == 1 else [(2, extras), (0, copy_sums)])
        finished(*[(s, RING * n) for s in (s_oh, s_mm, s_ex, s_one)], *[(s, D.NT // 2) for s in s_acc], (s_z, 2), (s_sum, half * n),
                 *[(s, 16 * n) for s in s_ld])


def read_list(nc, sem, D, K, Bl):
    chunks = D.chunks()
    with ExitStack() as ctx:
        raw = ctx.enter_context(nc.sbuf_tensor("rl_raw", [P, 2, P, 4], F32))
        tps = [ctx.enter_context(nc.psum_tensor(f"rl_t{u}", [P, 3, P], F32)) for u in range(2)]
        s_ld = [sem(f"rl_loaded{u}") for u in range(2)]
        s_t, s_c = sem("rl_turned"), sem("rl_copied")
        with nc.Block() as block:
            @block.sync
            def _(sp):
                for q, (c, w) in enumerate(chunks):
                    wait(sp, s_t, q - 1)
                    sp.dma_start(raw[0:w, q % 2, :, :].rearrange("t p c -> t (p c)"),
                                 Bl[c * P:(c + w) * P, :].rearrange("(t p) c -> t (p c)", p=P)).then_inc(s_ld[q % 2], 16)

            @block.tensor
            def _(pe):
                for q, (c, w) in enumerate(chunks):
                    pe.wait_ge(s_ld[q % 2], (q // 2 + 1) * 16)
                    wait(pe, s_c, q - 1)
                    for f in range(3):
                        m = nc.tensor.transpose(tps[q % 2][:, f, 0:w], raw[0:w, q % 2, :, f], K.ident[0:w, 0:w])
                    m.then_inc(s_t, 1)

            @block.vector
            def _(dve):
                for q, (c, w) in enumerate(chunks):
                    dve.wait_ge(s_t, q + 1)
                    nc.vector.tensor_tensor(K.kl[1][:, c:c + w], tps[q % 2][:, 0, 0:w], K.first[:, 1, c:c + w], ALU.subtract)
                    nc.vector.tensor_copy(K.idx[1][:, c:c + w], tps[q % 2][:, 1, 0:w])
                    nc.vector.tensor_copy(K.ec[1][:, c:c + w], tps[q % 2][:, 2, 0:w]).then_inc(s_c, 1)


def attention_logits(nc, counts, D, K, name, k, table, dnode, logit, V, beside=None):
    n = D.NT // BODY
    width = C + 2
    with ExitStack() as ctx:
        def sb(nm, s, d=F32):
            return ctx.enter_context(nc.sbuf_tensor(f"{name}_{nm}", s, d))
        idx = sb("idx", [P, RING, G], I32)
        rows = sb("rows", [P, RING, G, REC])
        oh = sb("oh", [P, 2, G, P], BF16)
        ohT = sb("ohT", [P, 2, G, P])
        part = sb("sum", [P, 2, G])
        ot = [ctx.enter_context(nc.psum_tensor(f"{name}_ot{u}", [P, G, P], BF16)) for u in range(2)]
        loc = [ctx.enter_context(nc.psum_tensor(f"{name}_loc{u}", [P, G], F32)) for u in range(2)]
        s_idx, s_oh, s_ot, s_ohT, s_loc, s_sum, s_log = (counts.get(f"att_{x}") for x in (
            "indices", "onehots", "turned", "turned_copied", "node_terms", "sums", "logits"))
        s_ga = [counts.get(f"att_gathered{u}") for u in range(RING)]
        s_vs = [counts.get(f"att_stored{u}") for u in range(RING)]
        vv = V.rearrange("(g p j) c -> p g j c", j=G, p=P)
        if beside is not None:
            kb, Vb, X, last, acc = beside
            wrows = sb("w_rows", [P, RING, G, C])
            msg = sb("w_msg", [P, RING, G, REC])
            woh = sb("w_oh", [P, RING, G, P])
            wpart = [ctx.enter_context(nc.psum_tensor(f"{name}_w_part{u}", [P, G, P], F32)) for u in range(RING)]
            s_msg, s_mm, s_z, s_ex, s_one, s_acc = (counts.get(f"weigh_{x}") for x in (
                "messages", "products", "zeroed", "extras", "onehots", "added"))
            s_ld = [counts.get(f"weigh_loaded{u}") for u in range(RING)]
            vb = Vb.rearrange("(g p j) c -> p g j c", j=G, p=P)
        with nc.Block() as block:
            @block.sync
            def _(sp):
                def store(i, u):
                    g = i * RING + u
                    wait(sp, s_ga[u], (i + 1) * 16 * G)
                    sp.dma_start(vv[:, bass.ds(g, 1), :, :].rearrange("p o j c -> p (o j) c"), rows[:, u, :, 0:C]).then_inc(s_vs[u].sem, 16)

                def load(i, u):
                    g = i * RING + u
                    wait(sp, s_msg, g - RING + 1)
                    sp.dma_start(wrows[:, u, :, :], vb[:, bass.ds(g, 1), :, :].rearrange("p o j c -> p (o j) c")).then_inc(s_ld[u].sem, 16)
                skewed(sp, n, [(0, store)] if beside is None else [(3, load), (0, store)])
                for u in range(RING):
                    wait(sp, s_vs[u], n * 16)

            @block.gpsimd
            def _(pool):
                if beside is not None:
                    nc.gpsimd.memset(acc[:, :, :], 0.0).then_inc(s_z.sem, 1)

                def body(i, last_):
                    for u in range(RING):
                        g = i * RING + u
                        wait(pool, s_idx, g + 1)
                        pool.nop(nofuse=True)
                        for j in range(G):
                            nc.gpsimd.indirect_dma_start(out=rows[:, u, j, :], out_offset=None, in_=table,
                                                         in_offset=bass.IndirectOffsetOnAxis(ap=idx[:, u, j:j + 1], axis=0)).then_inc(s_ga[u].sem, 16)
                loop(pool, n, body)

            @block.scalar
            def _(act):
                def index(i, u):
                    g = i * RING + u
                    wait(act, s_log, g - RING + 1)
                    wait(act, s_vs[u], i * 16)
                    nc.scalar.copy(idx[:, u, :], K.idx[k][:, bass.ds(g * G, G)]).then_inc(s_idx.sem, 1)

                def copy_onehot(i, u):
                    g = i * RING + u
                    wait(act, s_ot, g + 1)
                    wait(act, s_loc, g - 1)
                    nc.scalar.copy(ohT[:, u % 2, :, :], ot[u % 2][:, :, :]).then_inc(s_ohT.sem, 1)

                def extras(i, u):
                    g = i * RING + u
                    wait(act, s_mm, g - RING + 1)
                    nc.scalar.copy(msg[:, u, :, C:C + 1], X[:, bass.ds(g * G, G), :])
                    nc.scalar.copy(msg[:, u, :, C + 1], last[:, bass.ds(g * G, G)]).then_inc(s_ex.sem, 1)

                def message(i, u):
                    g = i * RING + u
                    wait(act, s_ex, g + 1)
                    wait(act, s_ld[u], (i + 1) * 16)
                    for j in range(G):
                        m = nc.scalar.activation(msg[:, u, j, 0:C], wrows[:, u, j, :], ACT.Copy, scale=msg[:, u, j, C:C + 1])
                    m.then_inc(s_msg.sem, 1)
                if beside is None:
                    skewed(act, n, [(2, copy_onehot), (3, index)])
                else:
                    skewed(act, n, [(2, copy_onehot), (3, extras), (2, message), (3, index)])

            @block.tensor
            def _(pe):
                held = {}

                def turn(i, u):
                    g = i * RING + u
                    wait(pe, s_oh, g + 1)
                    wait(pe, s_ohT, g - 1)
                    for j in range(G):
                        m = nc.tensor.transpose(ot[u % 2][:, j, :], oh[:, u % 2, j, :], K.identb[:, :])
                    m.then_inc(s_ot.sem, 1)

                def terms(i, u):
                    g = i * RING + u
                    wait(pe, s_ohT, g + 1)
                    wait(pe, s_sum, g - 1)
                    for j in range(G):
                        b = held["b"][(u - 1) % RING * G + j]
                        m = nc.tensor.matmul(loc[u % 2][:, j:j + 1], ohT[:, u % 2, j, :], dnode[:, bass.ds(b, 1)], start=True, stop=True)
                    m.then_inc(s_loc.sem, 1)

                def products(i, u):
                    g = i * RING + u
                    wait(pe, s_msg, g + 1)
                    wait(pe, s_one, g + 1)
                    wait(pe, s_acc, (g - RING + 1) * G)
                    for j in range(G):
                        m = nc.tensor.matmul(wpart[u][:, j, 0:width], woh[:, u, j, :], msg[:, u, j, 0:width], start=True, stop=True)
                    m.then_inc(s_mm.sem, 1)

                def blocks(i):
                    held["b"] = nc.values_load_multi_w_load_instructions(
                        K.blk[0:1, k, bass.ds(i * BODY + G, BODY)], engines=PE_ONLY, min_val=0, max_val=D.NB - 1)[1]
                held["b"] = [0] * (3 * G) + list(nc.values_load_multi_w_load_instructions(
                    K.blk[0:1, k, 0:G], engines=PE_ONLY, min_val=0, max_val=D.NB - 1)[1])
                if beside is None:
                    skewed(pe, n, [(1, terms), (2, turn)], blocks)
                else:
                    skewed(pe, n, [(1, terms), (2, turn), (1, products)], blocks)

            @block.vector
            def _(dve):
                held = {}

                def prep(i, u):
                    g = i * RING + u
                    wait(dve, s_ot, g - 1)
                    nc.vector.tensor_tensor(oh[:, u % 2, :, :], bcast(K.iota[:, :], 1, [P, G, P]),
                                            bcast(K.kl[k][:, bass.ds(g * G, G)], 2, [P, G, P]), ALU.is_equal).then_inc(s_oh.sem, 1)

                def node_and_edge(i, u):
                    g = i * RING + u
                    wait(dve, s_loc, g + 1)
                    wait(dve, s_log, g - 1)
                    nc.vector.tensor_tensor(part[:, u % 2, :], loc[u % 2][:, :], K.ec[k][:, bass.ds(g * G, G)], ALU.add).then_inc(s_sum.sem, 1)

                def logits(i, u):
                    g = i * RING + u
                    wait(dve, s_sum, g + 1)
                    wait(dve, s_ga[u], (i + 1) * 16 * G)
                    nc.vector.tensor_tensor(logit[:, bass.ds(g * G, G), :].rearrange("p j o -> p (j o)"), part[:, u % 2, :],
                                            rows[:, u, :, C], ALU.add).then_inc(s_log.sem, 1)

                def onehots(i, u):
                    g = i * RING + u
                    wait(dve, s_mm, g - RING + 1)
                    nc.vector.tensor_tensor(woh[:, u, :, :], bcast(K.iota[:, :], 1, [P, G, P]),
                                            bcast(K.kl[kb][:, bass.ds(g * G, G)], 2, [P, G, P]), ALU.is_equal).then_inc(s_one.sem, 1)

                def add(j):
                    def run(i, u):
                        g = i * RING + u
                        if j == 0:
                            wait(dve, s_mm, g + 1)
                        wait(dve, s_acc, g * G + j)
                        b = held["b"][u * G + j]
                        nc.vector.tensor_tensor(acc[:, bass.ds(b, 1), 0:width], acc[:, bass.ds(b, 1), 0:width],
                                                wpart[u][:, j:j + 1, 0:width], ALU.add).then_inc(s_acc.sem, 1)
                    return run

                def blocks(i):
                    held["b"] = nc.values_load_multi_w_load_instructions(
                        K.blk[0:1, kb, bass.ds(i * BODY, BODY)], engines=DVE_ONLY, min_val=0, max_val=D.NB - 1)[1]
                if beside is None:
                    skewed(dve, n, [(3, prep), (0, node_and_edge), (0, logits)])
                else:
                    wait(dve, s_z, 1)
                    skewed(dve, n, [(0, add(0)), (3, prep), (0, add(1)), (3, onehots), (0, add(2)), (0, node_and_edge),
                                    (0, add(3)), (0, logits)], blocks)
        finished(*[(s, RING * n) for s in (s_idx, s_oh, s_ot, s_ohT, s_loc, s_sum, s_log)],
                 *[(s, 16 * G * n) for s in s_ga], *[(s, 16 * n) for s in s_vs])
        if beside is not None:
            finished(*[(s, RING * n) for s in (s_msg, s_mm, s_ex, s_one)], (s_acc, D.NT), (s_z, 1), *[(s, 16 * n) for s in s_ld])


def load_params(nc, sem, K, dram, sb):
    K.w_tab = sb("w_tab", [C + 1, 3 * C], F32)
    K.w_kv = sb("w_kv", [C + 1, 2 * C], F32)
    K.w_proj = sb("w_proj", [C + 1, C], F32)
    K.w_l1 = sb("w_l1", [C + 1, C], F32)
    K.w_l2 = sb("w_l2", [P, C], F32)
    K.w_l3 = sb("w_l3", [C, C + 2], F32)
    s_p, s_z, s_t, s_d = sem("node_params"), sem("node_params_zeroed"), sem("node_params_turned"), sem("node_params_steps")
    with ExitStack() as ctx:
        raw = ctx.enter_context(nc.sbuf_tensor("w_l1_raw", [C, C], F32))
        arow = ctx.enter_context(nc.sbuf_tensor("a_rows", [C, 2, C], F32))
        pr = ctx.enter_context(nc.sbuf_tensor("a_prod", [C, 2, C], F32))
        tps = ctx.enter_context(nc.psum_tensor("w_l1_t", [C, C], F32))
        with nc.Block() as block:
            @block.sync
            def _(sp):
                n = [0]

                def load(out, in_):
                    n[0] += 16
                    sp.dma_start(out, in_).then_inc(s_p, 16)
                sp.wait_ge(s_z, 1)
                for c, nm in ((0, "L0_gnn_W_src"), (1, "L0_gnn_W_dst"), (2, "L0_gnn_Wq")):
                    load(K.w_tab[0:C, c * C:(c + 1) * C], dram[nm])
                load(K.w_tab[C:C + 1, 0:C], dram["L0_gnn_b_src"].rearrange("(o c) -> o c", o=1))
                load(K.w_tab[C:C + 1, 2 * C:3 * C], dram["L0_gnn_bq"].rearrange("(o c) -> o c", o=1))
                load(K.w_kv[0:C, :], dram["L0_gnn_W_kv"])
                load(K.w_kv[C:C + 1, :], dram["L0_gnn_b_kv"].rearrange("(o c) -> o c", o=1))
                load(K.w_proj[0:C, :], dram["L0_gnn_W_proj"])
                load(K.w_proj[C:C + 1, :], dram["L0_gnn_b_proj"].rearrange("(o c) -> o c", o=1))
                load(raw[:, :], dram["L1_gnn_W"])
                load(K.w_l1[C:C + 1, :], dram["L1_gnn_b"].rearrange("(o c) -> o c", o=1))
                load(K.w_l2[0:C, :], dram["L2_gnn_weight1"])
                load(K.w_l2[C:2 * C, :], dram["L2_gnn_weight2"])
                load(K.w_l3[:, 0:C], dram["L3_gnn_W"])
                for s in range(2):
                    load(arow[:, s, :], dram["L3_gnn_a"][s * C:(s + 1) * C, :].rearrange("c o -> o c").to_broadcast([C, C]))
                assert n[0] == 16 * 16

            @block.tensor
            def _(pe):
                pe.wait_ge(s_p, 256)
                nc.tensor.transpose(tps[:, :], raw[:, :], K.ident[0:C, 0:C]).then_inc(s_t, 1)

            @block.vector
            def _(dve):
                step = stepper(dve, s_d)
                nc.vector.memset(K.w_tab[:, :], 0.0).then_inc(s_z, 1)
                dve.wait_ge(s_t, 1)
                step(nc.vector.tensor_copy(K.w_l1[0:C, :], tps[:, :]))
                step(nc.vector.tensor_single_scalar(K.w_tab[:, 2 * C:3 * C], K.w_tab[:, 2 * C:3 * C], 0.25, ALU.mult))
                for s in range(2):
                    step(nc.vector.tensor_tensor(pr[:, s, :], K.w_l3[:, 0:C], arow[:, s, :], ALU.mult))
                step(nc.vector.tensor_reduce(K.w_l3[:, C:C + 2], pr[:, :, :], AX.X, ALU.add))


def vector_block(nc, sem, name, ops):
    s = sem(name)
    with nc.Block() as block:
        @block.vector
        def _(dve):
            for n, (who, make) in enumerate(ops):
                if who == "v":
                    make(nc.vector).then_inc(s, 1)
                dve.wait_ge(s, n + 1)

        @block.scalar
        def _(act):
            for n, (who, make) in enumerate(ops):
                if who == "a":
                    wait(act, s, n)
                    make(nc.scalar).then_inc(s, 1)


def build(nc, dram, out):
    D = Dims(dram["x"].shape[0], dram["src"].shape[0])
    K = Shared()
    NB, NT, NSLOT = D.NB, D.NT, D.NSLOT
    with ExitStack() as ctx:
        def sb(n, s, d):
            return ctx.enter_context(nc.sbuf_tensor(n, s, d))

        def sem(n):
            return ctx.enter_context(nc.semaphore(n))

        def node_dram(name, width):
            return nc.dram_tensor(name, (NB * P, width), F32).ap()
        counts = Counts(sem)
        K.first = sb("first_node", [P, 2, NT], F32)
        K.blk = sb("tile_block", [1, 2, NT + G], I32)
        K.deg = sb("degrees", [P, 2, NB], F32)
        constants(nc, sb, sem, K)
        A = nc.dram_tensor("edges_by_dst", (NSLOT, REC), F32).ap()
        Bl = nc.dram_tensor("edges_by_src", (NSLOT, 4), F32).ap()
        sort_edges(nc, sem, D, K, dram, A, Bl)

        K.x = sb("x_nodes", [P, NB, C], F32)
        K.kl = [sb(f"key_in_block{k}", [P, NT], F32) for k in range(2)]
        K.idx = [sb(f"other_end{k}", [P, NT], I32) for k in range(2)]
        K.ec = [sb(f"edge_term{k}", [P, NT], F32) for k in range(2)]
        load_params(nc, sem, K, dram, sb)
        load_nodes(nc, sem, D, K, dram)
        rows_dram = [nc.dram_tensor(f"rows_in_order{k}", (NSLOT, C), F32).ap() for k in range(2)]

        with ExitStack() as l1:
            al = l1.enter_context(nc.sbuf_tensor("scores", [P, NT, HEADS], F32))
            with ExitStack() as t:
                tabD = t.enter_context(nc.sbuf_tensor("dst_table", [P, NB, 2 * C], F32))
                tabS = node_dram("src_table", C)

                def feed(dve, g, o):
                    return nc.vector.tensor_copy(o, K.x[:, bass.ds(g * 4, 4), :])

                def evict(dve, g, prods, stage):
                    nc.vector.tensor_copy(tabD[:, bass.ds(g * 4, 4), :], prods[1])
                    return nc.vector.tensor_copy(stage, prods[0])
                node_stage(nc, counts, D, K, "tables", C, K.w_tab, (C, 2 * C), feed, evict, tabS)
                score_edges(nc, sem, D, K, A, tabS, tabD, K.w_kv, al, rows_dram[0])
            segment_softmax(nc, counts, D, K, "sm0", al, HEADS, 0)
            acc = l1.enter_context(nc.sbuf_tensor("acc0", [P, NB, REC], F32))
            weighted_sum(nc, counts, D, K, "ws0", 0, rows_dram[0], al, HEADS, acc)
            den = l1.enter_context(nc.sbuf_tensor("den0", [P, NB, HEADS], F32))
            vector_block(nc, sem, "den_steps", [
                ("v", lambda e: e.tensor_single_scalar(den[:, :, :], acc[:, :, C:C + HEADS], 1e-16, ALU.add)),
                ("v", lambda e: e.reciprocal(den[:, :, :], den[:, :, :]))])

            def feed(dve, g, o):
                return nc.vector.tensor_tensor(o.rearrange("p j (h d) -> p j h d", h=HEADS),
                                               acc[:, bass.ds(g * 4, 4), 0:C].rearrange("p j (h d) -> p j h d", h=HEADS),
                                               den[:, bass.ds(g * 4, 4), :].unsqueeze(3).to_broadcast([P, 4, HEADS, C // HEADS]), ALU.mult)

            def evict(dve, g, prods, stage):
                xs = K.x[:, bass.ds(g * 4, 4), :]
                return nc.vector.tensor_tensor(xs, xs, prods[0], ALU.add)
            node_stage(nc, counts, D, K, "proj", C, K.w_proj, (C,), feed, evict)
        layer_norm(nc, counts, D, K, "ln0")

        read_list(nc, sem, D, K, Bl)
        scale = sb("node_scale", [P, 3, NB], F32)
        vector_block(nc, sem, "scale_steps", [
            ("v", lambda e: e.tensor_tensor(scale[:, 0, :], K.deg[:, 0, :], K.deg[:, 1, :], ALU.add)),
            ("v", lambda e: e.tensor_single_scalar(scale[:, 0, :], scale[:, 0, :], 1.0, ALU.add)),
            ("v", lambda e: e.tensor_single_scalar(scale[:, 1, :], K.deg[:, 1, :], 1.0, ALU.max)),
            ("v", lambda e: e.tensor_single_scalar(scale[:, 2, :], K.deg[:, 0, :], 1.0, ALU.max)),
            ("a", lambda e: e.activation(scale[:, :, :], scale[:, :, :], ACT.Sqrt)),
            ("v", lambda e: e.reciprocal(scale[:, :, :], scale[:, :, :]))])
        with ExitStack() as l2:
            acc = l2.enter_context(nc.sbuf_tensor("acc1", [P, NB, C], F32))
            tab = node_dram("layer2_table", C)

            def feed(dve, g, o):
                return nc.vector.tensor_copy(o, K.x[:, bass.ds(g * 4, 4), :])

            def evict(dve, g, prods, stage):
                ds = bass.ds(g * 4, 4)
                nc.vector.tensor_tensor(acc[:, ds, :], prods[0], scale[:, 0, ds].unsqueeze(2).to_broadcast([P, 4, C]), ALU.mult)
                return nc.vector.tensor_tensor(stage, prods[0], scale[:, 0, ds].unsqueeze(2).to_broadcast([P, 4, C]), ALU.mult)
            node_stage(nc, counts, D, K, "lin1", C, K.w_l1, (C,), feed, evict, tab)
            gather_sum(nc, counts, D, K, "gs1f", 0, tab, acc)
            gather_sum(nc, counts, D, K, "gs1b", 1, tab, acc)
            vector_block(nc, sem, "layer2_steps", [
                ("v", lambda e: e.tensor_tensor(acc[:, :, :], acc[:, :, :], bcast(scale[:, 0, :], 2, [P, NB, C]), ALU.mult)),
                ("v", lambda e: e.tensor_tensor(K.x[:, :, :], K.x[:, :, :], acc[:, :, :], ALU.add))])
        layer_norm(nc, counts, D, K, "ln1")

        with ExitStack() as l3:
            acc = l3.enter_context(nc.sbuf_tensor("acc2", [P, NB, C], F32))
            fn = l3.enter_context(nc.sbuf_tensor("scaled_x", [P, NB, C], F32))
            tmp = l3.enter_context(nc.sbuf_tensor("layer3_tmp", [P, 2, 4, C], F32))
            tab = node_dram("layer3_table", C)
            s_f, s_t = sem("layer3_scaled"), sem("layer3_table_stored")
            with nc.Block() as block:
                @block.vector
                def _(dve):
                    nc.vector.tensor_tensor(fn[:, :, :], K.x[:, :, :], bcast(scale[:, 1, :], 2, [P, NB, C]), ALU.mult).then_inc(s_f, 1)

                @block.gpsimd
                def _(pool):
                    nc.gpsimd.memset(acc[:, :, :], 0.0)

                @block.sync
                def _(sp):
                    sp.wait_ge(s_f, 1)
                    sp.dma_start(tab.rearrange("(b p) c -> p b c", p=P), fn[:, :, :]).then_inc(s_t, 16)
                    sp.wait_ge(s_t, 16)
            gather_sum(nc, counts, D, K, "gs2", 0, tab, acc)

            def feed(dve, g, o):
                ds = bass.ds(g * 4, 4)
                nc.vector.tensor_copy(o[:, :, 0:C], acc[:, ds, :])
                return nc.vector.tensor_tensor(o[:, :, C:2 * C], acc[:, ds, :], fn[:, ds, :], ALU.mult)
            turn = [0]
            s_step = sem("layer3_scaled_sums")

            def evict(dve, g, prods, stage):
                ds = bass.ds(g * 4, 4)
                u = turn[0] % 2
                turn[0] += 1
                t = tmp[:, u, :, :]
                nc.vector.tensor_tensor(t, prods[0], scale[:, 2, ds].unsqueeze(2).to_broadcast([P, 4, C]), ALU.mult).then_inc(s_step, 1)
                dve.wait_ge(s_step, g + 1)
                return nc.vector.tensor_tensor(K.x[:, ds, :], K.x[:, ds, :], t, ALU.add)
            node_stage(nc, counts, D, K, "lin2", 2 * C, K.w_l2, (C,), feed, evict, bias=False)
        layer_norm(nc, counts, D, K, "ln2")

        tab = node_dram("layer4_table", REC)
        sd = sb("s_and_d", [P, 2, NB], F32)

        def feed(dve, g, o):
            return nc.vector.tensor_copy(o, K.x[:, bass.ds(g * 4, 4), :])

        def evict(dve, g, prods, stage):
            ds = bass.ds(g * 4, 4)
            nc.vector.tensor_copy(sd[:, :, ds].rearrange("p s b -> p b s"), prods[0][:, :, C:C + 2])
            return nc.vector.tensor_copy(stage[:, :, 0:C + 2], prods[0])
        node_stage(nc, counts, D, K, "lin3", C, K.w_l3, (C + 2,), feed, evict, tab, bias=False)
        z = [sb(f"logits{k}", [P, NT, 1], F32) for k in range(2)]
        acc = []
        for k in range(2):
            attention_logits(nc, counts, D, K, f"al{k}", k, tab, sd[:, 1, :], z[k], rows_dram[k],
                             beside=None if k == 0 else (0, rows_dram[0], z[0], K.ec[0], acc[0]))
            segment_softmax(nc, counts, D, K, f"sm3{k}", z[k], 1, k, slope=0.2, last=K.ec[k])
            acc.append(sb(f"acc3{k}", [P, NB, C + 2], F32))
        weighted_sum(nc, counts, D, K, "ws3", 1, rows_dram[1], z[1], 1, acc[1], last=K.ec[1],
                     spare=K.first[:, :, :].rearrange("p k t -> p (k t)"))
        merge_attention(nc, sem, D, K, tab, sd, acc)
        layer_norm(nc, counts, D, K, "ln3", out)


def merge_attention(nc, sem, D, K, tab, sd, acc):
    NB = D.NB
    with ExitStack() as ctx:
        xt = ctx.enter_context(nc.sbuf_tensor("mg_xt", [P, NB, C], F32))
        m = ctx.enter_context(nc.sbuf_tensor("mg_m", [P, 4, NB], F32))
        has = ctx.enter_context(nc.sbuf_tensor("mg_has", [P, 2, NB], F32))
        w = ctx.enter_context(nc.sbuf_tensor("mg_w", [P, 3, NB], F32))
        den = ctx.enter_context(nc.sbuf_tensor("mg_den", [P, 3, NB], F32))
        s_ld = sem("mg_loaded")
        with nc.Block() as block:
            @block.sync
            def _(sp):
                sp.dma_start(xt[:, :, :], tab.rearrange("(b p) c -> p b c", p=P)[:, :, 0:C]).then_inc(s_ld, 16)
                sp.wait_ge(s_ld, 16)
        ops = []

        def v(f):
            ops.append(("v", f))
        v(lambda e: e.tensor_single_scalar(has[:, :, :], K.deg[:, :, :], 1.0, ALU.min))
        v(lambda e: e.tensor_scalar(has[:, :, :], has[:, :, :], BIG, -BIG, ALU.mult, ALU.add))
        for k in range(2):
            v(lambda e, k=k: e.tensor_tensor(m[:, k, :], acc[k][:, :, C + 1], has[:, k, :], ALU.add))
        v(lambda e: e.tensor_tensor(m[:, 3, :], sd[:, 0, :], sd[:, 1, :], ALU.add))
        v(lambda e: e.scalar_tensor_tensor(m[:, 2, :], m[:, 3, :], 0.2, m[:, 3, :], ALU.mult, ALU.max))
        v(lambda e: e.tensor_tensor(m[:, 3, :], m[:, 0, :], m[:, 1, :], ALU.max))
        v(lambda e: e.tensor_tensor(m[:, 3, :], m[:, 3, :], m[:, 2, :], ALU.max))
        for k in range(3):
            v(lambda e, k=k: e.tensor_tensor(w[:, k, :], m[:, k, :], m[:, 3, :], ALU.subtract))
        ops.append(("a", lambda e: e.activation(w[:, :, :], w[:, :, :], ACT.Exp)))
        for k in range(2):
            v(lambda e, k=k: e.tensor_tensor(den[:, k, :], acc[k][:, :, C], w[:, k, :], ALU.mult))
        v(lambda e: e.tensor_tensor(den[:, 0, :], den[:, 0, :], den[:, 1, :], ALU.add))
        v(lambda e: e.tensor_tensor(den[:, 0, :], den[:, 0, :], w[:, 2, :], ALU.add))
        v(lambda e: e.reciprocal(den[:, 2, :], den[:, 0, :]))
        for k in range(3):
            v(lambda e, k=k: e.tensor_tensor(w[:, k, :], w[:, k, :], den[:, 2, :], ALU.mult))
        for k in range(2):
            v(lambda e, k=k: e.tensor_tensor(acc[k][:, :, 0:C], acc[k][:, :, 0:C], bcast(w[:, k, :], 2, [P, NB, C]), ALU.mult))
        v(lambda e: e.tensor_tensor(xt[:, :, :], xt[:, :, :], bcast(w[:, 2, :], 2, [P, NB, C]), ALU.mult))
        for k in range(2):
            v(lambda e, k=k: e.tensor_tensor(K.x[:, :, :], K.x[:, :, :], acc[k][:, :, 0:C], ALU.add))
        v(lambda e: e.tensor_tensor(K.x[:, :, :], K.x[:, :, :], xt[:, :, :], ALU.add))
        vector_block(nc, sem, "mg_steps", ops)


def kernel(**inputs):
    import numpy as _np
    import concourse.bacc as _bacc
    from concourse import mybir as _mybir
    from concourse.bass_utils import run_bass_kernel_spmd as _run
    nc = _bacc.Bacc("TRN2", target_bir_lowering=False, num_devices=1)
    arrays, dram = {}, {}
    for name, value in inputs.items():
        a = _np.ascontiguousarray(value)
        arrays[f"in_{name}_dram"] = a
        dram[name] = nc.dram_tensor(f"in_{name}_dram", a.shape, _mybir.dt.from_np(a.dtype), kind="ExternalInput").ap()
    out = nc.dram_tensor("out_x", inputs["x"].shape, F32, kind="ExternalOutput").ap()
    build(nc, dram, out)
    r = _run(nc, [arrays], core_ids=[0])
    return r.results[0]["out_x"]
```
